# Optimizing a Trainium2 kernel written in Bass

```python
import numpy as np
import jax
import jax.numpy as jnp

def _softmax(x, axis=-1):
    return jax.nn.softmax(x, axis=axis)

def _gelu(x):
    return jax.nn.gelu(x, approximate=True)

def _silu(x):
    return jax.nn.silu(x)

def _sigmoid(x):
    return jax.nn.sigmoid(x)

def _layernorm(x, axis=-1, eps=1e-05):
    m = jnp.mean(x, axis=axis, keepdims=True)
    v = jnp.var(x, axis=axis, keepdims=True)
    return (x - m) / jnp.sqrt(v + eps)

def _scatter_add(tgt, idx, src, axis=0):
    return tgt.at[idx].add(src)

def _segment_sum(src, seg, n):
    return jax.ops.segment_sum(src, seg, n)
kernel_name = 'mk_flamingo_gated_d2_seqx_r8_593f73'

def setup_inputs(seed: int=0):
    np.random.seed(seed)
    _w = jnp.asarray

    def _rec_inputs():
        import jax
        import jax.numpy as jnp
        _rk = jax.random.key(seed)
        x = -0.000125 + 0.9999 * jax.random.normal(jax.random.fold_in(_rk, 1), (16, 128, 128), jnp.float32)
        _lenS = 128 - jax.random.randint(jax.random.fold_in(_rk, 7), (16,), 0, max(1, 128 // 4) + 1, jnp.int32)
        _lenS2 = 77 - jax.random.randint(jax.random.fold_in(_rk, 8), (16,), 0, max(1, 77 // 4) + 1, jnp.int32)
        _ctx_1024P = jax.random.normal(jax.random.fold_in(_rk, 11), (16, 16, 128), jnp.float32)
        _ctx_1024c = jax.random.dirichlet(jax.random.fold_in(_rk, 511), 0.3 * jnp.ones((16,), jnp.float32), (16, 77))
        _ctx_1024t = jnp.einsum('bsk,bkd->bsd', _ctx_1024c, _ctx_1024P)
        _ctx_1024t = _ctx_1024t * jax.lax.rsqrt(jnp.mean(jnp.square(_ctx_1024t)) + 1e-12) * 0.953939
        ctx_1024 = -1.52775e-05 + 0.999936 * (_ctx_1024t + 0.3 * jax.random.normal(jax.random.fold_in(_rk, 611), (16, 77, 128), jnp.float32))
        fside_BxS2_0 = jax.random.uniform(jax.random.fold_in(_rk, 12), (16, 77), jnp.float32, 0.0, 0.999833)
        _g = jax.random.normal(jax.random.fold_in(_rk, 9001), (2, 2), jnp.float32)
        _g = jnp.sign(_g) * jnp.maximum(jnp.abs(_g), 1.0) + (_g == 0) * 1.0
        g_xattn = _g[0]
        g_ffn = _g[1]
        return (x, ctx_1024, fside_BxS2_0, g_xattn, g_ffn)
    x, ctx_1024, fside_BxS2_0, g_xattn, g_ffn = _rec_inputs()

    def _L0_xattn_setup():
        import jax, jax.numpy as jnp
        import numpy as np
        B, S, D = (8, 512, 128)
        key = jax.random.key(seed)
        kq, kk, kv, kw, kb = jax.random.split(key, 5)
        query = jax.random.normal(kq, (B, S, D), dtype=jnp.float32)
        k = jax.random.normal(kk, (B, S, D), dtype=jnp.float32)
        value = jax.random.normal(kv, (B, S, D), dtype=jnp.float32)
        bound = 1.0 / np.sqrt(D)
        W_out = jax.random.uniform(kw, (D, D), minval=-bound, maxval=bound, dtype=jnp.float32)
        b_out = jax.random.uniform(kb, (D,), minval=-bound, maxval=bound, dtype=jnp.float32)
        return {'query': query, 'key': k, 'value': value, 'W_out': W_out, 'b_out': b_out}
    _L0_xattn_all = _L0_xattn_setup()
    _L0_xattn_in = {k: v for k, v in _L0_xattn_all.items() if k in ('W_out', 'b_out')}
    del _L0_xattn_all

    def _L0_ffn_setup():
        import jax, jax.numpy as jnp
        import numpy as np
        DMODEL = 128
        N_EXPERTS = 16
        EXPERT_SIZE = 32
        K = 4
        key = jax.random.key(seed)
        k1, k2, k3, k4 = jax.random.split(key, 4)
        std_sel = 1.0 / np.sqrt(DMODEL)
        std_val = 1.0 / np.sqrt(N_EXPERTS * EXPERT_SIZE)
        return {'x': jax.random.normal(k1, (4, 256, DMODEL), dtype=jnp.float32), 'expert_sel': jax.random.normal(k2, (N_EXPERTS, DMODEL), dtype=jnp.float32) * std_sel, 'keys': jax.random.normal(k3, (N_EXPERTS, DMODEL, EXPERT_SIZE), dtype=jnp.float32) * std_sel, 'values': jax.random.normal(k4, (N_EXPERTS, EXPERT_SIZE, DMODEL), dtype=jnp.float32) * std_val, 'route_scale': jnp.ones((1,), dtype=jnp.float32)}
    _L0_ffn_all = _L0_ffn_setup()
    _L0_ffn_in = {k: v for k, v in _L0_ffn_all.items() if k in ('expert_sel', 'keys', 'values', 'route_scale')}
    del _L0_ffn_all

    def _L1_xattn_setup():
        import jax, jax.numpy as jnp
        import numpy as np
        B, NQ, S, D = (2, 256, 256, 128)
        H, HD, OUT = (16, 64, 128)
        key = jax.random.key(seed)
        ks = jax.random.split(key, 8)
        scale = 1.0 / np.sqrt(D)
        return {'queries': jax.random.normal(ks[0], (B, NQ, D), jnp.float32), 'keys': jax.random.normal(ks[1], (B, S, D), jnp.float32), 'values': jax.random.normal(ks[2], (B, S, D), jnp.float32), 'indicators': jax.random.uniform(ks[3], (B, S), jnp.float32), 'Wq': jax.random.normal(ks[4], (D, H * HD), jnp.float32) * scale, 'Wk': jax.random.normal(ks[5], (D, H * HD), jnp.float32) * scale, 'Wv': jax.random.normal(ks[6], (D, H * HD), jnp.float32) * scale, 'Wo': jax.random.normal(ks[7], (H * HD, OUT), jnp.float32) * scale}
    _L1_xattn_all = _L1_xattn_setup()
    _L1_xattn_in = {k: v for k, v in _L1_xattn_all.items() if k in ('Wq', 'Wk', 'Wv', 'Wo')}
    del _L1_xattn_all

    def _L1_ffn_setup():
        import jax, jax.numpy as jnp
        import numpy as np
        E = 8
        K = 2
        CAP_RATIO = 1.05
        key = jax.random.key(seed)
        ks = jax.random.split(key, 4)
        B, S, D, H = (2, 256, 128, 512)
        x = jax.random.normal(ks[0], (B, S, D), jnp.float32)
        Wg = jax.random.normal(ks[1], (E, D), jnp.float32) * 0.02
        W1 = jax.random.normal(ks[2], (E, D, H), jnp.float32) * 0.02
        b1 = jnp.zeros((E, H), jnp.float32)
        W2 = jax.random.normal(ks[3], (E, H, D), jnp.float32) * 0.02
        b2 = jnp.zeros((E, D), jnp.float32)
        return {'x': x, 'Wg': Wg, 'W1': W1, 'b1': b1, 'W2': W2, 'b2': b2}
    _L1_ffn_all = _L1_ffn_setup()
    _L1_ffn_in = {k: v for k, v in _L1_ffn_all.items() if k in ('Wg', 'W1', 'b1', 'W2', 'b2')}
    del _L1_ffn_all
    return {'x': x, 'ctx_1024': ctx_1024, 'fside_BxS2_0': fside_BxS2_0, 'g_xattn': g_xattn, 'g_ffn': g_ffn, 'L0_xattn_W_out': _L0_xattn_in['W_out'], 'L0_xattn_b_out': _L0_xattn_in['b_out'], 'L0_ffn_expert_sel': _L0_ffn_in['expert_sel'], 'L0_ffn_keys': _L0_ffn_in['keys'], 'L0_ffn_values': _L0_ffn_in['values'], 'L0_ffn_route_scale': _L0_ffn_in['route_scale'], 'L1_xattn_Wq': _L1_xattn_in['Wq'], 'L1_xattn_Wk': _L1_xattn_in['Wk'], 'L1_xattn_Wv': _L1_xattn_in['Wv'], 'L1_xattn_Wo': _L1_xattn_in['Wo'], 'L1_ffn_Wg': _L1_ffn_in['Wg'], 'L1_ffn_W1': _L1_ffn_in['W1'], 'L1_ffn_b1': _L1_ffn_in['b1'], 'L1_ffn_W2': _L1_ffn_in['W2'], 'L1_ffn_b2': _L1_ffn_in['b2']}

def reference(x, ctx_1024, fside_BxS2_0, g_xattn, g_ffn, L0_xattn_W_out, L0_xattn_b_out, L0_ffn_expert_sel, L0_ffn_keys, L0_ffn_values, L0_ffn_route_scale, L1_xattn_Wq, L1_xattn_Wk, L1_xattn_Wv, L1_xattn_Wo, L1_ffn_Wg, L1_ffn_W1, L1_ffn_b1, L1_ffn_W2, L1_ffn_b2):
    import jax
    import jax.numpy as jnp

    def _L0_xattn_ref(query, key, value, W_out, b_out):
        import jax, jax.numpy as jnp
        import numpy as np
        B, S, D = (8, 512, 128)
        d = query.shape[-1]
        scale = 1.0 / jnp.sqrt(jnp.asarray(d, dtype=query.dtype))
        scores = jnp.einsum('bqd,bkd->bqk', query, key) * scale
        attn = jax.nn.softmax(scores, axis=-1)
        ctx = jnp.einsum('bqk,bkd->bqd', attn, value)
        out = jnp.einsum('bqd,ed->bqe', ctx, W_out) + b_out
        return out

    def _L0_ffn_ref(x, expert_sel, keys, values, route_scale):
        import jax, jax.numpy as jnp
        import numpy as np
        DMODEL = 128
        N_EXPERTS = 16
        EXPERT_SIZE = 32
        K = 4
        sel_logits = jnp.einsum('btd,ed->bte', x, expert_sel)
        sel_probs = jax.nn.sigmoid(sel_logits)
        _, sel_index = jax.lax.top_k(sel_probs, K)
        sel_val = jnp.take_along_axis(sel_probs, sel_index, axis=-1)
        sel_val = sel_val / jnp.clip(sel_val.sum(-1, keepdims=True), 1e-09)
        sel_val = sel_val * route_scale
        scores_all = jax.nn.relu(jnp.einsum('btd,edh->bteh', x, keys))
        values_all = jnp.einsum('bteh,ehv->btev', scores_all, values)
        sel_idx_exp = sel_index[..., None]
        selected = jnp.take_along_axis(values_all, sel_idx_exp, axis=2)
        out = (selected * sel_val[..., None]).sum(axis=2)
        return out

    def _L1_xattn_ref(queries, keys, values, indicators, Wq, Wk, Wv, Wo):
        import jax, jax.numpy as jnp
        import numpy as np
        B, NQ, S, D = (2, 256, 256, 128)
        H, HD, OUT = (16, 64, 128)
        b, nq, _ = queries.shape
        s = keys.shape[1]
        Q = (queries @ Wq).reshape(b, nq, H, HD).transpose(0, 2, 1, 3)
        K = (keys @ Wk).reshape(b, s, H, HD).transpose(0, 2, 1, 3)
        V = (values @ Wv).reshape(b, s, H, HD).transpose(0, 2, 1, 3)
        scores = jnp.einsum('bhqd,bhkd->bhqk', Q, K) / jnp.sqrt(jnp.float32(HD))
        probs = jax.nn.softmax(scores, axis=-1)
        probs = probs * indicators[:, None, None, :]
        ctx = jnp.einsum('bhqk,bhkd->bhqd', probs, V)
        ctx = ctx.transpose(0, 2, 1, 3).reshape(b, nq, H * HD)
        return ctx @ Wo

    def _L1_ffn_ref(x, Wg, W1, b1, W2, b2):
        import jax, jax.numpy as jnp
        import numpy as np
        E = 8
        K = 2
        CAP_RATIO = 1.05
        B, S, D = x.shape
        T = B * S
        xf = x.reshape(T, D)
        gates = jax.nn.softmax(xf @ Wg.T, axis=-1)
        topw, topi = jax.lax.top_k(gates, K)
        C = int(round(K * T * CAP_RATIO / E))
        e_ord = topi.T.reshape(-1)
        tok_ord = jnp.tile(jnp.arange(T), K)
        oh = jax.nn.one_hot(e_ord, E, dtype=jnp.int32)
        cnt = jnp.take_along_axis(jnp.cumsum(oh, 0) - oh, e_ord[:, None], 1)[:, 0]
        within = cnt < C
        pos = jnp.where(within, cnt, C)
        x_disp = xf[tok_ord]
        buf = jnp.zeros((E, C + 1, D), xf.dtype).at[e_ord, pos].add(x_disp)[:, :C]
        h = jax.nn.gelu(jnp.einsum('ecd,edh->ech', buf, W1) + b1[:, None, :], approximate=False)
        y = jnp.einsum('ech,ehd->ecd', h, W2) + b2[:, None, :]
        y_ord = y[e_ord, jnp.minimum(pos, C - 1)] * within[:, None].astype(y.dtype)
        y_tk = y_ord.reshape(K, T, D).transpose(1, 0, 2)
        cw = topw * within.reshape(K, T).T.astype(topw.dtype)
        out = jnp.einsum('tk,tkd->td', cw, y_tk)
        return out.reshape(B, S, D)
    x = x + jnp.tanh(g_xattn[0]) * _L0_xattn_ref(_layernorm(x, axis=-1), ctx_1024, ctx_1024, L0_xattn_W_out, L0_xattn_b_out)
    x = x + jnp.tanh(g_ffn[0]) * _L0_ffn_ref(_layernorm(x, axis=-1), L0_ffn_expert_sel, L0_ffn_keys, L0_ffn_values, L0_ffn_route_scale)
    x = x + jnp.tanh(g_xattn[1]) * _L1_xattn_ref(_layernorm(x, axis=-1), ctx_1024, ctx_1024, fside_BxS2_0, L1_xattn_Wq, L1_xattn_Wk, L1_xattn_Wv, L1_xattn_Wo)
    x = x + jnp.tanh(g_ffn[1]) * _L1_ffn_ref(_layernorm(x, axis=-1), L1_ffn_Wg, L1_ffn_W1, L1_ffn_b1, L1_ffn_W2, L1_ffn_b2)
    return x

_drawn_inputs = setup_inputs


def setup_inputs(seed=0):
    import zlib

    import numpy as np

    out = dict(_drawn_inputs(seed))
    spreads = {'g_ffn': (-1.0, 0.6), 'L1_ffn_b1': (0.0, 0.8), 'L1_ffn_b2': (0.0, 0.549)}
    factors = {'L1_ffn_Wg': 3.795, 'L1_ffn_W1': 7.438, 'L1_ffn_W2': 6.713}
    for name, (base, spread) in spreads.items():
        noise = np.random.default_rng([zlib.crc32(name.encode()), seed]).standard_normal(out[name].shape)
        drawn = base * np.exp(spread * noise) if base else spread * noise
        out[name] = jnp.asarray(drawn.astype(out[name].dtype))
    for name, factor in factors.items():
        out[name] = (out[name] * factor).astype(out[name].dtype)
    return out
```

```python
from collections import namedtuple
from contextlib import ExitStack

import numpy as np

import concourse.bass as bass
from concourse import mybir

ALU = mybir.AluOpType
ACT = mybir.ActivationFunctionType
AX = mybir.AxisListType
F32 = mybir.dt.float32
F32R = mybir.dt.float32r
BF16 = mybir.dt.bfloat16
U32 = mybir.dt.uint32

P = 128
EPS = 1e-5
BIG = float(1 << 20)


def gated_layers_kernel(nc, t, out):
    NB, NQ, D = t["x"].shape[1], t["x"].shape[0], t["x"].shape[2]
    NK = t["ind"].shape[0]
    NH = t["wqT"].shape[0] * t["wqT"].shape[1] // 64
    HD = 64
    NE0 = t["selT"].shape[1]
    H0 = t["keys"].shape[1]
    ES = H0 // NE0
    TOPK0 = 4
    NE = t["wgT"].shape[1]
    HID = t["w1"].shape[2]
    MC = HID // P
    T = NB * NQ
    CAP = int(round(2 * T * 1.05 / NE))
    ST = -(-CAP // P)
    TAIL = CAP - (ST - 1) * P
    HALF = CAP // 2
    RW = D + 4
    HCUT = [0, 5, 10, 16]
    GB = 4
    GN = GB * NK
    assert NQ == D == P and NH == 16 and CAP % 2 == 0

    ctx = ExitStack()
    with ctx:
        def sb(name, shape, dt=F32):
            return ctx.enter_context(nc.sbuf_tensor(name, shape, dt))

        def sem(name):
            return ctx.enter_context(nc.semaphore(name))

        x_sb = sb("x_sb", [P, NB, D])
        res = sb("res", [P, NB, D])
        G = sb("G", [P, NB, NH * NK])
        ctxT = sb("ctxT", [P, NB * NK])
        ctx_hi = sb("ctx_hi", [P, NB * NK], F32R)
        ctx_lo = sb("ctx_lo", [P, NB * NK], F32R)
        wv_hi = sb("wv_hi", [P, NH * HD], F32R)
        wv_lo = sb("wv_lo", [P, NH * HD], F32R)
        m_hi = sb("m_hi", [P, NH * P], F32R)
        m_lo = sb("m_lo", [P, NH * P], F32R)
        stage = sb("stage", [P, 4, NH * HD])
        woutT = sb("woutT", [P, D])
        selT = sb("selT", [P, NE0])
        keys = sb("keys", [P, H0])
        vals = sb("vals", [P, H0 // P, D])
        wo = sb("wo", [P, NH * HD // P, D])
        wgT = sb("wgT", [P, NE])
        ind = sb("ind", [NK, NB])
        b1 = sb("b1", [P, NE * MC])
        bout = sb("bout", [P, D])
        gates = sb("gates", [P, 5])
        tg = sb("tg", [P, 4])
        valg = sb("valg", [P, 1])
        ident = sb("ident", [P, P])
        ones_bf = sb("ones_bf", [P, P], BF16)
        before = sb("before", [P, P], BF16)
        mhalf = sb("mhalf", [P, 1])
        eps = sb("eps", [P, 1])
        iota16 = sb("iota16", [P, NE0])
        slot0 = sb("slot0", [P, 2, NE])
        sgn = sb("sgn", [P, 2, NE])
        token = sb("token", [P, NB])
        empty = sb("empty", [P, ST, RW])
        carry = sb("carry", [P, 2, NE])
        st = [sb(f"st{n}", [P, 6]) for n in range(4)]
        mv = [sb(f"mv{n}", [P, 2]) for n in range(4)]
        ve = [sb(f"ve{n}", [P, 1]) for n in range(4)]
        rs = [sb(f"rs{n}", [P, 1]) for n in range(4)]
        xn = [sb(f"xn{n}", [P, D]) for n in range(3)]
        xnT = [sb(f"xnT{n}", [P, NQ]) for n in range(4)]
        ctA = sb("ctA", [P, NK])
        ctD_hi = sb("ctD_hi", [P, NK], F32R)
        ctD_lo = sb("ctD_lo", [P, NK], F32R)
        indD = sb("indD", [NK, 1])
        v0 = sb("v0", [NK, D])
        nm0 = sb("nm0", [P, 1])
        p0 = sb("p0", [P, NK])
        sum0 = sb("sum0", [P, 1])
        ri0 = sb("ri0", [P, 1])
        p0T = sb("p0T", [NK, NQ])
        er = sb("er", [P, NE0])
        er1 = sb("er1", [P, NE0])
        sig = sb("sig", [P, NE0])
        top = sb("top", [P, 8])
        topi = sb("topi", [P, 8], U32)
        den = sb("den", [P, 1])
        den1 = sb("den1", [P, 1])
        rden = sb("rden", [P, 1])
        eq = sb("eq", [P, TOPK0, NE0])
        mask = sb("mask", [P, NE0])
        w0 = sb("w0", [P, NE0])
        hw = sb("hw", [P, H0])
        hwT = sb("hwT", [P, H0])
        nm1 = sb("nm1", [P, NH])
        p1 = sb("p1", [P, NH, NK])
        sum1 = sb("sum1", [P, NH])
        ri1 = sb("ri1", [P, NH])
        p1n = sb("p1n", [P, NH, NK])
        p1T = sb("p1T", [NK, NH * NQ])
        v1 = sb("v1", [NK, NH * HD])
        cT = sb("cT", [P, NH * HD // P, NQ])
        rows = sb("rows", [P, 2, RW])
        nmg = sb("nmg", [P, 1])
        eg = sb("eg", [P, NE])
        sumg = sb("sumg", [P, 1])
        rig = sb("rig", [P, 1])
        topg = sb("topg", [P, 8])
        topgi = sb("topgi", [P, 8], U32)
        oh = sb("oh", [P, 2, NE], BF16)
        pos = sb("pos", [P, 2, NE])
        slot = sb("slot", [P, 2, NE])
        over = sb("over", [P, 2, NE])
        sidx = sb("sidx", [P, 2], U32)

        g_flat = G[:, :, :].rearrange("p b n -> p (b n)")
        cut = [0]

        def over_g(n):
            a = cut[0]
            cut[0] += n
            assert cut[0] <= NB * NH * NK
            return g_flat[:, a:a + n]

        xe = [over_g(ST * RW).rearrange("p (s c) -> p s c", c=RW) for _ in range(2)]
        xeT = [over_g(CAP) for _ in range(2)]
        hT = [over_g(MC * CAP).rearrange("p (m s) -> p m s", s=CAP) for _ in range(2)]
        ye = [over_g(ST * D).rearrange("p (s d) -> p s d", d=D) for _ in range(2)]
        b2 = over_g(NE * D).rearrange("p (e d) -> p e d", d=D)
        tok_u = [sb(f"tok_u{n}", [P, ST], U32) for n in range(2)]
        b1e = [sb(f"b1e{n}", [P, MC]) for n in range(2)]
        w1_sb = [stage[:, n, 0:HID] for n in range(2)]
        w2_sb = [stage[:, n, HID:2 * HID].rearrange("p (m d) -> p m d", d=D) for n in range(2)]

        banks = [ctx.enter_context(nc.psum_tensor(f"bank{n}", [P, 512], F32)) for n in range(8)]
        K, (TA, TB, HB, SB, QB) = banks[0:3], banks[3:8]

        slots_dram = nc.dram_tensor("slots", [NE * CAP, RW], F32, kind="Internal").ap()

        names = """ld_m ld_x ld_w ld_b2 consts tanh_ready xb_ready m_mm m_hi_ready m_lo_ready
        ctx_split wv_hi_ready wv_split g_mm g_act g_dve scaled
        st0 st1 st2 st3 mv0 mv1 mv2 mv3 ve0 ve1 ve2 ve3 rs0 rs1 rs2 rs3 xn0 xn1 xn2 xn3
        xn0_t xn1_t xn2_t xn3_t xnT0 xnT1 xnT2 xnT3
        ctA_ready s0_mm nm0_ready p0_ready v0_mm v0_ready ri0_ready p0_t p0T_ready o0_mm x1_ready
        r0_mm er_ready er1_ready sig_ready top_ready topi_ready eq_ready mask_ready den_ready
        den1_ready rden_ready w0_ready h0_mm hw_ready hw_t hwT_ready y0_mm x2_ready
        s1_mm nm1_ready s1_sub p1_exp sum1_ready ri1_ready p1n_ready
        ctD_ready v1_mm v1_ready p1_t p1T_act p1T_dve pv_mm cT_act cT_dve o1_mm x3_ready
        rg_mm nmg_ready eg_ready rig_ready topg_ready topgi_ready oh_ready cw_ready tok_ready
        pos_mm pos_ready carry_ready slot_a slot_b slot_c slot_d slot_e slot_f sidx_ready
        sc0_done sc1_done out_rows init_rows out_pad
        w_load0 w_load1 xe_load0 xe_load1 xeT_mm xeT_act xeT_dve h_mm h_ready y_mm yb_ready yw_ready tok_conv add_done b1_ready yw_tail_ready
        """.split()
        S = namedtuple("Semaphores", names)(*[sem(n) for n in names])

        block = ctx.enter_context(nc.Block())

        LAG = 5
        Batches = namedtuple("Batches", "l a b c d e")

        def at(eng, s, n):
            if not isinstance(n, int) or n > 0:
                eng.wait_ge(s, n)

        def own_wait(eng):
            eng.wait_ge(S.consts, 1)

        def pipeline(eng, step):
            def batches(i):
                if not isinstance(i, int):
                    return Batches(*[i - s for s in range(LAG + 1)])
                return Batches(*[i - s if 0 <= i - s < NB else None for s in range(LAG + 1)])

            for i in range(LAG + 1):
                step(batches(i))
            with eng.Fori(LAG + 2, NB + 1) as i:
                step(batches(i - 1))
            for i in range(NB, NB + LAG):
                step(batches(i))

        def cols(n, w):
            return bass.ds(n * w, w) if not isinstance(n, int) else slice(n * w, n * w + w)

        def one(n):
            return bass.ds(n, 1) if not isinstance(n, int) else slice(n, n + 1)

        def row_of(tensor, n):
            return tensor[:, one(n), :].rearrange("p o d -> p (o d)")

        @block.sync
        def _(sp):
            sp.dma_start(stage[:, 0, :], t["wqT"].rearrange("p m d -> p (m d)")).then_inc(S.ld_m, 16)
            sp.dma_start(stage[:, 1, :], t["wkT"].rearrange("p m d -> p (m d)")).then_inc(S.ld_m, 16)
            sp.dma_start(ctxT[:, :], t["ctxT"]).then_inc(S.ld_m, 16)
            sp.dma_start(stage[:, 2, :], t["wv"]).then_inc(S.ld_m, 16)
            for g, at_g in ((t["g_xattn"], 0), (t["g_ffn"], 2), (t["rscale"], 4)):
                n = g.shape[1]
                sp.dma_start(gates[:, at_g:at_g + n], g.broadcast_to([P, n])).then_inc(S.ld_x, 16)
            sp.dma_start(bout[:, :], t["bout"].broadcast_to([P, D])).then_inc(S.ld_x, 16)
            sp.dma_start(x_sb[:, :, :], t["x"]).then_inc(S.ld_x, 16)
            for dst, name in ((woutT, "woutT"), (selT, "selT"), (keys, "keys"), (wgT, "wgT"), (ind, "ind"),
                              (b1, "b1")):
                sp.dma_start(dst[:, :], t[name]).then_inc(S.ld_w, 16)
            sp.dma_start(vals[:, :, :], t["vals"]).then_inc(S.ld_w, 16)
            sp.dma_start(wo[:, :, :], t["wo"]).then_inc(S.ld_w, 16)
            sp.wait_ge(S.consts, 1)
            for e in range(NE):
                dst = slots_dram[e * CAP:e * CAP + (ST - 1) * P, :].rearrange("(s p) c -> p s c", p=P)
                sp.dma_start(dst, empty[:, 0:ST - 1, :]).then_inc(S.init_rows, 16)
                sp.dma_start(slots_dram[e * CAP + (ST - 1) * P:(e + 1) * CAP, :],
                             empty[0:TAIL, ST - 1, :]).then_inc(S.init_rows, 16)
            sp.dma_start(out[T:T + ST * P, :].rearrange("(s p) d -> p s d", p=P), empty[:, :, 0:D]).then_inc(S.out_pad, 16)

            def step(n):
                if n.d is not None:
                    sp.wait_ge(S.x3_ready, n.d + 1)
                    sp.dma_start(out[cols(n.d, P), :], row_of(res, n.d)).then_inc(S.out_rows, 16)
            pipeline(sp, step)

            def load(e, n):
                at(sp, S.yw_ready, e - 1)
                at(sp, S.yw_tail_ready, e - 1)
                if isinstance(e, int):
                    lo = slice(e * CAP, e * CAP + (ST - 1) * P)
                    hi = slice(e * CAP + (ST - 1) * P, (e + 1) * CAP)
                else:
                    lo = bass.ds(e * CAP, (ST - 1) * P)
                    hi = bass.ds(e * CAP + (ST - 1) * P, TAIL)
                sp.dma_start(xe[n][:, 0:ST - 1, :],
                             slots_dram[lo, :].rearrange("(s p) c -> p s c", p=P)).then_inc((S.xe_load0, S.xe_load1)[n], 16)
                sp.dma_start(xe[n][0:TAIL, ST - 1, :], slots_dram[hi, :]).then_inc((S.xe_load0, S.xe_load1)[n], 16)

            def weights(e, n):
                at(sp, S.y_mm, 2 * (e - 1))
                sp.dma_start(w1_sb[n], t["w1"][one(e), :, :].rearrange("o p h -> p (o h)")).then_inc((S.w_load0, S.w_load1)[n], 16)
                sp.dma_start(w2_sb[n], t["w2"][one(e), :, :, :].rearrange("o p m d -> p (o m) d")).then_inc((S.w_load0, S.w_load1)[n], 16)

            sp.wait_ge(S.m_mm, 4)
            weights(0, 0)
            weights(1, 1)
            sp.wait_ge(S.s1_mm, 3 * NB)
            sp.dma_start(b2, t["b2"][None, :, :].broadcast_to([P, NE, D])).then_inc(S.ld_b2, 16)
            sp.wait_ge(S.sc0_done, 16 * NB)
            sp.wait_ge(S.sc1_done, 16 * NB)
            load(0, 0)
            load(1, 1)
            with sp.Fori(1, NE // 2) as e:
                for n in range(2):
                    load(2 * e + n, n)
                    weights(2 * e + n, n)
            sp.wait_ge(S.add_done, 16 * ST * NE)
            sp.wait_ge(S.out_pad, 16)
            sp.wait_ge(S.out_rows, 16 * NB)

        @block.gpsimd
        def _(pool):
            pool.memset(empty[:, :, :], 0.0)
            pool.memset(mhalf[:, :], -0.5)
            pool.memset(eps[:, :], EPS)
            pool.memset(ones_bf[:, :], 1.0)
            pool.memset(carry[:, :, :], 0.0)
            pool.memset(sgn[:, 0, :], 1.0)
            pool.memset(sgn[:, 1, :], -1.0)
            pool.memset(rows[:, :, :], 0.0)
            pool.iota(iota16[:, :], [[1, NE0]], base=0, channel_multiplier=0, allow_small_or_imprecise_dtypes=True)
            pool.iota(slot0[:, :, :], [[CAP - 1, 2], [CAP, NE]], base=0, channel_multiplier=0,
                      allow_small_or_imprecise_dtypes=True)
            pool.iota(token[:, :], [[NQ, NB]], base=0, channel_multiplier=1, allow_small_or_imprecise_dtypes=True)
            pool.memset(ident[:, :], 0.0).then_inc(S.slot_a, 1)
            pool.wait_ge(S.slot_a, 1)
            pool.iota(empty[:, :, D:D + 1], [[P, ST], [0, 1]], base=T, channel_multiplier=1, allow_small_or_imprecise_dtypes=True)
            pool.affine_select(out=ident[:, :], in_=ident[:, :], compare_op=ALU.not_equal, fill=1.0, base=0,
                               pattern=[[-1, P]], channel_multiplier=1)
            pool.affine_select(out=before[:, :], in_=ones_bf[:, :], compare_op=ALU.is_gt, fill=0.0, base=0,
                               pattern=[[1, P]], channel_multiplier=-1).then_inc(S.consts, 1)
            pool.wait_ge(S.ld_m, 64)
            pool.tensor_copy(wv_hi[:, :], stage[:, 2, :]).then_inc(S.wv_hi_ready, 1)
            pool.wait_ge(S.wv_hi_ready, 1)
            pool.tensor_tensor(wv_lo[:, :], stage[:, 2, :], wv_hi[:, :].bitcast(F32), ALU.subtract).then_inc(S.wv_split, 1)

            def rstd(k, n):
                pool.wait_ge([S.mv0, S.mv1, S.mv2, S.mv3][k], n + 1)
                at(pool, [S.xn0, S.xn1, S.xn2, S.xn3][k], n)
                pool.tensor_tensor(ve[k][:, :], mv[k][:, 1:2], eps[:, :], ALU.add).then_inc([S.ve0, S.ve1, S.ve2, S.ve3][k], 1)
                pool.wait_ge([S.ve0, S.ve1, S.ve2, S.ve3][k], n + 1)
                pool.tensor_tensor(rs[k][:, :], ve[k][:, :], mhalf[:, :], ALU.pow).then_inc([S.rs0, S.rs1, S.rs2, S.rs3][k], 1)

            def step(n):
                if n.a is not None:
                    at(pool, S.v0_mm, n.a)
                    at(pool, S.s0_mm, n.a)
                    pool.tensor_copy(ctA[:, :], ctxT[:, cols(n.a, NK)]).then_inc(S.ctA_ready, 1)
                if n.l is not None:
                    rstd(0, n.l)
                if n.e is not None:
                    at(pool, S.sc0_done, 16 * n.e)
                    at(pool, S.sc1_done, 16 * n.e)
                    pool.tensor_copy(rows[:, :, D:D + 1], token[:, one(n.e)][:, None, :].broadcast_to([P, 2, 1])).then_inc(S.tok_ready, 1)
                if n.c is not None:
                    pool.wait_ge(S.ri1_ready, n.c + 1)
                    at(pool, S.p1_t, 4 * n.c)
                    pool.tensor_tensor(p1n[:, :, :], p1[:, :, :], ri1[:, :, None].broadcast_to([P, NH, NK]),
                                       ALU.mult).then_inc(S.p1n_ready, 1)
                    at(pool, S.v1_mm, 2 * n.c)
                    at(pool, S.v1_ready, 2 * n.c)
                    pool.tensor_copy(ctD_hi[:, :], ctx_hi[:, cols(n.c, NK)].bitcast(F32))
                    pool.tensor_copy(indD[:, :], ind[:, one(n.c)])
                    pool.tensor_copy(ctD_lo[:, :], ctx_lo[:, cols(n.c, NK)].bitcast(F32)).then_inc(S.ctD_ready, 1)
                if n.a is not None:
                    rstd(1, n.a)
                if n.e is not None:
                    pool.wait_ge(S.pos_ready, n.e + 1)
                    pool.wait_ge(S.carry_ready, n.e + 1)
                    at(pool, S.sidx_ready, n.e)
                    k = 1 + n.e
                    pool.tensor_tensor(slot[:, :, :], pos[:, :, :], sgn[:, :, :], ALU.mult).then_inc(S.slot_a, 1)
                    pool.wait_ge(S.slot_a, k + 1)
                    pool.tensor_tensor(slot[:, :, :], slot[:, :, :], slot0[:, :, :], ALU.add).then_inc(S.slot_b, 1)
                    pool.tensor_tensor(pos[:, 1, :], pos[:, 1, :], carry[:, 0, :], ALU.add).then_inc(S.slot_c, 1)
                    own_wait(pool)
                    pool.wait_ge(S.slot_c, k)
                    pool.tensor_scalar(over[:, :, :], pos[:, :, :], float(CAP), BIG, ALU.is_ge, ALU.mult).then_inc(S.slot_d, 1)
                    pool.wait_ge(S.slot_b, k)
                    pool.wait_ge(S.slot_d, k)
                    pool.tensor_tensor(slot[:, :, :], slot[:, :, :], over[:, :, :], ALU.add).then_inc(S.slot_e, 1)
                    pool.wait_ge(S.slot_e, k)
                    pool.tensor_tensor(slot[:, :, :], slot[:, :, :], oh[:, :, :], ALU.mult).then_inc(S.slot_f, 1)
                if n.d is not None:
                    rstd(3, n.d)
                if n.b is not None:
                    rstd(2, n.b)
                if n.e is not None:
                    own_wait(pool)
                    pool.wait_ge(S.sidx_ready, n.e + 1)
                    pool.wait_ge(S.cw_ready, n.e + 1)
                    pool.wait_ge(S.tok_ready, n.e + 1)
                    if isinstance(n.e, int) and n.e == 0:
                        pool.wait_ge(S.init_rows, 32 * NE)
                    for k, done in ((0, S.sc0_done), (1, S.sc1_done)):
                        pool.indirect_dma_start(slots_dram, bass.IndirectOffsetOnAxis(ap=sidx[:, k:k + 1], axis=0),
                                                rows[:, k, :], None, bounds_check=NE * CAP - 1,
                                                oob_is_err=False).then_inc(done, 16)
            pipeline(pool, step)

            pool.wait_ge(S.out_rows, 16 * NB)
            pool.wait_ge(S.out_pad, 16)

            def bias(e, n):
                at(pool, S.h_ready, 2 * MC * (e - 1))
                pool.tensor_copy(b1e[n][:, :], b1[:, cols(e, MC)]).then_inc(S.b1_ready, 1)

            def add(e, n):
                pool.wait_ge(S.tok_conv, e + 1)
                pool.wait_ge(S.yb_ready, 2 * e + 2)
                at(pool, S.add_done, 16 * ST * e)
                pool.tensor_tensor(ye[n][0:TAIL, ST - 1, :], ye[n][0:TAIL, ST - 1, :],
                                   xe[n][0:TAIL, ST - 1, D + 1:D + 2].broadcast_to([TAIL, D]), ALU.mult).then_inc(S.yw_tail_ready, 1)
                own_wait(pool)
                pool.wait_ge(S.tok_conv, e + 1)
                pool.wait_ge(S.yw_ready, e + 1)
                for s in range(ST):
                    k = P if s < ST - 1 else TAIL
                    if s == ST - 1:
                        own_wait(pool)
                        pool.wait_ge(S.yw_tail_ready, e + 1)
                    pool.indirect_dma_start(out, bass.IndirectOffsetOnAxis(ap=tok_u[n][0:k, s:s + 1], axis=0),
                                            ye[n][0:k, s, :], None, bounds_check=T + ST * P - 1, oob_is_err=True,
                                            compute_op=ALU.add).then_inc(S.add_done, 16)
            bias(0, 0)
            bias(1, 1)
            add(0, 0)
            with pool.Fori(1, NE // 2) as e:
                bias(2 * e, 0)
                add(2 * e - 1, 1)
                bias(2 * e + 1, 1)
                add(2 * e, 0)
            add(NE - 1, 1)

        @block.tensor
        def _(pe):
            ctx_hi4 = ctx_hi[:, :]
            ctx_lo4 = ctx_lo[:, :]
            pe.wait_ge(S.ld_m, 64)
            for q in range(4):
                for j in range(4):
                    h = 4 * q + j
                    r = slice(HD * (h % 2), HD * (h % 2) + HD)
                    c = slice(P * (h // 2), P * (h // 2) + P)
                    mm = pe.matmul(banks[q + 4 * (h % 2)][:, P * (j // 2):P * (j // 2) + P], stage[r, 1, c], stage[r, 0, c], start=True, stop=True)
                mm.then_inc(S.m_mm, 1)
            pe.wait_ge(S.m_lo_ready, 8)
            pe.wait_ge(S.ctx_split, 2)

            def g_group(g):
                for h in range(NH):
                    k = NH // 2 * g + h // 2
                    at(pe, S.g_act if h % 2 == 0 else S.g_dve, k - 3)
                    c = cols(g, GN)
                    w = slice(P * h, P * h + P)
                    dst = banks[h % 8][:, 0:GN]
                    pe.matmul(dst, m_hi[:, w], ctx_hi[:, c], start=True, stop=False)
                    pe.matmul(dst, m_hi[:, w], ctx_lo[:, c], start=False, stop=False)
                    pe.matmul(dst, m_lo[:, w], ctx_hi[:, c], start=False, stop=True).then_inc(S.g_mm, 1)
            g_group(0)
            with pe.Fori(1, NB // GB) as g:
                g_group(g)
            pe.wait_ge(S.g_act, NB // GB * NH // 2)
            pe.wait_ge(S.g_dve, NB // GB * NH // 2)
            pe.wait_ge(S.scaled, 3)
            pe.wait_ge(S.wv_split, 1)
            pe.wait_ge(S.consts, 1)
            pe.wait_ge(S.ld_w, 16 * 8)

            def step(n):
                if n.a is not None:
                    pe.wait_ge(S.xn0, n.a + 1)
                    at(pe, S.x1_ready, n.a)
                    at(pe, S.carry_ready, n.a - 4)
                    at(pe, S.pos_ready, n.a - 4)
                    pe.transpose(SB[:, 0:P], xn[0][:, :], ident[:, :]).then_inc(S.xn0_t, 1)
                if n.d is not None:
                    pe.wait_ge(S.ctD_ready, n.d + 1)
                    at(pe, S.cT_act, n.d)
                    at(pe, S.cT_dve, n.d)
                    for j, bank in enumerate((TA, TB)):
                        c = slice(512 * j, 512 * j + 512)
                        pe.matmul(bank[0:NK, :], ctD_hi[:, :], wv_hi[:, c], start=True, stop=False)
                        pe.matmul(bank[0:NK, :], ctD_hi[:, :], wv_lo[:, c], start=False, stop=False)
                        pe.matmul(bank[0:NK, :], ctD_lo[:, :], wv_hi[:, c], start=False, stop=True).then_inc(S.v1_mm, 1)
                if n.a is not None:
                    pe.wait_ge(S.xnT0, n.a + 1)
                    pe.wait_ge(S.ctA_ready, n.a + 1)
                    pe.matmul(SB[:, 0:NK], xnT[0][:, :], ctA[:, :], start=True, stop=True).then_inc(S.s0_mm, 1)
                    at(pe, S.x3_ready, n.a - 3)
                    at(pe, S.er_ready, n.a - 1)
                    at(pe, S.xnT2, n.a - 2)
                    at(pe, S.v0_ready, n.a)
                    pe.matmul(QB[0:NK, 0:D], ctA[:, :], woutT[:, :], start=True, stop=True).then_inc(S.v0_mm, 1)
                if n.e is not None:
                    pe.wait_ge(S.xn3, n.e + 1)
                    at(pe, S.x2_ready, min(n.e + 3, NB) if isinstance(n.e, int) else n.e + 3)
                    at(pe, S.eg_ready, n.e)
                    at(pe, S.nmg_ready, n.e)
                    pe.transpose(HB[:, 0:P], rows[:, 0, 0:D], ident[:, :]).then_inc(S.xn3_t, 1)
                if n.d is not None:
                    pe.wait_ge(S.p1n_ready, n.d + 1)
                    for j, bank in enumerate((TA, TB)):
                        pe.wait_ge(S.v1_ready, 2 * n.d + 1 + j)
                        for h in range(4 * j, 4 * j + 4):
                            mm = pe.transpose(bank[0:NK, P * (h % 4):P * (h % 4) + P], p1n[:, h, :], ident[:, :])
                        mm.then_inc(S.p1_t, 1)
                if n.c is not None:
                    pe.wait_ge(S.xn2, n.c + 1)
                    if n.a is not None:
                        pe.wait_ge(S.v0_ready, n.a + 1)
                    else:
                        at(pe, S.x3_ready, n.c - 1)
                    pe.transpose(QB[:, 0:P], xn[2][:, :], ident[:, :]).then_inc(S.xn2_t, 1)
                if n.e is not None:
                    pe.wait_ge(S.xnT3, n.e + 1)
                    pe.matmul(HB[:, 0:NE], xnT[3][:, :], wgT[:, :], start=True, stop=True).then_inc(S.rg_mm, 1)
                if n.a is not None:
                    pe.wait_ge(S.p0_ready, n.a + 1)
                    pe.transpose(SB[0:NK, 0:P], p0[:, :], ident[:, :]).then_inc(S.p0_t, 1)
                if n.c is not None:
                    pe.wait_ge(S.xnT2, n.c + 1)
                    for j in range(3):
                        at(pe, S.s1_sub, 3 * n.c - 2 + j if not isinstance(n.c, int) or n.c > 0 else 0)
                        a, b = HCUT[j] * NK, HCUT[j + 1] * NK
                        g_row = row_of(G, n.c)
                        pe.matmul(K[j][:, 0:b - a], xnT[2][:, :], g_row[:, a:b], start=True, stop=True).then_inc(S.s1_mm, 1)
                if n.d is not None:
                    for j, bank in enumerate((TA, TB)):
                        pe.wait_ge(S.p1T_act if j == 0 else S.p1T_dve, 2 * n.d + 1)
                        for h in range(8 + 4 * j, 12 + 4 * j):
                            mm = pe.transpose(bank[0:NK, P * (h % 4):P * (h % 4) + P], p1n[:, h, :], ident[:, :])
                        mm.then_inc(S.p1_t, 1)
                if n.b is not None:
                    pe.wait_ge(S.xn1, n.b + 1)
                    if n.e is not None:
                        pe.wait_ge(S.eg_ready, n.e + 1)
                        pe.wait_ge(S.nmg_ready, n.e + 1)
                    at(pe, S.x2_ready, n.b)
                    pe.transpose(HB[:, 0:P], xn[1][:, :], ident[:, :]).then_inc(S.xn1_t, 1)
                if n.a is not None:
                    pe.wait_ge(S.p0T_ready, n.a + 1)
                    pe.wait_ge(S.v0_ready, n.a + 1)
                    pe.matmul(SB[:, 0:D], p0T[:, :], v0[:, :], start=True, stop=True).then_inc(S.o0_mm, 1)
                if n.b is not None:
                    pe.wait_ge(S.xnT1, n.b + 1)
                    if n.c is not None:
                        pe.wait_ge(S.xnT2, n.c + 1)
                    if n.a is not None:
                        pe.wait_ge(S.v0_ready, n.a + 1)
                    at(pe, S.x3_ready, n.b - 2)
                    at(pe, S.er_ready, n.b)
                    pe.matmul(QB[:, 0:NE0], xnT[1][:, :], selT[:, :], start=True, stop=True).then_inc(S.r0_mm, 1)
                    pe.matmul(HB[:, :], xnT[1][:, :], keys[:, :], start=True, stop=True).then_inc(S.h0_mm, 1)
                if n.d is not None:
                    pe.wait_ge(S.v1_ready, 2 * n.d + 2)
                    for j, bank in enumerate((TA, TB)):
                        pe.wait_ge(S.p1T_act, 2 * n.d + 2)
                        pe.wait_ge(S.p1T_dve, 2 * n.d + 2)
                        for m in range(4 * j, 4 * j + 4):
                            for o in range(2):
                                h = 2 * m + o
                                mm = pe.matmul(bank[HD * o:HD * o + HD, P * (m % 4):P * (m % 4) + P],
                                               v1[:, HD * h:HD * h + HD], p1T[:, P * h:P * h + P], start=True, stop=True)
                        mm.then_inc(S.pv_mm, 1)
                if n.e is not None:
                    pe.wait_ge(S.oh_ready, n.e + 1)
                    if n.a is not None:
                        pe.wait_ge(S.x1_ready, n.a + 1)
                    at(pe, S.pos_ready, n.e)
                    at(pe, S.carry_ready, n.e)
                    ohf = oh[:, :, :].rearrange("p k e -> p (k e)")
                    pe.matmul(SB[:, 0:2 * NE], before[:, :], ohf, start=True, stop=True)
                    pe.matmul(SB[:, 2 * NE:4 * NE], ones_bf[:, :], ohf, start=True, stop=True).then_inc(S.pos_mm, 1)
                if n.d is not None:
                    pe.wait_ge(S.cT_act, n.d + 1)
                    pe.wait_ge(S.cT_dve, n.d + 1)
                    if n.b is not None:
                        pe.wait_ge(S.er_ready, n.b + 1)
                    if n.c is not None:
                        pe.wait_ge(S.xnT2, n.c + 1)
                    at(pe, S.x3_ready, n.d)
                    for m in range(NH * HD // P):
                        mm = pe.matmul(QB[:, 0:D], cT[:, m, :], wo[:, m, :], start=m == 0, stop=m == NH * HD // P - 1)
                    mm.then_inc(S.o1_mm, 1)
                if n.b is not None:
                    pe.wait_ge(S.hw_ready, n.b + 1)
                    for m in range(H0 // P):
                        mm = pe.transpose(HB[:, P * m:P * m + P], hw[:, P * m:P * m + P], ident[:, :])
                    mm.then_inc(S.hw_t, 1)
                    pe.wait_ge(S.hwT_ready, n.b + 1)
                    for m in range(H0 // P):
                        mm = pe.matmul(HB[:, 0:D], hwT[:, P * m:P * m + P], vals[:, m, :], start=m == 0, stop=m == H0 // P - 1)
                    mm.then_inc(S.y0_mm, 1)
            pipeline(pe, step)

            def expert(e, n):
                pe.wait_ge((S.xe_load0, S.xe_load1)[n], 16 * (e - n) + 32)
                at(pe, S.xeT_act, e)
                at(pe, S.xeT_dve, e)
                for s in range(ST):
                    k = P if s < ST - 1 else TAIL
                    mm = pe.transpose(banks[s // 4][:, P * (s % 4):P * (s % 4) + k], xe[n][0:k, s, 0:D], ident[0:k, 0:k])
                mm.then_inc(S.xeT_mm, 1)
                pe.wait_ge((S.w_load0, S.w_load1)[n], 16 * (e - n) + 32)
                pe.wait_ge(S.xeT_act, e + 1)
                pe.wait_ge(S.xeT_dve, e + 1)
                for m in range(MC):
                    for j in range(2):
                        k = 2 * m + j
                        at(pe, S.h_ready, 2 * MC * e + k - 3)
                        pe.matmul(banks[2 + k % 4][:, 0:HALF], w1_sb[n][:, P * m:P * m + P],
                                  xeT[n][:, HALF * j:HALF * j + HALF], start=True, stop=True).then_inc(S.h_mm, 1)
                pe.wait_ge(S.h_ready, 2 * MC * (e + 1))
                at(pe, S.yb_ready, 2 * e)
                for s in range(ST):
                    k = P if s < ST - 1 else TAIL
                    for m in range(MC):
                        mm = pe.matmul(banks[6 + s // 4][0:k, P * (s % 4):P * (s % 4) + D], hT[n][:, m, P * s:P * s + k],
                                       w2_sb[n][:, m, :], start=m == 0, stop=m == MC - 1)
                    if s >= ST - 2:
                        mm.then_inc(S.y_mm, 1)
            expert(0, 0)
            expert(1, 1)
            with pe.Fori(1, NE // 2) as e:
                for n in range(2):
                    expert(2 * e + n, n)

        @block.scalar
        def _(act):
            act.wait_ge(S.ld_x, 16 * 5)
            act.activation(tg[:, :], gates[:, 0:4], ACT.Tanh, bias=0.0).then_inc(S.tanh_ready, 1)
            for q in range(4):
                act.wait_ge(S.m_mm, q + 1)
                for o in range(2):
                    dst = m_hi[:, :].rearrange("p (h d) -> p h d", d=P)[:, 4 * q + o:4 * q + o + 3:2, :]
                    act.copy(dst, banks[q + 4 * o][:, 0:2 * P].rearrange("p (h d) -> p h d", d=P)).then_inc(S.m_hi_ready, 1)

            def g_group(g):
                for h in range(0, NH, 2):
                    act.wait_ge(S.g_mm, NH * g + h + 1)
                    dst = G[:, cols(g, GB), NK * h:NK * h + NK]
                    act.copy(dst, banks[h % 8][:, 0:GN].rearrange("p (b k) -> p b k", k=NK)).then_inc(S.g_act, 1)
            g_group(0)
            with act.Fori(1, NB // GB) as g:
                g_group(g)

            def step(n):
                if n.a is not None:
                    act.wait_ge(S.xn0_t, n.a + 1)
                    at(act, S.s0_mm, n.a)
                    act.mul(xnT[0][:, :], SB[:, 0:P], float(D) ** -0.5).then_inc(S.xnT0, 1)
                if n.d is not None:
                    for j, bank in enumerate((TA, TB)):
                        act.wait_ge(S.v1_mm, 2 * n.d + 1 + j)
                        at(act, S.pv_mm, 2 * n.d)
                        act.activation(v1[:, 512 * j:512 * j + 512], bank[0:NK, :], ACT.Copy,
                                       scale=indD[:, :]).then_inc(S.v1_ready, 1)
                if n.a is not None:
                    act.wait_ge(S.v0_mm, n.a + 1)
                    at(act, S.o0_mm, n.a)
                    act.activation(v0[:, :], QB[0:NK, 0:D], ACT.Copy, scale=tg[0:NK, 0:1]).then_inc(S.v0_ready, 1)
                    act.wait_ge(S.nm0_ready, n.a + 1)
                    at(act, S.p0_t, n.a)
                    at(act, S.ri0_ready, n.a)
                    act.activation(p0[:, :], SB[:, 0:NK], ACT.Exp, bias=nm0[:, :], accum_out=sum0[:, :]).then_inc(S.p0_ready, 1)
                if n.e is not None:
                    act.wait_ge(S.xn3_t, n.e + 1)
                    act.copy(xnT[3][:, :], HB[:, 0:P]).then_inc(S.xnT3, 1)
                if n.d is not None:
                    act.wait_ge(S.p1_t, 4 * n.d + 1)
                    act.copy(p1T[:, 0:512], TA[0:NK, :]).then_inc(S.p1T_act, 1)
                if n.c is not None:
                    act.wait_ge(S.xn2_t, n.c + 1)
                    at(act, S.s1_mm, 3 * n.c)
                    act.mul(xnT[2][:, :], QB[:, 0:P], float(HD) ** -0.5).then_inc(S.xnT2, 1)
                if n.e is not None:
                    act.wait_ge(S.nmg_ready, n.e + 1)
                    at(act, S.topgi_ready, n.e)
                    at(act, S.rig_ready, n.e)
                    act.activation(eg[:, :], HB[:, 0:NE], ACT.Exp, bias=nmg[:, :], accum_out=sumg[:, :]).then_inc(S.eg_ready, 1)
                if n.a is not None:
                    act.wait_ge(S.p0_t, n.a + 1)
                    act.copy(p0T[:, :], SB[0:NK, 0:P]).then_inc(S.p0T_ready, 1)
                if n.c is not None:
                    for j in range(3):
                        act.wait_ge(S.s1_sub, 3 * n.c + 1 + j)
                        h = slice(HCUT[j], HCUT[j + 1])
                        act.activation(p1[:, h, :], p1[:, h, :], ACT.Exp, bias=0.0).then_inc(S.p1_exp, 1)
                if n.d is not None:
                    act.wait_ge(S.p1_t, 4 * n.d + 3)
                    act.copy(p1T[:, 1024:1536], TA[0:NK, :]).then_inc(S.p1T_act, 1)
                if n.b is not None:
                    act.wait_ge(S.xn1_t, n.b + 1)
                    act.copy(xnT[1][:, :], HB[:, 0:P]).then_inc(S.xnT1, 1)
                    act.wait_ge(S.r0_mm, n.b + 1)
                    at(act, S.er1_ready, n.b)
                    act.activation(er[:, :], QB[:, 0:NE0], ACT.Exp, bias=0.0, scale=-1.0).then_inc(S.er_ready, 1)
                if n.d is not None:
                    act.wait_ge(S.pv_mm, 2 * n.d + 1)
                    at(act, S.o1_mm, n.d)
                    act.copy(cT[:, 0:4, :], TA[:, :].rearrange("p (m q) -> p m q", q=NQ)).then_inc(S.cT_act, 1)
                if n.b is not None:
                    act.wait_ge(S.hw_t, n.b + 1)
                    act.copy(hwT[:, :], HB[:, :]).then_inc(S.hwT_ready, 1)
            pipeline(act, step)

            def expert(e, n):
                act.wait_ge(S.xeT_mm, e + 1)
                act.copy(xeT[n][:, 0:512], banks[0][:, :]).then_inc(S.xeT_act, 1)
                for m in range(MC):
                    for j in range(2):
                        k = 2 * m + j
                        act.wait_ge(S.h_mm, 2 * MC * e + k + 1)
                        at(act, S.y_mm, 2 * (e - 1))
                        act.wait_ge(S.b1_ready, e + 1)
                        act.activation(hT[n][:, m, HALF * j:HALF * j + HALF], banks[2 + k % 4][:, 0:HALF], ACT.Gelu,
                                       bias=b1e[n][:, m:m + 1]).then_inc(S.h_ready, 1)
            expert(0, 0)
            expert(1, 1)
            with act.Fori(1, NE // 2) as e:
                for n in range(2):
                    expert(2 * e + n, n)

        @block.vector
        def _(dve):
            dve.wait_ge(S.ld_m, 64)
            dve.tensor_copy(ctx_hi[:, :], ctxT[:, :]).then_inc(S.ctx_split, 1)
            dve.wait_ge(S.ctx_split, 1)
            dve.tensor_tensor(ctx_lo[:, :], ctxT[:, :], ctx_hi[:, :].bitcast(F32), ALU.subtract).then_inc(S.ctx_split, 1)
            for q in range(4):
                for o in range(2):
                    dve.wait_ge(S.m_hi_ready, 2 * q + o + 1)
                    h = slice(4 * q + o, 4 * q + o + 3, 2)
                    hi = m_hi[:, :].rearrange("p (h d) -> p h d", d=P)[:, h, :].bitcast(F32)
                    lo = m_lo[:, :].rearrange("p (h d) -> p h d", d=P)[:, h, :]
                    dve.tensor_tensor(lo, banks[q + 4 * o][:, 0:2 * P].rearrange("p (h d) -> p h d", d=P), hi,
                                      ALU.subtract).then_inc(S.m_lo_ready, 1)

            def g_group(g):
                for h in range(1, NH, 2):
                    dve.wait_ge(S.g_mm, NH * g + h + 1)
                    dst = G[:, cols(g, GB), NK * h:NK * h + NK]
                    dve.tensor_copy(dst, banks[h % 8][:, 0:GN].rearrange("p (b k) -> p b k", k=NK)).then_inc(S.g_dve, 1)
            g_group(0)
            with dve.Fori(1, NB // GB) as g:
                g_group(g)
            dve.wait_ge(S.tanh_ready, 1)
            dve.wait_ge(S.ld_w, 16 * 8)
            dve.tensor_tensor(valg[:, :], tg[:, 2:3], gates[:, 4:5], ALU.mult).then_inc(S.scaled, 1)
            dve.wait_ge(S.scaled, 1)
            dve.tensor_scalar(vals[:, :, :], vals[:, :, :], valg[:, :], None, ALU.mult).then_inc(S.scaled, 1)
            dve.tensor_scalar(wo[:, :, :], wo[:, :, :], tg[:, 1:2], None, ALU.mult).then_inc(S.scaled, 1)
            dve.tensor_scalar(bout[:, :], bout[:, :], tg[:, 0:1], None, ALU.mult).then_inc(S.xb_ready, 1)
            dve.wait_ge(S.xb_ready, 1)
            dve.tensor_tensor(res[:, :, :], x_sb[:, :, :], bout[:, None, :].broadcast_to([P, NB, D]),
                              ALU.add).then_inc(S.xb_ready, 1)
            dve.wait_ge(S.xb_ready, 2)
            dve.wait_ge(S.consts, 1)

            def stats(k, n, src, src_ready):
                own_wait(dve)
                if src_ready is not None:
                    dve.wait_ge(src_ready, n + 1)
                dve.bn_stats(st[k][:, :], row_of(src, n)).then_inc([S.st0, S.st1, S.st2, S.st3][k], 1)
                own_wait(dve)
                dve.wait_ge([S.st0, S.st1, S.st2, S.st3][k], n + 1)
                at(dve, [S.rs0, S.rs1, S.rs2, S.rs3][k], n)
                dve.bn_aggr(mv[k][:, :], st[k][:, :]).then_inc([S.mv0, S.mv1, S.mv2, S.mv3][k], 1)

            def normed(k, n, src, dst, reader):
                dve.wait_ge([S.mv0, S.mv1, S.mv2, S.mv3][k], n + 1)
                dve.wait_ge([S.rs0, S.rs1, S.rs2, S.rs3][k], n + 1)
                at(dve, reader, n)
                dve.tensor_scalar(dst, row_of(src, n), mv[k][:, 0:1], rs[k][:, :], ALU.subtract,
                                  ALU.mult).then_inc([S.xn0, S.xn1, S.xn2, S.xn3][k], 1)

            def step(n):
                if n.l is not None:
                    stats(0, n.l, x_sb, None)
                if n.a is not None:
                    dve.wait_ge(S.s0_mm, n.a + 1)
                    at(dve, S.p0_ready, n.a)
                    dve.tensor_reduce(nm0[:, :], SB[:, 0:NK], AX.X, ALU.max, negate=True).then_inc(S.nm0_ready, 1)
                if n.l is not None:
                    normed(0, n.l, x_sb, xn[0][:, :], S.xn0_t)
                if n.d is not None:
                    dve.wait_ge(S.p1_t, 4 * n.d + 2)
                    dve.tensor_copy(p1T[:, 512:1024], TB[0:NK, :]).then_inc(S.p1T_dve, 1)
                if n.a is not None:
                    dve.wait_ge(S.p0_ready, n.a + 1)
                    at(dve, S.x1_ready, n.a)
                    dve.reciprocal(ri0[:, :], sum0[:, :]).then_inc(S.ri0_ready, 1)
                if n.e is not None:
                    dve.wait_ge(S.rg_mm, n.e + 1)
                    at(dve, S.eg_ready, n.e)
                    dve.tensor_reduce(nmg[:, :], HB[:, 0:NE], AX.X, ALU.max, negate=True).then_inc(S.nmg_ready, 1)
                if n.c is not None:
                    at(dve, S.p1n_ready, n.c)
                    for j in range(3):
                        h = slice(HCUT[j], HCUT[j + 1])
                        nh = HCUT[j + 1] - HCUT[j]
                        s1 = K[j][:, 0:nh * NK].rearrange("p (h k) -> p h k", k=NK)
                        dve.wait_ge(S.s1_mm, 3 * n.c + 1 + j)
                        dve.tensor_reduce(nm1[:, h], s1, AX.X, ALU.max, negate=True).then_inc(S.nm1_ready, 1)
                        dve.wait_ge(S.nm1_ready, 3 * n.c + 1 + j)
                        dve.tensor_tensor(p1[:, h, :], s1, nm1[:, h, None].broadcast_to([P, nh, NK]),
                                          ALU.add).then_inc(S.s1_sub, 1)
                if n.d is not None:
                    dve.wait_ge(S.p1_t, 4 * n.d + 4)
                    dve.tensor_copy(p1T[:, 1536:2048], TB[0:NK, :]).then_inc(S.p1T_dve, 1)
                if n.e is not None:
                    own_wait(dve)
                    dve.wait_ge(S.eg_ready, n.e + 1)
                    dve.max(topg[:, :], eg[:, :]).then_inc(S.topg_ready, 1)
                    dve.reciprocal(rig[:, :], sumg[:, :]).then_inc(S.rig_ready, 1)
                    own_wait(dve)
                    dve.wait_ge(S.topg_ready, n.e + 1)
                    dve.max_index(topgi[:, :], topg[:, :], eg[:, :]).then_inc(S.topgi_ready, 1)
                    dve.wait_ge(S.rig_ready, n.e + 1)
                    dve.tensor_scalar(rows[:, :, D + 1:D + 2], topg[:, 0:2][:, :, None], rig[:, :], tg[:, 3:4], ALU.mult,
                                      ALU.mult).then_inc(S.cw_ready, 1)
                if n.a is not None:
                    dve.wait_ge(S.o0_mm, n.a + 1)
                    dve.wait_ge(S.ri0_ready, n.a + 1)
                    dve.scalar_tensor_tensor(out=row_of(res, n.a), in0=SB[:, 0:D], scalar=ri0[:, :], in1=row_of(res, n.a),
                                             op0=ALU.mult, op1=ALU.add).then_inc(S.x1_ready, 1)
                if n.e is not None:
                    dve.wait_ge(S.topgi_ready, n.e + 1)
                    at(dve, S.slot_f, n.e)
                    at(dve, S.pos_mm, n.e)
                    dve.tensor_tensor(oh[:, :, :], iota16[:, None, 0:NE].broadcast_to([P, 2, NE]),
                                      topgi[:, 0:2, None].broadcast_to([P, 2, NE]), ALU.is_equal).then_inc(S.oh_ready, 1)
                if n.a is not None:
                    stats(1, n.a, res, S.x1_ready)
                if n.c is not None:
                    dve.wait_ge(S.p1_exp, 3 * n.c + 3)
                    dve.tensor_reduce(sum1[:, :], p1[:, :, :], AX.X, ALU.add).then_inc(S.sum1_ready, 1)
                    dve.wait_ge(S.sum1_ready, n.c + 1)
                    dve.reciprocal(ri1[:, :], sum1[:, :]).then_inc(S.ri1_ready, 1)
                if n.b is not None:
                    dve.wait_ge(S.er_ready, n.b + 1)
                    dve.tensor_scalar(er1[:, :], er[:, :], 1.0, None, ALU.add).then_inc(S.er1_ready, 1)
                    dve.wait_ge(S.er1_ready, n.b + 1)
                    dve.reciprocal(sig[:, :], er1[:, :]).then_inc(S.sig_ready, 1)
                    own_wait(dve)
                    dve.wait_ge(S.sig_ready, n.b + 1)
                    dve.max(top[:, :], sig[:, :]).then_inc(S.top_ready, 1)
                if n.a is not None:
                    normed(1, n.a, res, xn[1][:, :], S.xn1_t)
                if n.b is not None:
                    own_wait(dve)
                    dve.wait_ge(S.top_ready, n.b + 1)
                    dve.max_index(topi[:, :], top[:, :], sig[:, :]).then_inc(S.topi_ready, 1)
                    dve.tensor_reduce(den[:, :], top[:, 0:TOPK0], AX.X, ALU.add).then_inc(S.den_ready, 1)
                    dve.wait_ge(S.topi_ready, n.b + 1)
                    dve.tensor_tensor(eq[:, :, :], iota16[:, None, :].broadcast_to([P, TOPK0, NE0]),
                                      topi[:, 0:TOPK0, None].broadcast_to([P, TOPK0, NE0]), ALU.is_equal).then_inc(S.eq_ready, 1)
                    dve.wait_ge(S.den_ready, n.b + 1)
                    dve.tensor_scalar(den1[:, :], den[:, :], 1e-9, None, ALU.max).then_inc(S.den1_ready, 1)
                    dve.wait_ge(S.eq_ready, n.b + 1)
                    dve.tensor_reduce(mask[:, :], eq[:, :, :].rearrange("p k e -> p e k"), AX.X, ALU.add).then_inc(S.mask_ready, 1)
                    dve.wait_ge(S.den1_ready, n.b + 1)
                    dve.reciprocal(rden[:, :], den1[:, :]).then_inc(S.rden_ready, 1)
                    dve.wait_ge(S.rden_ready, n.b + 1)
                    dve.wait_ge(S.mask_ready, n.b + 1)
                    dve.scalar_tensor_tensor(out=w0[:, :], in0=sig[:, :], scalar=rden[:, :], in1=mask[:, :], op0=ALU.mult,
                                             op1=ALU.mult).then_inc(S.w0_ready, 1)
                    dve.wait_ge(S.w0_ready, n.b + 1)
                    dve.wait_ge(S.h0_mm, n.b + 1)
                    at(dve, S.hw_t, n.b)
                    dve.scalar_tensor_tensor(out=hw[:, :].rearrange("p (e s) -> p e s", s=ES),
                                             in0=HB[:, :].rearrange("p (e s) -> p e s", s=ES), scalar=0.0,
                                             in1=w0[:, :, None].broadcast_to([P, NE0, ES]), op0=ALU.max,
                                             op1=ALU.mult).then_inc(S.hw_ready, 1)
                if n.d is not None:
                    dve.wait_ge(S.pv_mm, 2 * n.d + 2)
                    at(dve, S.o1_mm, n.d)
                    dve.tensor_copy(cT[:, 4:8, :], TB[:, :].rearrange("p (m q) -> p m q", q=NQ)).then_inc(S.cT_dve, 1)
                if n.e is not None:
                    dve.wait_ge(S.pos_mm, n.e + 1)
                    at(dve, S.slot_e, n.e)
                    dve.tensor_tensor(pos[:, :, :], SB[:, 0:2 * NE].rearrange("p (k e) -> p k e", k=2), carry[:, :, :],
                                      ALU.add).then_inc(S.pos_ready, 1)
                    dve.tensor_tensor(carry[:, :, :], SB[:, 2 * NE:4 * NE].rearrange("p (k e) -> p k e", k=2), carry[:, :, :],
                                      ALU.add).then_inc(S.carry_ready, 1)
                if n.d is not None:
                    dve.wait_ge(S.o1_mm, n.d + 1)
                    dve.tensor_tensor(row_of(res, n.d), QB[:, 0:D], row_of(res, n.d), ALU.add).then_inc(S.x3_ready, 1)
                    stats(3, n.d, res, S.x3_ready)
                if n.e is not None:
                    dve.wait_ge(S.slot_f, n.e + 1)
                    at(dve, S.sc0_done, 16 * n.e)
                    at(dve, S.sc1_done, 16 * n.e)
                    with nc.allow_low_precision(reason="one whole number below 2^24 and zeros"):
                        dve.tensor_reduce(sidx[:, :], slot[:, :, :], AX.X, ALU.add).then_inc(S.sidx_ready, 1)
                if n.b is not None:
                    dve.wait_ge(S.y0_mm, n.b + 1)
                    dve.tensor_tensor(row_of(res, n.b), HB[:, 0:D], row_of(res, n.b), ALU.add).then_inc(S.x2_ready, 1)
                    stats(2, n.b, res, S.x2_ready)
                if n.d is not None:
                    dve.wait_ge(S.mv3, n.d + 1)
                    dve.wait_ge(S.rs3, n.d + 1)
                    at(dve, S.xn3_t, n.d)
                    at(dve, S.sc0_done, 16 * n.d)
                    at(dve, S.sc1_done, 16 * n.d)
                    x3 = res[:, one(n.d), :].broadcast_to([P, 2, D])
                    dve.tensor_scalar(rows[:, :, 0:D], x3, mv[3][:, 0:1], rs[3][:, :], ALU.subtract, ALU.mult).then_inc(S.xn3, 1)
                if n.b is not None:
                    normed(2, n.b, res, xn[2][:, :], S.xn2_t)
            pipeline(dve, step)

            dve.wait_ge(S.ld_b2, 16)

            def expert(e, n):
                dve.wait_ge(S.xeT_mm, e + 1)
                dve.tensor_copy(xeT[n][:, 512:CAP], banks[1][:, 0:TAIL]).then_inc(S.xeT_dve, 1)
                b2e = b2[:, one(e), :]
                dve.wait_ge((S.xe_load0, S.xe_load1)[n], 16 * (e - n) + 32)
                at(dve, S.add_done, 16 * ST * (e - 1))
                dve.tensor_copy(tok_u[n][:, 0:ST - 1], xe[n][:, 0:ST - 1, D])
                dve.tensor_copy(tok_u[n][0:TAIL, ST - 1:ST], xe[n][0:TAIL, ST - 1, D:D + 1]).then_inc(S.tok_conv, 1)
                dve.wait_ge(S.y_mm, 2 * e + 1)
                at(dve, S.add_done, 16 * ST * (e - 1))
                dve.tensor_tensor(ye[n][:, 0:ST - 1, :], banks[6][:, :].rearrange("p (s d) -> p s d", d=D),
                                  b2e.broadcast_to([P, ST - 1, D]), ALU.add).then_inc(S.yb_ready, 1)
                dve.wait_ge(S.y_mm, 2 * e + 2)
                dve.tensor_tensor(ye[n][0:TAIL, ST - 1, :], banks[7][0:TAIL, 0:D],
                                  b2e[0:TAIL].rearrange("p o d -> p (o d)"), ALU.add).then_inc(S.yb_ready, 1)
                dve.wait_ge(S.yb_ready, 2 * e + 1)
                dve.tensor_tensor(ye[n][:, 0:ST - 1, :], ye[n][:, 0:ST - 1, :],
                                  xe[n][:, 0:ST - 1, D + 1:D + 2].broadcast_to([P, ST - 1, D]), ALU.mult).then_inc(S.yw_ready, 1)
            expert(0, 0)
            expert(1, 1)
            with dve.Fori(1, NE // 2) as e:
                for n in range(2):
                    expert(2 * e + n, n)


def kernel(x, ctx_1024, fside_BxS2_0, g_xattn, g_ffn, L0_xattn_W_out, L0_xattn_b_out, L0_ffn_expert_sel, L0_ffn_keys,
           L0_ffn_values, L0_ffn_route_scale, L1_xattn_Wq, L1_xattn_Wk, L1_xattn_Wv, L1_xattn_Wo, L1_ffn_Wg, L1_ffn_W1,
           L1_ffn_b1, L1_ffn_W2, L1_ffn_b2):
    import concourse.bacc as _bacc
    from concourse.bass_utils import run_bass_kernel_spmd as _run

    x = np.asarray(x)
    NB, NQ, D = x.shape
    E, _, H = L1_ffn_W1.shape
    NE0, _, ES = L0_ffn_keys.shape
    lay = {
        "x": x.transpose(1, 0, 2),
        "ctxT": np.asarray(ctx_1024).transpose(2, 0, 1).reshape(D, -1),
        "ind": np.asarray(fside_BxS2_0).T,
        "g_xattn": np.asarray(g_xattn)[None, :],
        "g_ffn": np.asarray(g_ffn)[None, :],
        "rscale": np.asarray(L0_ffn_route_scale)[None, :],
        "woutT": np.asarray(L0_xattn_W_out).T,
        "bout": np.asarray(L0_xattn_b_out)[None, :],
        "selT": np.asarray(L0_ffn_expert_sel).T,
        "keys": np.asarray(L0_ffn_keys).transpose(1, 0, 2).reshape(D, NE0 * ES),
        "vals": np.asarray(L0_ffn_values).reshape(NE0 * ES // P, P, D).transpose(1, 0, 2),
        "wqT": np.asarray(L1_xattn_Wq).T.reshape(-1, P, D).transpose(1, 0, 2),
        "wkT": np.asarray(L1_xattn_Wk).T.reshape(-1, P, D).transpose(1, 0, 2),
        "wv": np.asarray(L1_xattn_Wv),
        "wo": np.asarray(L1_xattn_Wo).reshape(-1, P, D).transpose(1, 0, 2),
        "wgT": np.asarray(L1_ffn_Wg).T,
        "w1": np.asarray(L1_ffn_W1),
        "b1": np.asarray(L1_ffn_b1).reshape(E * H // P, P).T,
        "w2": np.asarray(L1_ffn_W2).reshape(E, H // P, P, D).transpose(0, 2, 1, 3),
        "b2": np.asarray(L1_ffn_b2),
    }
    nc = _bacc.Bacc("TRN2", target_bir_lowering=False, num_devices=1)
    arrays, t = {}, {}
    for name, a in lay.items():
        arrays[f"in_{name}"] = np.ascontiguousarray(a)
        t[name] = nc.dram_tensor(f"in_{name}", a.shape, mybir.dt.from_np(a.dtype), kind="ExternalInput").ap()
    pad = -(-int(round(2 * NB * NQ * 1.05 / E)) // P) * P
    out = nc.dram_tensor("out", (NB * NQ + pad, D), F32, kind="ExternalOutput").ap()
    gated_layers_kernel(nc, t, out)
    r = _run(nc, [arrays], core_ids=[0])
    return r.results[0]["out"][:NB * NQ].reshape(NB, NQ, D)
```

```python
from collections import namedtuple
from contextlib import ExitStack

import numpy as np

import concourse.bass as bass
from concourse import mybir

ALU = mybir.AluOpType
ACT = mybir.ActivationFunctionType
AX = mybir.AxisListType
F32 = mybir.dt.float32
F32R = mybir.dt.float32r
BF16 = mybir.dt.bfloat16
U32 = mybir.dt.uint32

P = 128
EPS = 1e-5
BIG = float(1 << 20)


def gated_layers_kernel(nc, t, out):
    NB, NQ, D = t["x"].shape[1], t["x"].shape[0], t["x"].shape[2]
    NK = t["ind"].shape[0]
    NH = t["wqT"].shape[0] * t["wqT"].shape[1] // 64
    HD = 64
    NE0 = t["selT"].shape[1]
    H0 = t["keys"].shape[1]
    ES = H0 // NE0
    TOPK0 = 4
    NE = t["wgT"].shape[1]
    HID = t["w1"].shape[2]
    MC = HID // P
    T = NB * NQ
    CAP = int(round(2 * T * 1.05 / NE))
    ST = -(-CAP // P)
    TAIL = CAP - (ST - 1) * P
    HALF = CAP // 2
    RW = D + 4
    HCUT = [0, 5, 10, 16]
    GB = 4
    GN = GB * NK
    assert NQ == D == P and NH == 16 and CAP % 2 == 0

    ctx = ExitStack()
    with ctx:
        def sb(name, shape, dt=F32):
            return ctx.enter_context(nc.sbuf_tensor(name, shape, dt))

        def sem(name):
            return ctx.enter_context(nc.semaphore(name))

        x_sb = sb("x_sb", [P, NB, D])
        res = sb("res", [P, NB, D])
        G = sb("G", [P, NB, NH * NK])
        ctxT = sb("ctxT", [P, NB * NK])
        ctx_split = sb("ctx_split", [P, 2, NB * NK], F32R)
        wv_hi = sb("wv_hi", [P, NH * HD], F32R)
        wv_lo = sb("wv_lo", [P, NH * HD], F32R)
        m_hi = sb("m_hi", [P, NH * P], F32R)
        m_lo = sb("m_lo", [P, NH * P], F32R)
        stage = sb("stage", [P, 4, NH * HD])
        woutT = sb("woutT", [P, D])
        selT = sb("selT", [P, NE0])
        keys = sb("keys", [P, H0])
        vals = sb("vals", [P, H0 // P, D])
        wo = sb("wo", [P, NH * HD // P, D])
        wgT = sb("wgT", [P, NE])
        ind = sb("ind", [NK, NB])
        b1 = sb("b1", [P, NE * MC])
        bout = sb("bout", [P, D])
        gates = sb("gates", [P, 5])
        tg = sb("tg", [P, 4])
        valg = sb("valg", [P, 1])
        ident = sb("ident", [P, P])
        ones_bf = sb("ones_bf", [P, P], BF16)
        before = sb("before", [P, P], BF16)
        mhalf = sb("mhalf", [P, 1])
        eps = sb("eps", [P, 1])
        iota16 = sb("iota16", [P, NE0])
        slot0 = sb("slot0", [P, 2, NE])
        sgn = sb("sgn", [P, 2, NE])
        token = sb("token", [P, NB])
        empty = sb("empty", [P, ST, RW])
        carry = sb("carry", [P, 2, NE])
        st = [sb(f"st{n}", [P, 6]) for n in range(4)]
        mv = [sb(f"mv{n}", [P, 2]) for n in range(4)]
        ve = [sb(f"ve{n}", [P, 1]) for n in range(4)]
        rs = [sb(f"rs{n}", [P, 1]) for n in range(4)]
        st0 = sb("st0_all", [P, NB, 6])
        mv0 = sb("mv0_all", [P, NB, 2])
        ve0 = sb("ve0_all", [P, NB])
        rs0 = sb("rs0_all", [P, NB])
        xn = [sb(f"xn{n}", [P, D]) for n in range(3)]
        xnT = [sb(f"xnT{n}", [P, NQ]) for n in range(4)]
        ctA = sb("ctA", [P, NK])
        ctD = sb("ctD", [P, 2, NK], F32R)
        indD = sb("indD", [NK, 1])
        v0 = sb("v0", [NK, D])
        nm0 = sb("nm0", [P, 1])
        p0 = sb("p0", [P, NK])
        sum0 = sb("sum0", [P, 1])
        ri0 = sb("ri0", [P, 1])
        p0T = sb("p0T", [NK, NQ])
        er = sb("er", [P, NE0])
        er1 = sb("er1", [P, NE0])
        sig = sb("sig", [P, NE0])
        top = sb("top", [P, 8])
        topi = sb("topi", [P, 8], U32)
        den = sb("den", [P, 1])
        den1 = sb("den1", [P, 1])
        rden = sb("rden", [P, 1])
        eq = sb("eq", [P, TOPK0, NE0])
        mask = sb("mask", [P, NE0])
        w0 = sb("w0", [P, NE0])
        hw = sb("hw", [P, H0])
        hwT = sb("hwT", [P, H0])
        nm1 = sb("nm1", [P, NH])
        p1 = sb("p1", [P, NH, NK])
        sum1 = sb("sum1", [P, NH])
        ri1 = sb("ri1", [P, NH])
        p1n = sb("p1n", [P, NH, NK])
        p1T = sb("p1T", [NK, NH * NQ])
        v1 = sb("v1", [NK, NH * HD])
        cT = sb("cT", [P, NH * HD // P, NQ])
        rows = sb("rows", [P, 2, RW])
        nmg = sb("nmg", [P, 1])
        eg = sb("eg", [P, NE])
        sumg = sb("sumg", [P, 1])
        rig = sb("rig", [P, 1])
        topg = sb("topg", [P, 8])
        topgi = sb("topgi", [P, 8], U32)
        oh = sb("oh", [P, 2, NE], BF16)
        pos = sb("pos", [P, 2, NE])
        slot = sb("slot", [P, 2, NE])
        over = sb("over", [P, 2, NE])
        sidx = sb("sidx", [P, 2], U32)

        g_flat = G[:, :, :].rearrange("p b n -> p (b n)")
        cut = [0]

        def over_g(n):
            a = cut[0]
            cut[0] += n
            assert cut[0] <= NB * NH * NK
            return g_flat[:, a:a + n]

        xe = [over_g(ST * RW).rearrange("p (s c) -> p s c", c=RW) for _ in range(2)]
        xeT = [over_g(CAP) for _ in range(2)]
        hT = [over_g(MC * CAP).rearrange("p (m s) -> p m s", s=CAP) for _ in range(2)]
        ye = [over_g(ST * D).rearrange("p (s d) -> p s d", d=D) for _ in range(2)]
        b2 = over_g(NE * D).rearrange("p (e d) -> p e d", d=D)
        tok_u = [sb(f"tok_u{n}", [P, ST], U32) for n in range(2)]
        b1e = [sb(f"b1e{n}", [P, MC]) for n in range(2)]
        w1_sb = [stage[:, n, 0:HID] for n in range(2)]
        w2_sb = [stage[:, n, HID:2 * HID].rearrange("p (m d) -> p m d", d=D) for n in range(2)]

        banks = [ctx.enter_context(nc.psum_tensor(f"bank{n}", [P, 512], F32)) for n in range(8)]
        B0, B1, B2, B3, B4, B5, B6, B7 = banks

        slots_dram = nc.dram_tensor("slots", [NE * CAP, RW], F32, kind="Internal").ap()

        names = """ld_m ld_x ld_w ld_b2 consts tanh_ready xb_ready m_mm m_hi_ready m_lo_ready
        ctx_split wv_hi_ready wv_split g_mm g_act g_dve scaled
        st0 st1 st2 st3 mv0 mv1 mv2 mv3 ve0 ve1 ve2 ve3 rs0 rs1 rs2 rs3 xn0 xn1 xn2 xn3
        xn0_t xn1_t xn2_t xn3_t xnT0 xnT1 xnT2 xnT3
        ctA_ready s0_mm nm0_ready p0_ready v0_mm v0_ready ri0_ready p0_t p0T_ready o0_mm x1_ready
        r0_mm er_ready er1_ready sig_ready top_ready topi_ready eq_ready mask_ready den_ready
        den1_ready rden_ready w0_ready h0_mm hw_ready hw_t hwT_ready y0_mm x2_ready
        s1_mm nm1_ready p1_exp ri1_ready p1n_ready
        ctD_ready v1_mm v1_ready p1_t p1T_act p1T_dve pv_mm cT_act cT_dve o1_mm x3_ready
        rg_mm nmg_ready eg_ready rig_ready topg_ready topgi_ready oh_ready cw_ready tok_ready
        pos_mm pos_ready carry_ready slot_a slot_b slot_c slot_d slot_e slot_f sidx_ready
        sc0_done sc1_done out_rows init_rows out_pad
        w_load0 w_load1 xe_load0 xe_load1 xeT_mm xeT_act xeT_dve h_mm h_ready y_mm yb_ready yw_ready tok_conv add_done indD_ready b1_ready yw_tail_ready
        """.split()
        S = namedtuple("Semaphores", names)(*[sem(n) for n in names])

        block = ctx.enter_context(nc.Block())

        LAG = 5
        Batches = namedtuple("Batches", "i l n0 n1 n2 n3 n4")

        def at(eng, s, n):
            if not isinstance(n, int) or n > 0:
                eng.wait_ge(s, n)

        def own_wait(eng):
            eng.wait_ge(S.consts, 1)

        def pipeline(eng, step):
            def batches(i):
                if not isinstance(i, int):
                    return Batches(i, *[i - k for k in range(LAG + 1)])
                return Batches(i, *[i - k if 0 <= i - k < NB else None for k in range(LAG + 1)])

            for i in range(LAG + 1):
                step(batches(i))
            with eng.Fori(LAG + 2, NB + 1) as i:
                step(batches(i - 1))
            for i in range(NB, NB + LAG):
                step(batches(i))

        def bank_read(pe, n, *readings):
            for s, per, nth, place, ago in readings:
                b = n.i - 1 - place - ago
                if not isinstance(b, int) or 0 <= b < NB:
                    pe.wait_ge(s, per * b + nth)
                    return

        def cols(n, w):
            return bass.ds(n * w, w) if not isinstance(n, int) else slice(n * w, n * w + w)

        def one(n):
            return bass.ds(n, 1) if not isinstance(n, int) else slice(n, n + 1)

        def row_of(tensor, n):
            return tensor[:, one(n), :].rearrange("p o d -> p (o d)")

        @block.sync
        def _(sp):
            sp.dma_start(stage[:, 0, :], t["wqT"].rearrange("p m d -> p (m d)")).then_inc(S.ld_m, 16)
            sp.dma_start(stage[:, 1, :], t["wkT"].rearrange("p m d -> p (m d)")).then_inc(S.ld_m, 16)
            sp.dma_start(ctxT[:, :], t["ctxT"]).then_inc(S.ld_m, 16)
            sp.dma_start(stage[:, 2, :], t["wv"]).then_inc(S.ld_m, 16)
            for g, at_g in ((t["g_xattn"], 0), (t["g_ffn"], 2), (t["rscale"], 4)):
                n = g.shape[1]
                sp.dma_start(gates[:, at_g:at_g + n], g.broadcast_to([P, n])).then_inc(S.ld_x, 16)
            sp.dma_start(bout[:, :], t["bout"].broadcast_to([P, D])).then_inc(S.ld_x, 16)
            sp.dma_start(x_sb[:, :, :], t["x"]).then_inc(S.ld_x, 16)
            for dst, name in ((woutT, "woutT"), (selT, "selT"), (keys, "keys"), (wgT, "wgT"), (ind, "ind"),
                              (b1, "b1")):
                sp.dma_start(dst[:, :], t[name]).then_inc(S.ld_w, 16)
            sp.dma_start(vals[:, :, :], t["vals"]).then_inc(S.ld_w, 16)
            sp.dma_start(wo[:, :, :], t["wo"]).then_inc(S.ld_w, 16)
            sp.wait_ge(S.consts, 1)
            for e in range(NE):
                dst = slots_dram[e * CAP:e * CAP + (ST - 1) * P, :].rearrange("(s p) c -> p s c", p=P)
                sp.dma_start(dst, empty[:, 0:ST - 1, :]).then_inc(S.init_rows, 16)
                sp.dma_start(slots_dram[e * CAP + (ST - 1) * P:(e + 1) * CAP, :],
                             empty[0:TAIL, ST - 1, :]).then_inc(S.init_rows, 16)
            sp.dma_start(out[T:T + ST * P, :].rearrange("(s p) d -> p s d", p=P), empty[:, :, 0:D]).then_inc(S.out_pad, 16)

            def step(n):
                if n.n0 is not None:
                    at(sp, S.s0_mm, n.n0)
                    at(sp, S.v0_mm, n.n0)
                    sp.dma_start(ctA[:, :], t["ctxT"][:, cols(n.n0, NK)]).then_inc(S.ctA_ready, 16)
                if n.n2 is not None:
                    at(sp, S.v1_mm, 2 * n.n2)
                    sp.dma_start(ctD[:, :, :].bitcast(F32), ctx_split[:, :, cols(n.n2, NK)].bitcast(F32)).then_inc(S.ctD_ready, 16)
                if n.n4 is not None:
                    sp.wait_ge(S.x3_ready, n.n4 + 1)
                    sp.dma_start(out[cols(n.n4, P), :], row_of(res, n.n4)).then_inc(S.out_rows, 16)
            sp.wait_ge(S.ctx_split, 2)
            pipeline(sp, step)

            def load(e, n):
                at(sp, S.yw_ready, e - 1)
                at(sp, S.yw_tail_ready, e - 1)
                if isinstance(e, int):
                    lo = slice(e * CAP, e * CAP + (ST - 1) * P)
                    hi = slice(e * CAP + (ST - 1) * P, (e + 1) * CAP)
                else:
                    lo = bass.ds(e * CAP, (ST - 1) * P)
                    hi = bass.ds(e * CAP + (ST - 1) * P, TAIL)
                sp.dma_start(xe[n][:, 0:ST - 1, :],
                             slots_dram[lo, :].rearrange("(s p) c -> p s c", p=P)).then_inc((S.xe_load0, S.xe_load1)[n], 16)
                sp.dma_start(xe[n][0:TAIL, ST - 1, :], slots_dram[hi, :]).then_inc((S.xe_load0, S.xe_load1)[n], 16)

            def weights(e, n):
                at(sp, S.y_mm, 2 * (e - 1))
                sp.dma_start(w1_sb[n], t["w1"][one(e), :, :].rearrange("o p h -> p (o h)")).then_inc((S.w_load0, S.w_load1)[n], 16)
                sp.dma_start(w2_sb[n], t["w2"][one(e), :, :, :].rearrange("o p m d -> p (o m) d")).then_inc((S.w_load0, S.w_load1)[n], 16)

            sp.wait_ge(S.m_mm, 4)
            weights(0, 0)
            weights(1, 1)
            sp.wait_ge(S.s1_mm, 3 * NB)
            sp.dma_start(b2, t["b2"][None, :, :].broadcast_to([P, NE, D])).then_inc(S.ld_b2, 16)
            sp.wait_ge(S.sc0_done, 16 * NB)
            sp.wait_ge(S.sc1_done, 16 * NB)
            load(0, 0)
            load(1, 1)
            with sp.Fori(1, NE // 2) as e:
                for n in range(2):
                    load(2 * e + n, n)
                    weights(2 * e + n, n)
            sp.wait_ge(S.add_done, 16 * ST * NE)
            sp.wait_ge(S.out_pad, 16)
            sp.wait_ge(S.out_rows, 16 * NB)

        @block.gpsimd
        def _(pool):
            pool.memset(empty[:, :, :], 0.0)
            pool.memset(mhalf[:, :], -0.5)
            pool.memset(eps[:, :], EPS)
            pool.memset(ones_bf[:, :], 1.0)
            pool.memset(carry[:, :, :], 0.0)
            pool.memset(sgn[:, 0, :], 1.0)
            pool.memset(sgn[:, 1, :], -1.0)
            pool.memset(rows[:, :, :], 0.0)
            pool.iota(iota16[:, :], [[1, NE0]], base=0, channel_multiplier=0, allow_small_or_imprecise_dtypes=True)
            pool.iota(slot0[:, :, :], [[CAP - 1, 2], [CAP, NE]], base=0, channel_multiplier=0,
                      allow_small_or_imprecise_dtypes=True)
            pool.iota(token[:, :], [[NQ, NB]], base=0, channel_multiplier=1, allow_small_or_imprecise_dtypes=True)
            pool.memset(ident[:, :], 0.0).then_inc(S.slot_a, 1)
            pool.wait_ge(S.slot_a, 1)
            pool.iota(empty[:, :, D:D + 1], [[P, ST], [0, 1]], base=T, channel_multiplier=1, allow_small_or_imprecise_dtypes=True)
            pool.affine_select(out=ident[:, :], in_=ident[:, :], compare_op=ALU.not_equal, fill=1.0, base=0,
                               pattern=[[-1, P]], channel_multiplier=1)
            pool.affine_select(out=before[:, :], in_=ones_bf[:, :], compare_op=ALU.is_gt, fill=0.0, base=0,
                               pattern=[[1, P]], channel_multiplier=-1).then_inc(S.consts, 1)
            pool.wait_ge(S.ld_m, 64)
            pool.tensor_copy(wv_hi[:, :], stage[:, 2, :]).then_inc(S.wv_hi_ready, 1)
            pool.wait_ge(S.wv_hi_ready, 1)
            pool.tensor_tensor(wv_lo[:, :], stage[:, 2, :], wv_hi[:, :].bitcast(F32), ALU.subtract).then_inc(S.wv_split, 1)

            def rstd(k, n):
                at(pool, [S.xn0, S.xn1, S.xn2, S.xn3][k], n)
                pool.wait_ge([S.ve0, S.ve1, S.ve2, S.ve3][k], n + 1)
                pool.tensor_tensor(rs[k][:, :], ve[k][:, :], mhalf[:, :], ALU.pow).then_inc([S.rs0, S.rs1, S.rs2, S.rs3][k], 1)

            def var_eps(k, n):
                pool.wait_ge([S.mv0, S.mv1, S.mv2, S.mv3][k], n + 1)
                pool.tensor_tensor(ve[k][:, :], mv[k][:, 1:2], eps[:, :], ALU.add).then_inc([S.ve0, S.ve1, S.ve2, S.ve3][k], 1)

            pool.wait_ge(S.mv0, 1)
            pool.tensor_tensor(ve0[:, :], mv0[:, :, 1], eps[:, :].broadcast_to([P, NB]), ALU.add).then_inc(S.ve0, 1)
            pool.wait_ge(S.ve0, 1)
            pool.tensor_tensor(rs0[:, :], ve0[:, :], mhalf[:, :].broadcast_to([P, NB]), ALU.pow).then_inc(S.rs0, 1)

            def step(n):
                if n.n2 is not None:
                    at(pool, S.v1_ready, 2 * n.n2)
                    pool.tensor_copy(indD[:, :], ind[:, one(n.n2)]).then_inc(S.indD_ready, 1)
                if n.n1 is not None:
                    var_eps(2, n.n1)
                if n.n4 is not None:
                    at(pool, S.sc0_done, 16 * n.n4)
                    at(pool, S.sc1_done, 16 * n.n4)
                    pool.tensor_copy(rows[:, :, D:D + 1], token[:, one(n.n4)][:, None, :].broadcast_to([P, 2, 1])).then_inc(S.tok_ready, 1)
                if n.n1 is not None:
                    rstd(2, n.n1)
                if n.n2 is not None:
                    pool.wait_ge(S.ri1_ready, n.n2 + 1)
                    at(pool, S.p1_t, 4 * n.n2)
                    pool.tensor_tensor(p1n[:, :, :], p1[:, :, :], ri1[:, :, None].broadcast_to([P, NH, NK]),
                                       ALU.mult).then_inc(S.p1n_ready, 1)
                if n.n0 is not None:
                    var_eps(1, n.n0)
                    rstd(1, n.n0)
                if n.n4 is not None:
                    k = 1 + n.n4
                    pool.wait_ge(S.pos_ready, k)
                    pool.wait_ge(S.carry_ready, k)
                    at(pool, S.sidx_ready, n.n4)
                    pool.tensor_tensor(slot[:, :, :], pos[:, :, :], sgn[:, :, :], ALU.mult).then_inc(S.slot_a, 1)
                    pool.wait_ge(S.slot_a, k + 1)
                    pool.tensor_tensor(pos[:, 1, :], pos[:, 1, :], carry[:, 0, :], ALU.add).then_inc(S.slot_c, 1)
                    pool.tensor_tensor(slot[:, :, :], slot[:, :, :], slot0[:, :, :], ALU.add).then_inc(S.slot_b, 1)
                    own_wait(pool)
                    pool.wait_ge(S.slot_c, k)
                    pool.tensor_scalar(over[:, :, :], pos[:, :, :], float(CAP), BIG, ALU.is_ge, ALU.mult).then_inc(S.slot_d, 1)
                    pool.wait_ge(S.slot_b, k)
                    pool.wait_ge(S.slot_d, k)
                    pool.tensor_tensor(slot[:, :, :], slot[:, :, :], over[:, :, :], ALU.add).then_inc(S.slot_e, 1)
                    pool.wait_ge(S.slot_e, k)
                    pool.tensor_tensor(slot[:, :, :], slot[:, :, :], oh[:, :, :], ALU.mult).then_inc(S.slot_f, 1)
                    own_wait(pool)
                    pool.wait_ge(S.sidx_ready, k)
                    pool.wait_ge(S.cw_ready, k)
                    pool.wait_ge(S.tok_ready, k)
                    if isinstance(n.n4, int) and n.n4 == 0:
                        pool.wait_ge(S.init_rows, 32 * NE)
                    for c, done in ((0, S.sc0_done), (1, S.sc1_done)):
                        pool.indirect_dma_start(slots_dram, bass.IndirectOffsetOnAxis(ap=sidx[:, c:c + 1], axis=0),
                                                rows[:, c, :], None, bounds_check=NE * CAP - 1,
                                                oob_is_err=False).then_inc(done, 16)
                if n.n3 is not None:
                    var_eps(3, n.n3)
                    rstd(3, n.n3)
            pipeline(pool, step)

            pool.wait_ge(S.out_rows, 16 * NB)
            pool.wait_ge(S.out_pad, 16)

            def bias(e, n):
                at(pool, S.h_ready, 2 * MC * (e - 1))
                pool.tensor_copy(b1e[n][:, :], b1[:, cols(e, MC)]).then_inc(S.b1_ready, 1)

            def add(e, n):
                pool.wait_ge(S.tok_conv, e + 1)
                pool.wait_ge(S.yb_ready, 2 * e + 2)
                at(pool, S.add_done, 16 * ST * e)
                pool.tensor_tensor(ye[n][0:TAIL, ST - 1, :], ye[n][0:TAIL, ST - 1, :],
                                   xe[n][0:TAIL, ST - 1, D + 1:D + 2].broadcast_to([TAIL, D]), ALU.mult).then_inc(S.yw_tail_ready, 1)
                own_wait(pool)
                pool.wait_ge(S.tok_conv, e + 1)
                pool.wait_ge(S.yw_ready, e + 1)
                for s in range(ST):
                    k = P if s < ST - 1 else TAIL
                    if s == ST - 1:
                        own_wait(pool)
                        pool.wait_ge(S.yw_tail_ready, e + 1)
                    pool.indirect_dma_start(out, bass.IndirectOffsetOnAxis(ap=tok_u[n][0:k, s:s + 1], axis=0),
                                            ye[n][0:k, s, :], None, bounds_check=T + ST * P - 1, oob_is_err=True,
                                            compute_op=ALU.add).then_inc(S.add_done, 16)
            bias(0, 0)
            bias(1, 1)
            add(0, 0)
            with pool.Fori(1, NE // 2) as e:
                bias(2 * e, 0)
                add(2 * e - 1, 1)
                bias(2 * e + 1, 1)
                add(2 * e, 0)
            add(NE - 1, 1)

        @block.tensor
        def _(pe):
            pe.wait_ge(S.ld_m, 64)
            for q in range(4):
                for j in range(4):
                    h = 4 * q + j
                    r = slice(HD * (h % 2), HD * (h % 2) + HD)
                    c = slice(P * (h // 2), P * (h // 2) + P)
                    mm = pe.matmul(banks[q + 4 * (h % 2)][:, P * (j // 2):P * (j // 2) + P], stage[r, 1, c], stage[r, 0, c], start=True, stop=True)
                mm.then_inc(S.m_mm, 1)
            pe.wait_ge(S.m_lo_ready, 8)
            pe.wait_ge(S.ctx_split, 2)

            def g_group(g):
                for h in range(NH):
                    k = NH // 2 * g + h // 2
                    at(pe, S.g_act if h % 2 == 0 else S.g_dve, k - 3)
                    c = cols(g, GN)
                    w = slice(P * h, P * h + P)
                    dst = banks[h % 8][:, 0:GN]
                    pe.matmul(dst, m_hi[:, w], ctx_split[:, 0, c], start=True, stop=False)
                    pe.matmul(dst, m_hi[:, w], ctx_split[:, 1, c], start=False, stop=False)
                    pe.matmul(dst, m_lo[:, w], ctx_split[:, 0, c], start=False, stop=True).then_inc(S.g_mm, 1)
            g_group(0)
            with pe.Fori(1, NB // GB) as g:
                g_group(g)
            pe.wait_ge(S.g_act, NB // GB * NH // 2)
            pe.wait_ge(S.g_dve, NB // GB * NH // 2)
            pe.wait_ge(S.scaled, 3)
            pe.wait_ge(S.wv_split, 1)
            pe.wait_ge(S.consts, 1)
            pe.wait_ge(S.ld_w, 16 * 8)

            def context(bank, heads):
                for h in heads:
                    mm = pe.matmul(bank[HD * (h % 2):HD * (h % 2) + HD, P * (h // 2 % 4):P * (h // 2 % 4) + P],
                                   v1[:, HD * h:HD * h + HD], p1T[:, P * h:P * h + P], start=True, stop=True)
                return mm

            def values(j, bank):
                c = slice(512 * j, 512 * j + 512)
                pe.matmul(bank[0:NK, :], ctD[:, 0, :], wv_hi[:, c], start=True, stop=False)
                pe.matmul(bank[0:NK, :], ctD[:, 0, :], wv_lo[:, c], start=False, stop=False)
                pe.matmul(bank[0:NK, :], ctD[:, 1, :], wv_hi[:, c], start=False, stop=True).then_inc(S.v1_mm, 1)

            def scores(j, n, bank):
                a, b = HCUT[j] * NK, HCUT[j + 1] * NK
                pe.matmul(bank[:, 0:b - a], xnT[2][:, :], row_of(G, n)[:, a:b], start=True, stop=True).then_inc(S.s1_mm, 1)

            def probs_t(j, bank):
                for h in range(4 * j, 4 * j + 4):
                    mm = pe.transpose(bank[0:NK, P * (h % 4):P * (h % 4) + P], p1n[:, h, :], ident[:, :])
                mm.then_inc(S.p1_t, 1)

            def step(n):
                if n.n0 is not None:
                    pe.wait_ge(S.xn0, n.n0 + 1)
                    at(pe, S.hw_ready, n.n0)
                    pe.transpose(B1[:, 0:P], xn[0][:, :], ident[:, :]).then_inc(S.xn0_t, 1)
                if n.n3 is not None:
                    pe.wait_ge(S.v1_ready, 2 * n.n3 + 2)
                    pe.wait_ge(S.p1T_act, 2 * n.n3 + 2)
                    context(B5, range(8, 12))
                if n.n0 is not None:
                    pe.wait_ge(S.ctA_ready, 16 * n.n0 + 16)
                    at(pe, S.x2_ready, n.n0)
                    pe.matmul(B0[0:NK, 0:D], ctA[:, :], woutT[:, :], start=True, stop=True).then_inc(S.v0_mm, 1)
                    pe.wait_ge(S.xnT0, n.n0 + 1)
                    pe.matmul(B1[:, 0:NK], xnT[0][:, :], ctA[:, :], start=True, stop=True).then_inc(S.s0_mm, 1)
                if n.n2 is not None:
                    pe.wait_ge(S.ctD_ready, 16 * n.n2 + 16)
                    bank_read(pe, n, (S.x3_ready, 1, 1, 3, 1), (S.p1_exp, 3, 1, 1, 1), (S.v1_ready, 2, 1, 2, 1))
                    values(0, B2)
                if n.n4 is not None:
                    pe.wait_ge(S.xn3, n.n4 + 1)
                    bank_read(pe, n, (S.cT_act, 1, 1, 2, 1), (S.p1_exp, 3, 2, 1, 1), (S.eg_ready, 1, 1, 4, 1))
                    pe.transpose(B3[:, 0:P], rows[:, 0, 0:D], ident[:, :]).then_inc(S.xn3_t, 1)
                if n.n0 is not None:
                    pe.wait_ge(S.v0_ready, n.n0 + 1)
                    pe.wait_ge(S.p0_ready, n.n0 + 1)
                    pe.transpose(B0[0:NK, 0:P], p0[:, :], ident[:, :]).then_inc(S.p0_t, 1)
                if n.n3 is not None:
                    pe.wait_ge(S.p1T_dve, 2 * n.n3 + 2)
                    context(B5, range(12, 16)).then_inc(S.pv_mm, 1)
                if n.n4 is not None:
                    pe.wait_ge(S.xnT3, n.n4 + 1)
                    pe.matmul(B3[:, 0:NE], xnT[3][:, :], wgT[:, :], start=True, stop=True).then_inc(S.rg_mm, 1)
                if n.n0 is not None:
                    pe.wait_ge(S.p0T_ready, n.n0 + 1)
                    pe.matmul(B0[:, 0:D], p0T[:, :], v0[:, :], start=True, stop=True).then_inc(S.o0_mm, 1)
                if n.n1 is not None:
                    pe.wait_ge(S.xn2, n.n1 + 1)
                    bank_read(pe, n, (S.p0_ready, 1, 1, 0, 0), (S.hw_ready, 1, 1, 0, 1), (S.carry_ready, 1, 1, 4, 1),
                              (S.xnT2, 1, 1, 1, 1))
                    pe.transpose(B1[:, 0:P], xn[2][:, :], ident[:, :]).then_inc(S.xn2_t, 1)
                if n.n2 is not None:
                    bank_read(pe, n, (S.p1_exp, 3, 3, 1, 1), (S.v1_ready, 2, 2, 2, 1))
                    values(1, B4)
                if n.n1 is not None:
                    pe.wait_ge(S.xnT2, n.n1 + 1)
                    bank_read(pe, n, (S.v1_ready, 2, 1, 2, 0), (S.x3_ready, 1, 1, 3, 1), (S.p1_exp, 3, 1, 1, 1))
                    scores(0, n.n1, B2)
                    bank_read(pe, n, (S.eg_ready, 1, 1, 4, 0), (S.cT_act, 1, 1, 2, 1), (S.p1_exp, 3, 2, 1, 1))
                    scores(1, n.n1, B3)
                if n.n2 is not None:
                    pe.wait_ge(S.p1n_ready, n.n2 + 1)
                    bank_read(pe, n, (S.cT_dve, 1, 1, 3, 0), (S.p1T_act, 2, 1, 2, 1))
                    probs_t(0, B5)
                if n.n4 is not None:
                    pe.wait_ge(S.oh_ready, n.n4 + 1)
                    bank_read(pe, n, (S.xnT2, 1, 1, 1, 0), (S.p0_ready, 1, 1, 0, 0), (S.hw_ready, 1, 1, 0, 1),
                              (S.carry_ready, 1, 1, 4, 1))
                    ohf = oh[:, :, :].rearrange("p k e -> p (k e)")
                    pe.matmul(B1[:, 0:2 * NE], before[:, :], ohf, start=True, stop=True)
                    pe.matmul(B1[:, 2 * NE:4 * NE], ones_bf[:, :], ohf, start=True, stop=True).then_inc(S.pos_mm, 1)
                if n.n0 is not None:
                    pe.wait_ge(S.xn1, n.n0 + 1)
                    pe.transpose(B0[:, 0:P], xn[1][:, :], ident[:, :]).then_inc(S.xn1_t, 1)
                if n.n2 is not None:
                    bank_read(pe, n, (S.p1T_dve, 2, 2, 2, 1))
                    probs_t(1, B6)
                if n.n0 is not None:
                    pe.wait_ge(S.xnT1, n.n0 + 1)
                    pe.matmul(B0[:, 0:NE0], xnT[1][:, :], selT[:, :], start=True, stop=True).then_inc(S.r0_mm, 1)
                    bank_read(pe, n, (S.carry_ready, 1, 1, 4, 0), (S.xnT2, 1, 1, 1, 0), (S.p0_ready, 1, 1, 0, 0))
                    pe.matmul(B1[:, :], xnT[1][:, :], keys[:, :], start=True, stop=True).then_inc(S.h0_mm, 1)
                if n.n1 is not None:
                    bank_read(pe, n, (S.v1_ready, 2, 2, 2, 0), (S.p1_exp, 3, 3, 1, 1))
                    scores(2, n.n1, B4)
                if n.n2 is not None:
                    bank_read(pe, n, (S.p1T_act, 2, 2, 2, 1))
                    probs_t(2, B7)
                    pe.wait_ge(S.p1T_dve, 2 * n.n2 + 1)
                    probs_t(3, B6)
                    pe.wait_ge(S.v1_ready, 2 * n.n2 + 1)
                    bank_read(pe, n, (S.p1_exp, 3, 2, 1, 0), (S.eg_ready, 1, 1, 4, 0), (S.cT_act, 1, 1, 2, 1))
                    context(B3, range(4, 8))
                if n.n3 is not None:
                    pe.wait_ge(S.cT_act, n.n3 + 1)
                    bank_read(pe, n, (S.p1_exp, 3, 1, 1, 0), (S.v1_ready, 2, 1, 2, 0), (S.x3_ready, 1, 1, 3, 1))
                    for m in range(4):
                        pe.matmul(B2[:, 0:D], cT[:, m, :], wo[:, m, :], start=m == 0, stop=False)
                if n.n0 is not None:
                    pe.wait_ge(S.hw_ready, n.n0 + 1)
                    for m in range(H0 // P):
                        mm = pe.transpose(B0[:, P * m:P * m + P], hw[:, P * m:P * m + P], ident[:, :])
                    mm.then_inc(S.hw_t, 1)
                if n.n3 is not None:
                    pe.wait_ge(S.cT_dve, n.n3 + 1)
                    for m in range(4, 8):
                        mm = pe.matmul(B2[:, 0:D], cT[:, m, :], wo[:, m, :], start=False, stop=m == 7)
                    mm.then_inc(S.o1_mm, 1)
                if n.n0 is not None:
                    pe.wait_ge(S.hwT_ready, n.n0 + 1)
                    for m in range(H0 // P):
                        mm = pe.matmul(B0[:, 0:D], hwT[:, P * m:P * m + P], vals[:, m, :], start=m == 0, stop=m == H0 // P - 1)
                    mm.then_inc(S.y0_mm, 1)
                if n.n2 is not None:
                    pe.wait_ge(S.p1T_act, 2 * n.n2 + 1)
                    context(B3, range(0, 4)).then_inc(S.pv_mm, 1)
            pipeline(pe, step)

            def expert(e, n):
                pe.wait_ge((S.xe_load0, S.xe_load1)[n], 16 * (e - n) + 32)
                at(pe, S.xeT_act, e)
                at(pe, S.xeT_dve, e)
                for s in range(ST):
                    k = P if s < ST - 1 else TAIL
                    mm = pe.transpose(banks[s // 4][:, P * (s % 4):P * (s % 4) + k], xe[n][0:k, s, 0:D], ident[0:k, 0:k])
                mm.then_inc(S.xeT_mm, 1)
                pe.wait_ge((S.w_load0, S.w_load1)[n], 16 * (e - n) + 32)
                pe.wait_ge(S.xeT_act, e + 1)
                pe.wait_ge(S.xeT_dve, e + 1)
                for m in range(MC):
                    for j in range(2):
                        k = 2 * m + j
                        at(pe, S.h_ready, 2 * MC * e + k - 3)
                        pe.matmul(banks[2 + k % 4][:, 0:HALF], w1_sb[n][:, P * m:P * m + P],
                                  xeT[n][:, HALF * j:HALF * j + HALF], start=True, stop=True).then_inc(S.h_mm, 1)
                pe.wait_ge(S.h_ready, 2 * MC * (e + 1))
                at(pe, S.yb_ready, 2 * e)
                for s in range(ST):
                    k = P if s < ST - 1 else TAIL
                    for m in range(MC):
                        mm = pe.matmul(banks[6 + s // 4][0:k, P * (s % 4):P * (s % 4) + D], hT[n][:, m, P * s:P * s + k],
                                       w2_sb[n][:, m, :], start=m == 0, stop=m == MC - 1)
                    if s >= ST - 2:
                        mm.then_inc(S.y_mm, 1)
            expert(0, 0)
            expert(1, 1)
            with pe.Fori(1, NE // 2) as e:
                for n in range(2):
                    expert(2 * e + n, n)

        @block.scalar
        def _(act):
            act.wait_ge(S.ld_x, 16 * 5)
            act.activation(tg[:, :], gates[:, 0:4], ACT.Tanh, bias=0.0).then_inc(S.tanh_ready, 1)
            for q in range(4):
                act.wait_ge(S.m_mm, q + 1)
                for o in range(2):
                    dst = m_hi[:, :].rearrange("p (h d) -> p h d", d=P)[:, 4 * q + o:4 * q + o + 3:2, :]
                    act.copy(dst, banks[q + 4 * o][:, 0:2 * P].rearrange("p (h d) -> p h d", d=P)).then_inc(S.m_hi_ready, 1)

            def g_group(g):
                for h in range(0, NH, 2):
                    act.wait_ge(S.g_mm, NH * g + h + 1)
                    dst = G[:, cols(g, GB), NK * h:NK * h + NK]
                    act.copy(dst, banks[h % 8][:, 0:GN].rearrange("p (b k) -> p b k", k=NK)).then_inc(S.g_act, 1)
            g_group(0)
            with act.Fori(1, NB // GB) as g:
                g_group(g)

            def step(n):
                if n.n0 is not None:
                    act.wait_ge(S.xn0_t, n.n0 + 1)
                    at(act, S.s0_mm, n.n0)
                    act.mul(xnT[0][:, :], B1[:, 0:P], float(D) ** -0.5).then_inc(S.xnT0, 1)
                if n.n3 is not None:
                    act.wait_ge(S.pv_mm, 2 * n.n3 + 1)
                    at(act, S.o1_mm, n.n3)
                    act.copy(cT[:, 0:4, :], B3[:, :].rearrange("p (m q) -> p m q", q=NQ)).then_inc(S.cT_act, 1)
                if n.n0 is not None:
                    act.wait_ge(S.v0_mm, n.n0 + 1)
                    at(act, S.o0_mm, n.n0)
                    act.activation(v0[:, :], B0[0:NK, 0:D], ACT.Copy, scale=tg[0:NK, 0:1]).then_inc(S.v0_ready, 1)
                    act.wait_ge(S.nm0_ready, n.n0 + 1)
                    at(act, S.p0_t, n.n0)
                    at(act, S.ri0_ready, n.n0)
                    act.activation(p0[:, :], B1[:, 0:NK], ACT.Exp, bias=nm0[:, :], accum_out=sum0[:, :]).then_inc(S.p0_ready, 1)
                if n.n4 is not None:
                    act.wait_ge(S.xn3_t, n.n4 + 1)
                    act.copy(xnT[3][:, :], B3[:, 0:P]).then_inc(S.xnT3, 1)
                if n.n0 is not None:
                    act.wait_ge(S.p0_t, n.n0 + 1)
                    act.copy(p0T[:, :], B0[0:NK, 0:P]).then_inc(S.p0T_ready, 1)
                if n.n2 is not None:
                    act.wait_ge(S.v1_mm, 2 * n.n2 + 1)
                    act.wait_ge(S.indD_ready, n.n2 + 1)
                    at(act, S.pv_mm, 2 * n.n2 - 1 if not isinstance(n.n2, int) or n.n2 > 0 else 0)
                    act.activation(v1[:, 0:512], B2[0:NK, :], ACT.Copy, scale=indD[:, :]).then_inc(S.v1_ready, 1)
                if n.n1 is not None:
                    act.wait_ge(S.xn2_t, n.n1 + 1)
                    at(act, S.s1_mm, 3 * n.n1)
                    act.mul(xnT[2][:, :], B1[:, 0:P], float(HD) ** -0.5).then_inc(S.xnT2, 1)
                if n.n4 is not None:
                    act.wait_ge(S.nmg_ready, n.n4 + 1)
                    at(act, S.topgi_ready, n.n4)
                    at(act, S.rig_ready, n.n4)
                    act.activation(eg[:, :], B3[:, 0:NE], ACT.Exp, bias=nmg[:, :], accum_out=sumg[:, :]).then_inc(S.eg_ready, 1)
                if n.n2 is not None:
                    act.wait_ge(S.v1_mm, 2 * n.n2 + 2)
                    at(act, S.pv_mm, 2 * n.n2)
                    act.activation(v1[:, 512:1024], B4[0:NK, :], ACT.Copy, scale=indD[:, :]).then_inc(S.v1_ready, 1)
                if n.n0 is not None:
                    act.wait_ge(S.xn1_t, n.n0 + 1)
                    at(act, S.h0_mm, n.n0)
                    act.copy(xnT[1][:, :], B0[:, 0:P]).then_inc(S.xnT1, 1)
                    act.wait_ge(S.r0_mm, n.n0 + 1)
                    at(act, S.er1_ready, n.n0)
                    act.activation(er[:, :], B0[:, 0:NE0], ACT.Exp, bias=0.0, scale=-1.0).then_inc(S.er_ready, 1)

                def softmax_exp(j, bank):
                    act.wait_ge(S.nm1_ready, 3 * n.n1 + 1 + j)
                    if j == 0:
                        at(act, S.p1n_ready, n.n1)
                    for h in range(HCUT[j], HCUT[j + 1]):
                        c = NK * (h - HCUT[j])
                        last = act.activation(p1[:, h, :], bank[:, c:c + NK], ACT.Exp, bias=nm1[:, h:h + 1],
                                              accum_out=sum1[:, h:h + 1])
                    last.then_inc(S.p1_exp, 1)
                if n.n1 is not None:
                    softmax_exp(0, B2)
                    softmax_exp(1, B3)
                if n.n2 is not None:
                    act.wait_ge(S.p1_t, 4 * n.n2 + 1)
                    at(act, S.pv_mm, 2 * n.n2 - 1 if not isinstance(n.n2, int) or n.n2 > 0 else 0)
                    act.copy(p1T[:, 0:512], B5[0:NK, :]).then_inc(S.p1T_act, 1)
                    act.wait_ge(S.p1_t, 4 * n.n2 + 3)
                    at(act, S.pv_mm, 2 * n.n2)
                    act.copy(p1T[:, 1024:1536], B7[0:NK, :]).then_inc(S.p1T_act, 1)
                if n.n0 is not None:
                    act.wait_ge(S.hw_t, n.n0 + 1)
                    at(act, S.y0_mm, n.n0)
                    act.copy(hwT[:, :], B0[:, :]).then_inc(S.hwT_ready, 1)
                if n.n1 is not None:
                    softmax_exp(2, B4)
            pipeline(act, step)

            def expert(e, n):
                act.wait_ge(S.xeT_mm, e + 1)
                act.copy(xeT[n][:, 0:512], banks[0][:, :]).then_inc(S.xeT_act, 1)
                for m in range(MC):
                    for j in range(2):
                        k = 2 * m + j
                        act.wait_ge(S.h_mm, 2 * MC * e + k + 1)
                        at(act, S.y_mm, 2 * (e - 1))
                        act.wait_ge(S.b1_ready, e + 1)
                        act.activation(hT[n][:, m, HALF * j:HALF * j + HALF], banks[2 + k % 4][:, 0:HALF], ACT.Gelu,
                                       bias=b1e[n][:, m:m + 1]).then_inc(S.h_ready, 1)
            expert(0, 0)
            expert(1, 1)
            with act.Fori(1, NE // 2) as e:
                for n in range(2):
                    expert(2 * e + n, n)

        @block.vector
        def _(dve):
            dve.wait_ge(S.ld_m, 64)
            dve.tensor_copy(ctx_split[:, 0, :], ctxT[:, :]).then_inc(S.ctx_split, 1)
            dve.wait_ge(S.ctx_split, 1)
            dve.tensor_tensor(ctx_split[:, 1, :], ctxT[:, :], ctx_split[:, 0, :].bitcast(F32), ALU.subtract).then_inc(S.ctx_split, 1)
            for q in range(4):
                for o in range(2):
                    dve.wait_ge(S.m_hi_ready, 2 * q + o + 1)
                    h = slice(4 * q + o, 4 * q + o + 3, 2)
                    hi = m_hi[:, :].rearrange("p (h d) -> p h d", d=P)[:, h, :].bitcast(F32)
                    lo = m_lo[:, :].rearrange("p (h d) -> p h d", d=P)[:, h, :]
                    dve.tensor_tensor(lo, banks[q + 4 * o][:, 0:2 * P].rearrange("p (h d) -> p h d", d=P), hi,
                                      ALU.subtract).then_inc(S.m_lo_ready, 1)

            def g_group(g):
                for h in range(1, NH, 2):
                    dve.wait_ge(S.g_mm, NH * g + h + 1)
                    dst = G[:, cols(g, GB), NK * h:NK * h + NK]
                    dve.tensor_copy(dst, banks[h % 8][:, 0:GN].rearrange("p (b k) -> p b k", k=NK)).then_inc(S.g_dve, 1)
            g_group(0)
            with dve.Fori(1, NB // GB) as g:
                g_group(g)
            dve.wait_ge(S.ld_x, 16 * 5)
            for b in range(NB):
                dve.bn_stats(st0[:, b, :], x_sb[:, b, :]).then_inc(S.st0, 1)
            for b in range(NB):
                own_wait(dve)
                dve.wait_ge(S.st0, b + 1)
                last = dve.bn_aggr(mv0[:, b, :], st0[:, b, :])
            last.then_inc(S.mv0, 1)
            dve.wait_ge(S.tanh_ready, 1)
            dve.wait_ge(S.ld_w, 16 * 8)
            dve.tensor_tensor(valg[:, :], tg[:, 2:3], gates[:, 4:5], ALU.mult).then_inc(S.scaled, 1)
            dve.wait_ge(S.scaled, 1)
            dve.tensor_scalar(vals[:, :, :], vals[:, :, :], valg[:, :], None, ALU.mult).then_inc(S.scaled, 1)
            dve.tensor_scalar(wo[:, :, :], wo[:, :, :], tg[:, 1:2], None, ALU.mult).then_inc(S.scaled, 1)
            dve.tensor_scalar(bout[:, :], bout[:, :], tg[:, 0:1], None, ALU.mult).then_inc(S.xb_ready, 1)
            dve.wait_ge(S.xb_ready, 1)
            dve.tensor_tensor(res[:, :, :], x_sb[:, :, :], bout[:, None, :].broadcast_to([P, NB, D]),
                              ALU.add).then_inc(S.xb_ready, 1)
            dve.wait_ge(S.xb_ready, 2)
            dve.wait_ge(S.consts, 1)

            dve.wait_ge(S.rs0, 1)

            def stats(k, n, ready):
                own_wait(dve)
                dve.wait_ge(ready, n + 1)
                dve.bn_stats(st[k][:, :], row_of(res, n)).then_inc([S.st0, S.st1, S.st2, S.st3][k], 1)

            def mean_var(k, n):
                own_wait(dve)
                dve.wait_ge([S.st0, S.st1, S.st2, S.st3][k], n + 1)
                at(dve, [S.ve0, S.ve1, S.ve2, S.ve3][k], n)
                dve.bn_aggr(mv[k][:, :], st[k][:, :]).then_inc([S.mv0, S.mv1, S.mv2, S.mv3][k], 1)

            def normed(k, n, dst, reader):
                dve.wait_ge([S.rs0, S.rs1, S.rs2, S.rs3][k], n + 1)
                at(dve, reader, n)
                dve.tensor_scalar(dst, row_of(res, n), mv[k][:, 0:1], rs[k][:, :], ALU.subtract,
                                  ALU.mult).then_inc([S.xn0, S.xn1, S.xn2, S.xn3][k], 1)

            def row_max(j, n, bank):
                nh = HCUT[j + 1] - HCUT[j]
                dve.wait_ge(S.s1_mm, 3 * n + 1 + j)
                at(dve, S.p1_exp, 3 * n - 2 + j if not isinstance(n, int) or n > 0 else 0)
                dve.tensor_reduce(nm1[:, HCUT[j]:HCUT[j + 1]], bank[:, 0:nh * NK].rearrange("p (h k) -> p h k", k=NK), AX.X,
                                  ALU.max, negate=True).then_inc(S.nm1_ready, 1)

            def step(n):
                if n.n2 is not None:
                    dve.wait_ge(S.p1_exp, 3 * n.n2 + 3)
                    at(dve, S.p1n_ready, n.n2)
                    dve.reciprocal(ri1[:, :], sum1[:, :]).then_inc(S.ri1_ready, 1)
                if n.n4 is not None:
                    dve.wait_ge(S.rs3, n.n4 + 1)
                    at(dve, S.xn3_t, n.n4)
                    at(dve, S.sc0_done, 16 * n.n4)
                    at(dve, S.sc1_done, 16 * n.n4)
                    x3 = res[:, one(n.n4), :].broadcast_to([P, 2, D])
                    dve.tensor_scalar(rows[:, :, 0:D], x3, mv[3][:, 0:1], rs[3][:, :], ALU.subtract, ALU.mult).then_inc(S.xn3, 1)
                if n.n0 is not None:
                    dve.wait_ge(S.s0_mm, n.n0 + 1)
                    at(dve, S.p0_ready, n.n0)
                    dve.tensor_reduce(nm0[:, :], B1[:, 0:NK], AX.X, ALU.max, negate=True).then_inc(S.nm0_ready, 1)
                    dve.wait_ge(S.p0_ready, n.n0 + 1)
                    dve.reciprocal(ri0[:, :], sum0[:, :]).then_inc(S.ri0_ready, 1)
                if n.n1 is not None:
                    normed(2, n.n1, xn[2][:, :], S.xn2_t)
                if n.n4 is not None:
                    dve.wait_ge(S.rg_mm, n.n4 + 1)
                    at(dve, S.eg_ready, n.n4)
                    dve.tensor_reduce(nmg[:, :], B3[:, 0:NE], AX.X, ALU.max, negate=True).then_inc(S.nmg_ready, 1)
                if n.n0 is not None:
                    dve.wait_ge(S.o0_mm, n.n0 + 1)
                    dve.wait_ge(S.ri0_ready, n.n0 + 1)
                    dve.scalar_tensor_tensor(out=row_of(res, n.n0), in0=B0[:, 0:D], scalar=ri0[:, :], in1=row_of(res, n.n0),
                                             op0=ALU.mult, op1=ALU.add).then_inc(S.x1_ready, 1)
                if n.n3 is not None:
                    dve.wait_ge(S.pv_mm, 2 * n.n3 + 2)
                    at(dve, S.o1_mm, n.n3)
                    dve.tensor_copy(cT[:, 4:8, :], B5[:, :].rearrange("p (m q) -> p m q", q=NQ)).then_inc(S.cT_dve, 1)
                if n.n0 is not None:
                    stats(1, n.n0, S.x1_ready)
                if n.n4 is not None:
                    own_wait(dve)
                    dve.wait_ge(S.eg_ready, n.n4 + 1)
                    dve.max(topg[:, :], eg[:, :]).then_inc(S.topg_ready, 1)
                if n.n0 is not None:
                    mean_var(1, n.n0)
                if n.n4 is not None:
                    dve.reciprocal(rig[:, :], sumg[:, :]).then_inc(S.rig_ready, 1)
                    own_wait(dve)
                    dve.wait_ge(S.topg_ready, n.n4 + 1)
                    dve.max_index(topgi[:, :], topg[:, :], eg[:, :]).then_inc(S.topgi_ready, 1)
                    dve.wait_ge(S.rig_ready, n.n4 + 1)
                    dve.tensor_scalar(rows[:, :, D + 1:D + 2], topg[:, 0:2][:, :, None], rig[:, :], tg[:, 3:4], ALU.mult,
                                      ALU.mult).then_inc(S.cw_ready, 1)
                if n.n1 is not None:
                    row_max(0, n.n1, B2)
                if n.n4 is not None:
                    dve.wait_ge(S.topgi_ready, n.n4 + 1)
                    at(dve, S.slot_f, n.n4)
                    at(dve, S.pos_mm, n.n4)
                    dve.tensor_tensor(oh[:, :, :], iota16[:, None, 0:NE].broadcast_to([P, 2, NE]),
                                      topgi[:, 0:2, None].broadcast_to([P, 2, NE]), ALU.is_equal).then_inc(S.oh_ready, 1)
                if n.n0 is not None:
                    normed(1, n.n0, xn[1][:, :], S.xn1_t)
                if n.n1 is not None:
                    row_max(1, n.n1, B3)
                if n.n4 is not None:
                    dve.wait_ge(S.pos_mm, n.n4 + 1)
                    at(dve, S.slot_e, n.n4)
                    dve.tensor_tensor(pos[:, :, :], B1[:, 0:2 * NE].rearrange("p (k e) -> p k e", k=2), carry[:, :, :],
                                      ALU.add).then_inc(S.pos_ready, 1)
                    dve.tensor_tensor(carry[:, :, :], B1[:, 2 * NE:4 * NE].rearrange("p (k e) -> p k e", k=2), carry[:, :, :],
                                      ALU.add).then_inc(S.carry_ready, 1)
                if n.l is not None:
                    at(dve, S.xn0_t, n.l)
                    dve.tensor_scalar(xn[0][:, :], row_of(x_sb, n.l), mv0[:, one(n.l), 0], rs0[:, one(n.l)], ALU.subtract,
                                      ALU.mult).then_inc(S.xn0, 1)
                if n.n0 is not None:
                    dve.wait_ge(S.er_ready, n.n0 + 1)
                    dve.tensor_scalar(er1[:, :], er[:, :], 1.0, None, ALU.add).then_inc(S.er1_ready, 1)
                    dve.wait_ge(S.er1_ready, n.n0 + 1)
                    dve.reciprocal(sig[:, :], er1[:, :]).then_inc(S.sig_ready, 1)
                if n.n2 is not None:
                    dve.wait_ge(S.p1_t, 4 * n.n2 + 2)
                    dve.tensor_copy(p1T[:, 512:1024], B6[0:NK, :]).then_inc(S.p1T_dve, 1)
                if n.n4 is not None:
                    dve.wait_ge(S.slot_f, n.n4 + 1)
                    with nc.allow_low_precision(reason="one whole number below 2^24 and zeros"):
                        dve.tensor_reduce(sidx[:, :], slot[:, :, :], AX.X, ALU.add).then_inc(S.sidx_ready, 1)
                if n.n0 is not None:
                    own_wait(dve)
                    dve.wait_ge(S.sig_ready, n.n0 + 1)
                    dve.max(top[:, :], sig[:, :]).then_inc(S.top_ready, 1)
                    own_wait(dve)
                    dve.wait_ge(S.top_ready, n.n0 + 1)
                    dve.max_index(topi[:, :], top[:, :], sig[:, :]).then_inc(S.topi_ready, 1)
                    dve.tensor_reduce(den[:, :], top[:, 0:TOPK0], AX.X, ALU.add).then_inc(S.den_ready, 1)
                    dve.wait_ge(S.topi_ready, n.n0 + 1)
                    dve.tensor_tensor(eq[:, :, :], iota16[:, None, :].broadcast_to([P, TOPK0, NE0]),
                                      topi[:, 0:TOPK0, None].broadcast_to([P, TOPK0, NE0]), ALU.is_equal).then_inc(S.eq_ready, 1)
                    dve.wait_ge(S.den_ready, n.n0 + 1)
                    dve.tensor_scalar(den1[:, :], den[:, :], 1e-9, None, ALU.max).then_inc(S.den1_ready, 1)
                    dve.wait_ge(S.eq_ready, n.n0 + 1)
                    dve.tensor_reduce(mask[:, :], eq[:, :, :].rearrange("p k e -> p e k"), AX.X, ALU.add).then_inc(S.mask_ready, 1)
                    dve.wait_ge(S.den1_ready, n.n0 + 1)
                    dve.reciprocal(rden[:, :], den1[:, :]).then_inc(S.rden_ready, 1)
                    dve.wait_ge(S.rden_ready, n.n0 + 1)
                    dve.wait_ge(S.mask_ready, n.n0 + 1)
                    dve.scalar_tensor_tensor(out=w0[:, :], in0=sig[:, :], scalar=rden[:, :], in1=mask[:, :], op0=ALU.mult,
                                             op1=ALU.mult).then_inc(S.w0_ready, 1)
                    dve.wait_ge(S.w0_ready, n.n0 + 1)
                    dve.wait_ge(S.h0_mm, n.n0 + 1)
                    at(dve, S.hw_t, n.n0)
                    dve.scalar_tensor_tensor(out=hw[:, :].rearrange("p (e s) -> p e s", s=ES),
                                             in0=B1[:, :].rearrange("p (e s) -> p e s", s=ES), scalar=0.0,
                                             in1=w0[:, :, None].broadcast_to([P, NE0, ES]), op0=ALU.max,
                                             op1=ALU.mult).then_inc(S.hw_ready, 1)
                if n.n1 is not None:
                    row_max(2, n.n1, B4)
                if n.n2 is not None:
                    dve.wait_ge(S.p1_t, 4 * n.n2 + 4)
                    at(dve, S.pv_mm, 2 * n.n2)
                    dve.tensor_copy(p1T[:, 1536:2048], B6[0:NK, :]).then_inc(S.p1T_dve, 1)
                if n.n3 is not None:
                    dve.wait_ge(S.o1_mm, n.n3 + 1)
                    dve.tensor_tensor(row_of(res, n.n3), B2[:, 0:D], row_of(res, n.n3), ALU.add).then_inc(S.x3_ready, 1)
                    stats(3, n.n3, S.x3_ready)
                    mean_var(3, n.n3)
                if n.n0 is not None:
                    dve.wait_ge(S.y0_mm, n.n0 + 1)
                    dve.tensor_tensor(row_of(res, n.n0), B0[:, 0:D], row_of(res, n.n0), ALU.add).then_inc(S.x2_ready, 1)
                    stats(2, n.n0, S.x2_ready)
                    mean_var(2, n.n0)
            pipeline(dve, step)

            dve.wait_ge(S.ld_b2, 16)

            def expert(e, n):
                dve.wait_ge(S.xeT_mm, e + 1)
                dve.tensor_copy(xeT[n][:, 512:CAP], banks[1][:, 0:TAIL]).then_inc(S.xeT_dve, 1)
                b2e = b2[:, one(e), :]
                dve.wait_ge((S.xe_load0, S.xe_load1)[n], 16 * (e - n) + 32)
                at(dve, S.add_done, 16 * ST * (e - 1))
                dve.tensor_copy(tok_u[n][:, 0:ST - 1], xe[n][:, 0:ST - 1, D])
                dve.tensor_copy(tok_u[n][0:TAIL, ST - 1:ST], xe[n][0:TAIL, ST - 1, D:D + 1]).then_inc(S.tok_conv, 1)
                dve.wait_ge(S.y_mm, 2 * e + 1)
                at(dve, S.add_done, 16 * ST * (e - 1))
                dve.tensor_tensor(ye[n][:, 0:ST - 1, :], banks[6][:, :].rearrange("p (s d) -> p s d", d=D),
                                  b2e.broadcast_to([P, ST - 1, D]), ALU.add).then_inc(S.yb_ready, 1)
                dve.wait_ge(S.y_mm, 2 * e + 2)
                dve.tensor_tensor(ye[n][0:TAIL, ST - 1, :], banks[7][0:TAIL, 0:D],
                                  b2e[0:TAIL].rearrange("p o d -> p (o d)"), ALU.add).then_inc(S.yb_ready, 1)
                dve.wait_ge(S.yb_ready, 2 * e + 1)
                dve.tensor_tensor(ye[n][:, 0:ST - 1, :], ye[n][:, 0:ST - 1, :],
                                  xe[n][:, 0:ST - 1, D + 1:D + 2].broadcast_to([P, ST - 1, D]), ALU.mult).then_inc(S.yw_ready, 1)
            expert(0, 0)
            expert(1, 1)
            with dve.Fori(1, NE // 2) as e:
                for n in range(2):
                    expert(2 * e + n, n)


def kernel(x, ctx_1024, fside_BxS2_0, g_xattn, g_ffn, L0_xattn_W_out, L0_xattn_b_out, L0_ffn_expert_sel, L0_ffn_keys,
           L0_ffn_values, L0_ffn_route_scale, L1_xattn_Wq, L1_xattn_Wk, L1_xattn_Wv, L1_xattn_Wo, L1_ffn_Wg, L1_ffn_W1,
           L1_ffn_b1, L1_ffn_W2, L1_ffn_b2):
    import concourse.bacc as _bacc
    from concourse.bass_utils import run_bass_kernel_spmd as _run

    x = np.asarray(x)
    NB, NQ, D = x.shape
    E, _, H = L1_ffn_W1.shape
    NE0, _, ES = L0_ffn_keys.shape
    lay = {
        "x": x.transpose(1, 0, 2),
        "ctxT": np.asarray(ctx_1024).transpose(2, 0, 1).reshape(D, -1),
        "ind": np.asarray(fside_BxS2_0).T,
        "g_xattn": np.asarray(g_xattn)[None, :],
        "g_ffn": np.asarray(g_ffn)[None, :],
        "rscale": np.asarray(L0_ffn_route_scale)[None, :],
        "woutT": np.asarray(L0_xattn_W_out).T,
        "bout": np.asarray(L0_xattn_b_out)[None, :],
        "selT": np.asarray(L0_ffn_expert_sel).T,
        "keys": np.asarray(L0_ffn_keys).transpose(1, 0, 2).reshape(D, NE0 * ES),
        "vals": np.asarray(L0_ffn_values).reshape(NE0 * ES // P, P, D).transpose(1, 0, 2),
        "wqT": np.asarray(L1_xattn_Wq).T.reshape(-1, P, D).transpose(1, 0, 2),
        "wkT": np.asarray(L1_xattn_Wk).T.reshape(-1, P, D).transpose(1, 0, 2),
        "wv": np.asarray(L1_xattn_Wv),
        "wo": np.asarray(L1_xattn_Wo).reshape(-1, P, D).transpose(1, 0, 2),
        "wgT": np.asarray(L1_ffn_Wg).T,
        "w1": np.asarray(L1_ffn_W1),
        "b1": np.asarray(L1_ffn_b1).reshape(E * H // P, P).T,
        "w2": np.asarray(L1_ffn_W2).reshape(E, H // P, P, D).transpose(0, 2, 1, 3),
        "b2": np.asarray(L1_ffn_b2),
    }
    nc = _bacc.Bacc("TRN2", target_bir_lowering=False, num_devices=1)
    arrays, t = {}, {}
    for name, a in lay.items():
        arrays[f"in_{name}"] = np.ascontiguousarray(a)
        t[name] = nc.dram_tensor(f"in_{name}", a.shape, mybir.dt.from_np(a.dtype), kind="ExternalInput").ap()
    pad = -(-int(round(2 * NB * NQ * 1.05 / E)) // P) * P
    out = nc.dram_tensor("out", (NB * NQ + pad, D), F32, kind="ExternalOutput").ap()
    gated_layers_kernel(nc, t, out)
    r = _run(nc, [arrays], core_ids=[0])
    return r.results[0]["out"][:NB * NQ].reshape(NB, NQ, D)
```

```python
from collections import namedtuple
from contextlib import ExitStack

import numpy as np

import concourse.bass as bass
from concourse import mybir

ALU = mybir.AluOpType
ACT = mybir.ActivationFunctionType
AX = mybir.AxisListType
F32 = mybir.dt.float32
F32R = mybir.dt.float32r
BF16 = mybir.dt.bfloat16
U32 = mybir.dt.uint32

P = 128
EPS = 1e-5
BIG = float(1 << 20)


def gated_layers_kernel(nc, t, out):
    NB, NQ, D = t["x"].shape[1], t["x"].shape[0], t["x"].shape[2]
    NK = t["ind"].shape[0]
    NH = t["wqT"].shape[0] * t["wqT"].shape[1] // 64
    HD = 64
    NE0 = t["selT"].shape[1]
    H0 = t["keys"].shape[1]
    ES = H0 // NE0
    TOPK0 = 4
    NE = t["wgT"].shape[1]
    HID = t["w1"].shape[2]
    MC = HID // P
    T = NB * NQ
    CAP = int(round(2 * T * 1.05 / NE))
    ST = -(-CAP // P)
    TAIL = CAP - (ST - 1) * P
    RW = D + 4
    HCUT = [0, 4, 10, 16]
    GB = 4
    GN = GB * NK
    WARM_START, WARM_EXPERTS = 44, 110
    LN0_PARTS = ((0, 4), (4, NB))
    G_FIRST = 2
    G_FILL = {1: (2, 2, 8, 2, 8, 1, 0), 2: (2, 1, 4, 0, 2, 0, 0)}
    assert sum(map(sum, G_FILL.values())) == (NB // GB - G_FIRST) * NH
    assert NQ == D == P and NH == 16 and CAP % 2 == 0

    ctx = ExitStack()
    with ctx:
        def sb(name, shape, dt=F32):
            return ctx.enter_context(nc.sbuf_tensor(name, shape, dt))

        def sem(name):
            return ctx.enter_context(nc.semaphore(name))

        x_sb = sb("x_sb", [P, NB, D])
        res = sb("res", [P, NB, D])
        G = sb("G", [P, NB, NH * NK])
        ctxT = sb("ctxT", [P, NB * NK])
        ctx_split = sb("ctx_split", [P, 2, NB * NK], F32R)
        wv_hi = sb("wv_hi", [P, NH * HD], F32R)
        wv_lo = sb("wv_lo", [P, NH * HD], F32R)
        m_hi = sb("m_hi", [P, NH * P], F32R)
        m_lo = sb("m_lo", [P, NH * P], F32R)
        stage = sb("stage", [P, 4, NH * HD])
        woutT = sb("woutT", [P, D])
        selT = sb("selT", [P, NE0])
        keys = sb("keys", [P, H0])
        vals = sb("vals", [P, H0 // P, D])
        wo = sb("wo", [P, NH * HD // P, D])
        wgT = sb("wgT", [P, NE])
        ind = sb("ind", [NK, NB])
        b1 = sb("b1", [P, NE * MC])
        bout = sb("bout", [P, D])
        gates = sb("gates", [P, 5])
        tg = sb("tg", [P, 4])
        valg = sb("valg", [P, 1])
        ident = sb("ident", [P, P])
        ones_bf = sb("ones_bf", [P, P], BF16)
        before = sb("before", [P, P], BF16)
        mhalf = sb("mhalf", [P, 1])
        eps = sb("eps", [P, 1])
        eps_gelu = sb("eps_gelu", [P, 1])
        iota16 = sb("iota16", [P, NE0])
        slot0 = sb("slot0", [P, 2, NE])
        sgn = sb("sgn", [P, 2, NE])
        token = sb("token", [P, NB])
        empty = sb("empty", [P, ST, RW])
        carry = sb("carry", [P, 2, NE])
        st = {k: sb(f"st{k}", [P, 6]) for k in (1, 2, 3)}
        mv = {k: sb(f"mv{k}", [P, 2]) for k in (1, 2, 3)}
        ve = {k: sb(f"ve{k}", [P, 1]) for k in (1, 2, 3)}
        rs = {k: sb(f"rs{k}", [P, 1]) for k in (1, 2, 3)}
        st0 = sb("st0_all", [P, NB, 6])
        mv0 = sb("mv0_all", [P, NB, 2])
        ve0 = sb("ve0_all", [P, NB])
        rs0 = sb("rs0_all", [P, NB])
        xn = [sb(f"xn{n}", [P, D]) for n in range(3)]
        xnT = [sb(f"xnT{n}", [P, NQ]) for n in range(4)]
        ctA = sb("ctA", [P, NK])
        ctD = sb("ctD", [P, 2, NK], F32R)
        indD = sb("indD", [NK, 1])
        v0 = sb("v0", [NK, D])
        nm0 = sb("nm0", [P, 1])
        p0 = sb("p0", [P, NK])
        sum0 = sb("sum0", [P, 1])
        ri0 = sb("ri0", [P, 1])
        p0T = sb("p0T", [NK, NQ])
        er = sb("er", [P, NE0])
        er1 = sb("er1", [P, NE0])
        sig = sb("sig", [P, NE0])
        top = sb("top", [P, 8])
        topi = sb("topi", [P, 8], U32)
        den = sb("den", [P, 1])
        den1 = sb("den1", [P, 1])
        rden = sb("rden", [P, 1])
        eq = sb("eq", [P, TOPK0, NE0])
        mask = sb("mask", [P, NE0])
        w0 = sb("w0", [P, NE0])
        hw = sb("hw", [P, H0])
        hwT = sb("hwT", [P, H0])
        nm1 = sb("nm1", [P, NH])
        p1 = sb("p1", [P, NH, NK])
        sum1 = sb("sum1", [P, NH])
        ri1 = sb("ri1", [P, NH])
        p1n = sb("p1n", [P, NH, NK])
        p1T = sb("p1T", [NK, NH * NQ])
        v1 = sb("v1", [NK, NH * HD])
        cT = sb("cT", [P, NH * HD // P, NQ])
        rows = sb("rows", [P, 2, RW])
        nmg = sb("nmg", [P, 1])
        eg = sb("eg", [P, NE])
        sumg = sb("sumg", [P, 1])
        rig = sb("rig", [P, 1])
        topg = sb("topg", [P, 8])
        topgi = sb("topgi", [P, 8], U32)
        oh = sb("oh", [P, 2, NE], BF16)
        pos = sb("pos", [P, 2, NE])
        slot = sb("slot", [P, 2, NE])
        over = sb("over", [P, 2, NE])
        sidx = sb("sidx", [P, 2], U32)

        g_flat = G[:, :, :].rearrange("p b n -> p (b n)")
        cut = [0]

        def over_g(n):
            a = cut[0]
            cut[0] += n
            assert cut[0] <= NB * NH * NK
            return g_flat[:, a:a + n]

        xe = [over_g(ST * RW).rearrange("p (s c) -> p s c", c=RW) for _ in range(2)]
        xeT_over = ctx_split.rearrange("p a k -> p (a k)")
        xeT_hi = [xeT_over[:, CAP * n:CAP * (n + 1)] for n in range(2)]
        xeT_lo = [xeT_over[:, CAP * (n + 2):CAP * (n + 3)] for n in range(2)]
        w1_hi = [m_hi[:, HID * n:HID * (n + 1)] for n in range(2)]
        w1_lo = [m_hi[:, HID * (n + 2):HID * (n + 3)] for n in range(2)]
        SH = ((0, CAP // 4 * 2 + 2), (CAP // 4 * 2 + 2, CAP))
        hT = [over_g(MC * CAP).rearrange("p (m s) -> p m s", s=CAP) for _ in range(2)]
        gate_e = [over_g(ST).rearrange("p (s o) -> p s o", o=1) for _ in range(2)]
        ye = [over_g(ST * D).rearrange("p (s d) -> p s d", d=D) for _ in range(2)]
        b2 = over_g(NE * D).rearrange("p (e d) -> p e d", d=D)
        YS = ((0, 2), (2, ST - 1), (ST - 1, ST))
        tok_u = [sb(f"tok_u{n}", [P, ST], U32) for n in range(2)]
        b1e = [sb(f"b1e{n}", [P, MC]) for n in range(2)]
        w1_sb = [stage[:, n, 0:HID] for n in range(2)]
        w2_sb = [stage[:, n, HID:2 * HID].rearrange("p (m d) -> p m d", d=D) for n in range(2)]

        banks = [ctx.enter_context(nc.psum_tensor(f"bank{n}", [P, 512], F32)) for n in range(8)]
        B0, B1, B2, B3, B4, B5, B6, B7 = banks

        slots_dram = nc.dram_tensor("slots", [NE * CAP, RW], F32, kind="Internal").ap()

        names = """ones_ready ld_m ld_ctx ld_gates ld_wv ld_x ld_w ld_b2 consts tanh_ready xb_ready m_mm m_hi_ready m_lo_ready
        ctx_split wv_hi_ready wv_split g_mm g_act g_dve gf_mm gf_act scaled
        st0 st1 st2 st3 mv0 mv1 mv2 mv3 ve0 ve1 ve2 ve3 rs0 rs1 rs2 rs3 xn0 xn1 xn2 xn3
        xn0_t xn1_t xn2_t xn3_t xnT0 xnT1 xnT2 xnT3
        ctA_ready s0_mm nm0_ready p0_ready v0_mm v0_ready ri0_ready p0_t p0T_ready o0_mm x1_ready
        r0_mm er_ready er1_ready sig_ready top_ready topi_ready eq_ready mask_ready den_ready
        den1_ready rden_ready w0_ready h0_mm hw_ready hw_t hwT_ready y0_mm x2_ready
        s1_mm nm1_ready p1_exp ri1_ready p1n_ready
        ctD_ready v1_mm v1_ready p1_t p1T_act p1T_dve pv_mm cT_act cT_dve o1_mm x3_ready
        rg_mm nmg_ready eg_ready rig_ready topg_ready topgi_ready oh_ready cw_ready tok_ready
        pos_mm pos_ready carry_ready slot_a slot_b slot_c slot_d slot_e slot_f sidx_ready
        sc0_done sc1_done out_rows init_rows out_pad
        w1_load0 w1_load1 w2_load0 w2_load1 w1_hi w1_split xe_load0 xe_load1 xeT_mm xeT_hi xeT_lo h_mm
        h_ready y_mm yb_ready tok_conv add_done indD_ready b1_ready yw0_ready yw1_ready yw2_ready
        """.split()
        S = namedtuple("Semaphores", names)(*[sem(n) for n in names])

        block = ctx.enter_context(nc.Block())

        LAG = 5
        Batches = namedtuple("Batches", "i l n0 n1 n2 n3 n4")

        def at(eng, s, n):
            if not isinstance(n, int) or n > 0:
                eng.wait_ge(s, n)

        def own_wait(eng):
            eng.wait_ge(S.consts, 1)

        def pipeline(eng, step):
            def batches(i):
                if not isinstance(i, int):
                    return Batches(i, *[i - k for k in range(LAG + 1)])
                return Batches(i, *[i - k if 0 <= i - k < NB else None for k in range(LAG + 1)])

            for i in range(LAG + 1):
                step(batches(i))
            with eng.Fori(LAG + 2, NB + 1) as i:
                step(batches(i - 1))
            for i in range(NB, NB + LAG):
                step(batches(i))

        def bank_read(pe, n, *readings):
            for s, per, nth, place, ago in readings:
                b = n.i - 1 - place - ago
                if not isinstance(b, int) or 0 <= b < NB:
                    pe.wait_ge(s, per * b + nth)
                    return

        def g_products(n, place):
            counts = [G_FILL[i][p] for i in G_FILL for p in range(len(G_FILL[i]))]
            if n.l is None or not isinstance(n.i, int) or n.i not in G_FILL:
                return range(0)
            k = len(G_FILL[1]) * (n.i - 1) + place
            return range(sum(counts[:k]), sum(counts[:k + 1]))

        def cols(n, w):
            return bass.ds(n * w, w) if not isinstance(n, int) else slice(n * w, n * w + w)

        def one(n):
            return bass.ds(n, 1) if not isinstance(n, int) else slice(n, n + 1)

        def row_of(tensor, n):
            return tensor[:, one(n), :].rearrange("p o d -> p (o d)")

        @block.sync
        def _(sp):
            sp.dma_start(stage[:, 0, :], t["wqT"].rearrange("p m d -> p (m d)")).then_inc(S.ld_m, 16)
            sp.dma_start(stage[:, 1, :], t["wkT"].rearrange("p m d -> p (m d)")).then_inc(S.ld_m, 16)
            sp.dma_start(ctxT[:, :], t["ctxT"]).then_inc(S.ld_ctx, 16)
            sp.dma_start(x_sb[:, :, :], t["x"]).then_inc(S.ld_x, 16)
            for g, at_g in ((t["g_xattn"], 0), (t["g_ffn"], 2), (t["rscale"], 4)):
                n = g.shape[1]
                sp.dma_start(gates[:, at_g:at_g + n], g.broadcast_to([P, n])).then_inc(S.ld_gates, 16)
            sp.dma_start(bout[:, :], t["bout"].broadcast_to([P, D])).then_inc(S.ld_gates, 16)
            sp.dma_start(stage[:, 2, :], t["wv"]).then_inc(S.ld_wv, 16)
            for dst, name in ((woutT, "woutT"), (selT, "selT"), (keys, "keys"), (wgT, "wgT"), (ind, "ind"),
                              (b1, "b1")):
                sp.dma_start(dst[:, :], t[name]).then_inc(S.ld_w, 16)
            sp.dma_start(vals[:, :, :], t["vals"]).then_inc(S.ld_w, 16)
            sp.dma_start(wo[:, :, :], t["wo"]).then_inc(S.ld_w, 16)
            sp.wait_ge(S.consts, 1)
            for e in range(NE):
                dst = slots_dram[e * CAP:e * CAP + (ST - 1) * P, :].rearrange("(s p) c -> p s c", p=P)
                sp.dma_start(dst, empty[:, 0:ST - 1, :]).then_inc(S.init_rows, 16)
                sp.dma_start(slots_dram[e * CAP + (ST - 1) * P:(e + 1) * CAP, :],
                             empty[0:TAIL, ST - 1, :]).then_inc(S.init_rows, 16)
            sp.dma_start(out[T:T + ST * P, :].rearrange("(s p) d -> p s d", p=P),
                         empty[:, :, 0:D]).then_inc(S.out_pad, 16)

            def step(n):
                if n.n0 is not None:
                    at(sp, S.s0_mm, n.n0)
                    at(sp, S.v0_mm, n.n0)
                    sp.dma_start(ctA[:, :], t["ctxT"][:, cols(n.n0, NK)]).then_inc(S.ctA_ready, 16)
                if n.n2 is not None:
                    at(sp, S.v1_mm, 2 * n.n2)
                    sp.dma_start(ctD[:, :, :].bitcast(F32),
                                 ctx_split[:, :, cols(n.n2, NK)].bitcast(F32)).then_inc(S.ctD_ready, 16)
                if n.n4 is not None:
                    sp.wait_ge(S.x3_ready, n.n4 + 1)
                    sp.dma_start(out[cols(n.n4, P), :], row_of(res, n.n4)).then_inc(S.out_rows, 16)
            sp.wait_ge(S.ctx_split, 2)
            pipeline(sp, step)

            def load(e, n):
                at(sp, S.xeT_mm, e - 1)
                at(sp, S.tok_conv, e - 1)
                if isinstance(e, int):
                    lo = slice(e * CAP, e * CAP + (ST - 1) * P)
                    hi = slice(e * CAP + (ST - 1) * P, (e + 1) * CAP)
                else:
                    lo = bass.ds(e * CAP, (ST - 1) * P)
                    hi = bass.ds(e * CAP + (ST - 1) * P, TAIL)
                sp.dma_start(xe[n][:, 0:ST - 1, :],
                             slots_dram[lo, :].rearrange("(s p) c -> p s c",
                                                         p=P)).then_inc((S.xe_load0, S.xe_load1)[n], 16)
                sp.dma_start(xe[n][0:TAIL, ST - 1, :], slots_dram[hi, :]).then_inc((S.xe_load0, S.xe_load1)[n], 16)

            def weights(e, n):
                at(sp, S.w1_split, e - 1)
                w1 = t["w1"][one(e), :, :].rearrange("o p h -> p (o h)")
                sp.dma_start(w1_sb[n], w1).then_inc((S.w1_load0, S.w1_load1)[n], 16)
                at(sp, S.y_mm, 3 * (e - 1))
                w2 = t["w2"][one(e), :, :, :].rearrange("o p m d -> p (o m) d")
                sp.dma_start(w2_sb[n], w2).then_inc((S.w2_load0, S.w2_load1)[n], 16)

            sp.wait_ge(S.m_mm, 4)
            weights(0, 0)
            weights(1, 1)
            sp.wait_ge(S.s1_mm, 3 * NB)
            sp.dma_start(b2, t["b2"][None, :, :].broadcast_to([P, NE, D])).then_inc(S.ld_b2, 16)
            sp.wait_ge(S.sc0_done, 16 * NB)
            sp.wait_ge(S.sc1_done, 16 * NB)
            load(0, 0)
            load(1, 1)
            with sp.Fori(1, NE // 2) as e:
                for n in range(2):
                    load(2 * e + n, n)
                    weights(2 * e + n, n)
            sp.wait_ge(S.add_done, 16 * ST * NE)
            sp.wait_ge(S.out_pad, 16)
            sp.wait_ge(S.out_rows, 16 * NB)

        @block.gpsimd
        def _(pool):
            pool.memset(ones_bf[:, :], 1.0).then_inc(S.ones_ready, 1)
            pool.memset(empty[:, :, :], 0.0)
            pool.memset(mhalf[:, :], -0.5)
            pool.memset(eps[:, :], EPS)
            pool.memset(carry[:, :, :], 0.0)
            pool.memset(sgn[:, 0, :], 1.0)
            pool.memset(sgn[:, 1, :], -1.0)
            pool.memset(rows[:, :, :], 0.0)
            pool.iota(iota16[:, :], [[1, NE0]], base=0, channel_multiplier=0, allow_small_or_imprecise_dtypes=True)
            pool.iota(slot0[:, :, :], [[CAP - 1, 2], [CAP, NE]], base=0, channel_multiplier=0,
                      allow_small_or_imprecise_dtypes=True)
            pool.iota(token[:, :], [[NQ, NB]], base=0, channel_multiplier=1, allow_small_or_imprecise_dtypes=True)
            pool.memset(ident[:, :], 0.0).then_inc(S.slot_a, 1)
            pool.wait_ge(S.slot_a, 1)
            pool.iota(empty[:, :, D:D + 1], [[P, ST], [0, 1]], base=T, channel_multiplier=1, allow_small_or_imprecise_dtypes=True)
            pool.affine_select(out=ident[:, :], in_=ident[:, :], compare_op=ALU.not_equal, fill=1.0, base=0,
                               pattern=[[-1, P]], channel_multiplier=1)
            pool.affine_select(out=before[:, :], in_=ones_bf[:, :], compare_op=ALU.is_gt, fill=0.0, base=0,
                               pattern=[[1, P]], channel_multiplier=-1).then_inc(S.consts, 1)
            pool.wait_ge(S.tanh_ready, 1)
            pool.tensor_tensor(valg[:, :], tg[:, 2:3], gates[:, 4:5], ALU.mult).then_inc(S.scaled, 1)
            pool.tensor_scalar(bout[:, :], bout[:, :], tg[:, 0:1], None, ALU.mult).then_inc(S.xb_ready, 1)
            pool.wait_ge(S.xb_ready, 1)
            pool.wait_ge(S.ld_x, 16)
            pool.tensor_tensor(res[:, :, :], x_sb[:, :, :], bout[:, None, :].broadcast_to([P, NB, D]),
                               ALU.add).then_inc(S.xb_ready, 1)
            for k, (a, b) in enumerate(LN0_PARTS):
                pool.wait_ge(S.mv0, k + 1)
                pool.tensor_tensor(ve0[:, a:b], mv0[:, a:b, 1], eps[:, :].broadcast_to([P, b - a]),
                                   ALU.add).then_inc(S.ve0, 1)
                pool.wait_ge(S.ve0, k + 1)
                pool.tensor_tensor(rs0[:, a:b], ve0[:, a:b], mhalf[:, :].broadcast_to([P, b - a]),
                                   ALU.pow).then_inc(S.rs0, 1)

            def rstd(k, n):
                at(pool, [S.xn0, S.xn1, S.xn2, S.xn3][k], n)
                pool.wait_ge([S.ve0, S.ve1, S.ve2, S.ve3][k], n + 1)
                pool.tensor_tensor(rs[k][:, :], ve[k][:, :], mhalf[:, :],
                                   ALU.pow).then_inc([S.rs0, S.rs1, S.rs2, S.rs3][k], 1)

            def var_eps(k, n):
                pool.wait_ge([S.mv0, S.mv1, S.mv2, S.mv3][k], n + 1)
                pool.tensor_tensor(ve[k][:, :], mv[k][:, 1:2], eps[:, :],
                                   ALU.add).then_inc([S.ve0, S.ve1, S.ve2, S.ve3][k], 1)

            def step(n):
                if n.n2 is not None:
                    at(pool, S.v1_ready, 2 * n.n2)
                    pool.tensor_copy(indD[:, :], ind[:, one(n.n2)]).then_inc(S.indD_ready, 1)
                if n.n1 is not None:
                    var_eps(2, n.n1)
                if n.n4 is not None:
                    at(pool, S.sc0_done, 16 * n.n4)
                    at(pool, S.sc1_done, 16 * n.n4)
                    pool.tensor_copy(rows[:, :, D:D + 1],
                                     token[:, one(n.n4)][:, None, :].broadcast_to([P, 2, 1])).then_inc(S.tok_ready, 1)
                if n.n1 is not None:
                    rstd(2, n.n1)
                if n.n2 is not None:
                    pool.wait_ge(S.ri1_ready, n.n2 + 1)
                    at(pool, S.p1_t, 4 * n.n2)
                    pool.tensor_tensor(p1n[:, :, :], p1[:, :, :], ri1[:, :, None].broadcast_to([P, NH, NK]),
                                       ALU.mult).then_inc(S.p1n_ready, 1)
                if n.n0 is not None:
                    var_eps(1, n.n0)
                    rstd(1, n.n0)
                if n.n4 is not None:
                    k = 1 + n.n4
                    pool.wait_ge(S.pos_ready, k)
                    pool.wait_ge(S.carry_ready, k)
                    at(pool, S.sidx_ready, n.n4)
                    pool.tensor_tensor(slot[:, :, :], pos[:, :, :], sgn[:, :, :], ALU.mult).then_inc(S.slot_a, 1)
                    pool.wait_ge(S.slot_a, k + 1)
                    pool.tensor_tensor(pos[:, 1, :], pos[:, 1, :], carry[:, 0, :], ALU.add).then_inc(S.slot_c, 1)
                    pool.tensor_tensor(slot[:, :, :], slot[:, :, :], slot0[:, :, :], ALU.add).then_inc(S.slot_b, 1)
                    own_wait(pool)
                    pool.wait_ge(S.slot_c, k)
                    pool.tensor_scalar(over[:, :, :], pos[:, :, :], float(CAP), BIG, ALU.is_ge,
                                       ALU.mult).then_inc(S.slot_d, 1)
                    pool.wait_ge(S.slot_b, k)
                    pool.wait_ge(S.slot_d, k)
                    pool.tensor_tensor(slot[:, :, :], slot[:, :, :], over[:, :, :], ALU.add).then_inc(S.slot_e, 1)
                    pool.wait_ge(S.slot_e, k)
                    pool.tensor_tensor(slot[:, :, :], slot[:, :, :], oh[:, :, :], ALU.mult).then_inc(S.slot_f, 1)
                    own_wait(pool)
                    pool.wait_ge(S.sidx_ready, k)
                    pool.wait_ge(S.cw_ready, k)
                    pool.wait_ge(S.tok_ready, k)
                    if isinstance(n.n4, int) and n.n4 == 0:
                        pool.wait_ge(S.init_rows, 32 * NE)
                    for c, done in ((0, S.sc0_done), (1, S.sc1_done)):
                        pool.indirect_dma_start(slots_dram, bass.IndirectOffsetOnAxis(ap=sidx[:, c:c + 1], axis=0),
                                                rows[:, c, :], None, bounds_check=NE * CAP - 1,
                                                oob_is_err=False).then_inc(done, 16)
                if n.n3 is not None:
                    var_eps(3, n.n3)
                    rstd(3, n.n3)
            pipeline(pool, step)

            pool.wait_ge(S.out_rows, 16 * NB)
            pool.wait_ge(S.out_pad, 16)

            def bias(e, n):
                at(pool, S.h_ready, 2 * MC * (e - 1))
                pool.tensor_copy(b1e[n][:, :], b1[:, cols(e, MC)]).then_inc(S.b1_ready, 1)

            def add(e, n):
                pool.wait_ge(S.tok_conv, e + 1)
                pool.wait_ge(S.yb_ready, 3 * e + 1)
                at(pool, S.add_done, 16 * ST * e)
                a, b = YS[0]
                pool.tensor_tensor(ye[n][:, a:b, :], ye[n][:, a:b, :], gate_e[n][:, a:b, :].broadcast_to([P, b - a, D]),
                                   ALU.mult).then_inc(S.yw0_ready, 1)
                for j, (a, b) in enumerate(YS):
                    own_wait(pool)
                    pool.wait_ge((S.yw0_ready, S.yw1_ready, S.yw2_ready)[j], e + 1)
                    for s in range(a, b):
                        k = P if s < ST - 1 else TAIL
                        pool.indirect_dma_start(out, bass.IndirectOffsetOnAxis(ap=tok_u[n][0:k, s:s + 1], axis=0),
                                                ye[n][0:k, s, :], None, bounds_check=T + ST * P - 1, oob_is_err=True,
                                                compute_op=ALU.add).then_inc(S.add_done, 16)
            bias(0, 0)
            bias(1, 1)
            add(0, 0)
            with pool.Fori(1, NE // 2) as e:
                bias(2 * e, 0)
                add(2 * e - 1, 1)
                bias(2 * e + 1, 1)
                add(2 * e, 0)
            add(NE - 1, 1)

        @block.tensor
        def _(pe):
            def keep_warm(count):
                for _ in range(count):
                    pe.matmul(banks[7][:, 0:P], ones_bf[:, :], ones_bf[:, :], start=True, stop=True)

            pe.wait_ge(S.ones_ready, 1)
            keep_warm(WARM_START)
            pe.wait_ge(S.ld_m, 32)
            for q in range(4):
                for j in range(4):
                    h = 4 * q + j
                    r = slice(HD * (h % 2), HD * (h % 2) + HD)
                    c = slice(P * (h // 2), P * (h // 2) + P)
                    mm = pe.matmul(banks[q + 4 * (h % 2)][:, P * (j // 2):P * (j // 2) + P], stage[r, 1, c], stage[r, 0, c], start=True, stop=True)
                mm.then_inc(S.m_mm, 1)
            pe.wait_ge(S.ctx_split, 2)

            def g_group(g, first=False):
                for h in range(NH):
                    if first:
                        pe.wait_ge(S.m_lo_ready, max(2 * (h // 4) + h % 2, 2 * (h % 4) + h // 4 % 2) + 1)
                    k = NH // 2 * g + h // 2
                    at(pe, S.g_act if h % 2 == 0 else S.g_dve, k - 3)
                    c = cols(g, GN)
                    w = slice(P * h, P * h + P)
                    dst = banks[h % 8][:, 0:GN]
                    pe.matmul(dst, m_hi[:, w], ctx_split[:, 0, c], start=True, stop=False)
                    pe.matmul(dst, m_hi[:, w], ctx_split[:, 1, c], start=False, stop=False)
                    pe.matmul(dst, m_lo[:, w], ctx_split[:, 0, c], start=False, stop=True).then_inc(S.g_mm, 1)
            g_group(0, first=True)
            for g in range(1, G_FIRST):
                g_group(g)
            pe.wait_ge(S.g_act, G_FIRST * NH // 2)
            pe.wait_ge(S.g_dve, G_FIRST * NH // 2)
            pe.wait_ge(S.consts, 1)
            pe.wait_ge(S.ld_w, 16 * 8)

            def context(bank, heads):
                for h in heads:
                    mm = pe.matmul(bank[HD * (h % 2):HD * (h % 2) + HD, P * (h // 2 % 4):P * (h // 2 % 4) + P],
                                   v1[:, HD * h:HD * h + HD], p1T[:, P * h:P * h + P], start=True, stop=True)
                return mm

            def values(j, bank):
                c = slice(512 * j, 512 * j + 512)
                pe.matmul(bank[0:NK, :], ctD[:, 0, :], wv_hi[:, c], start=True, stop=False)
                pe.matmul(bank[0:NK, :], ctD[:, 0, :], wv_lo[:, c], start=False, stop=False)
                pe.matmul(bank[0:NK, :], ctD[:, 1, :], wv_hi[:, c], start=False, stop=True).then_inc(S.v1_mm, 1)

            def scores(j, n, bank):
                a, b = HCUT[j] * NK, HCUT[j + 1] * NK
                pe.matmul(bank[:, 0:b - a], xnT[2][:, :], row_of(G, n)[:, a:b], start=True,
                          stop=True).then_inc(S.s1_mm, 1)

            def probs_t(j, bank):
                for h in range(4 * j, 4 * j + 4):
                    mm = pe.transpose(bank[0:NK, P * (h % 4):P * (h % 4) + P], p1n[:, h, :], ident[:, :])
                mm.then_inc(S.p1_t, 1)

            def g_fill(n, place):
                for q in g_products(n, place):
                    g, hh = G_FIRST + q // NH, q % NH
                    at(pe, S.gf_act, q - 2)
                    c = cols(g, GN)
                    w = slice(P * hh, P * hh + P)
                    dst = banks[5 + q % 3][:, 0:GN]
                    pe.matmul(dst, m_hi[:, w], ctx_split[:, 0, c], start=True, stop=False)
                    pe.matmul(dst, m_hi[:, w], ctx_split[:, 1, c], start=False, stop=False)
                    pe.matmul(dst, m_lo[:, w], ctx_split[:, 0, c], start=False, stop=True).then_inc(S.gf_mm, 1)

            def step(n):
                if isinstance(n.i, int) and n.i == 3:
                    pe.wait_ge(S.gf_act, (NB // GB - G_FIRST) * NH)
                    pe.wait_ge(S.wv_split, 1)
                    pe.wait_ge(S.scaled, 3)
                if n.n0 is not None:
                    pe.wait_ge(S.xn0, n.n0 + 1)
                    at(pe, S.hw_ready, n.n0)
                    pe.transpose(B1[:, 0:P], xn[0][:, :], ident[:, :]).then_inc(S.xn0_t, 1)
                if n.n3 is not None:
                    pe.wait_ge(S.v1_ready, 2 * n.n3 + 2)
                    pe.wait_ge(S.p1T_act, 2 * n.n3 + 2)
                    context(B5, range(8, 12))
                if n.n0 is not None:
                    pe.wait_ge(S.ctA_ready, 16 * n.n0 + 16)
                    at(pe, S.x2_ready, n.n0)
                    pe.matmul(B0[0:NK, 0:D], ctA[:, :], woutT[:, :], start=True, stop=True).then_inc(S.v0_mm, 1)
                    pe.wait_ge(S.xnT0, n.n0 + 1)
                    pe.matmul(B1[:, 0:NK], xnT[0][:, :], ctA[:, :], start=True, stop=True).then_inc(S.s0_mm, 1)
                g_fill(n, 0)
                if n.n2 is not None:
                    pe.wait_ge(S.ctD_ready, 16 * n.n2 + 16)
                    bank_read(pe, n, (S.x3_ready, 1, 1, 3, 1), (S.p1_exp, 3, 1, 1, 1), (S.v1_ready, 2, 1, 2, 1))
                    values(0, B2)
                if n.n0 is not None:
                    pe.wait_ge(S.v0_ready, n.n0 + 1)
                    pe.wait_ge(S.p0_ready, n.n0 + 1)
                    pe.transpose(B0[0:NK, 0:P], p0[:, :], ident[:, :]).then_inc(S.p0_t, 1)
                if n.n4 is not None:
                    pe.wait_ge(S.xn3, n.n4 + 1)
                    bank_read(pe, n, (S.cT_act, 1, 1, 2, 1), (S.p1_exp, 3, 2, 1, 1), (S.eg_ready, 1, 1, 4, 1))
                    pe.transpose(B3[:, 0:P], rows[:, 0, 0:D], ident[:, :]).then_inc(S.xn3_t, 1)
                g_fill(n, 1)
                if n.n3 is not None:
                    pe.wait_ge(S.p1T_dve, 2 * n.n3 + 2)
                    context(B5, range(12, 16)).then_inc(S.pv_mm, 1)
                if n.n4 is not None:
                    pe.wait_ge(S.xnT3, n.n4 + 1)
                    pe.matmul(B3[:, 0:NE], xnT[3][:, :], wgT[:, :], start=True, stop=True).then_inc(S.rg_mm, 1)
                if n.n0 is not None:
                    pe.wait_ge(S.p0T_ready, n.n0 + 1)
                    pe.matmul(B0[:, 0:D], p0T[:, :], v0[:, :], start=True, stop=True).then_inc(S.o0_mm, 1)
                g_fill(n, 2)
                if n.n1 is not None:
                    pe.wait_ge(S.xn2, n.n1 + 1)
                    bank_read(pe, n, (S.p0_ready, 1, 1, 0, 0), (S.hw_ready, 1, 1, 0, 1), (S.carry_ready, 1, 1, 4, 1),
                              (S.xnT2, 1, 1, 1, 1))
                    pe.transpose(B1[:, 0:P], xn[2][:, :], ident[:, :]).then_inc(S.xn2_t, 1)
                if n.n2 is not None:
                    bank_read(pe, n, (S.p1_exp, 3, 3, 1, 1), (S.v1_ready, 2, 2, 2, 1))
                    values(1, B4)
                if n.n1 is not None:
                    pe.wait_ge(S.xnT2, n.n1 + 1)
                    bank_read(pe, n, (S.v1_ready, 2, 1, 2, 0), (S.x3_ready, 1, 1, 3, 1), (S.p1_exp, 3, 1, 1, 1))
                    scores(0, n.n1, B2)
                    bank_read(pe, n, (S.eg_ready, 1, 1, 4, 0), (S.cT_act, 1, 1, 2, 1), (S.p1_exp, 3, 2, 1, 1))
                    scores(1, n.n1, B3)
                if n.n2 is not None:
                    pe.wait_ge(S.p1n_ready, n.n2 + 1)
                    bank_read(pe, n, (S.cT_dve, 1, 1, 3, 0), (S.p1T_act, 2, 1, 2, 1))
                    probs_t(0, B5)
                if n.n4 is not None:
                    pe.wait_ge(S.oh_ready, n.n4 + 1)
                    bank_read(pe, n, (S.xnT2, 1, 1, 1, 0), (S.p0_ready, 1, 1, 0, 0), (S.hw_ready, 1, 1, 0, 1),
                              (S.carry_ready, 1, 1, 4, 1))
                    ohf = oh[:, :, :].rearrange("p k e -> p (k e)")
                    pe.matmul(B1[:, 0:2 * NE], before[:, :], ohf, start=True, stop=True)
                    pe.matmul(B1[:, 2 * NE:4 * NE], ones_bf[:, :], ohf, start=True, stop=True).then_inc(S.pos_mm, 1)
                if n.n0 is not None:
                    pe.wait_ge(S.xn1, n.n0 + 1)
                    pe.transpose(B0[:, 0:P], xn[1][:, :], ident[:, :]).then_inc(S.xn1_t, 1)
                g_fill(n, 3)
                if n.n2 is not None:
                    bank_read(pe, n, (S.p1T_dve, 2, 2, 2, 1))
                    probs_t(1, B6)
                    bank_read(pe, n, (S.p1T_act, 2, 2, 2, 1))
                    probs_t(2, B7)
                if n.n0 is not None:
                    pe.wait_ge(S.xnT1, n.n0 + 1)
                    pe.matmul(B0[:, 0:NE0], xnT[1][:, :], selT[:, :], start=True, stop=True).then_inc(S.r0_mm, 1)
                g_fill(n, 4)
                if n.n0 is not None:
                    bank_read(pe, n, (S.carry_ready, 1, 1, 4, 0), (S.xnT2, 1, 1, 1, 0), (S.p0_ready, 1, 1, 0, 0))
                    pe.matmul(B1[:, :], xnT[1][:, :], keys[:, :], start=True, stop=True).then_inc(S.h0_mm, 1)
                if n.n1 is not None:
                    bank_read(pe, n, (S.v1_ready, 2, 2, 2, 0), (S.p1_exp, 3, 3, 1, 1))
                    scores(2, n.n1, B4)
                if n.n2 is not None:
                    pe.wait_ge(S.p1T_dve, 2 * n.n2 + 1)
                    probs_t(3, B6)
                if n.n3 is not None:
                    pe.wait_ge(S.cT_act, n.n3 + 1)
                    bank_read(pe, n, (S.p1_exp, 3, 1, 1, 0), (S.v1_ready, 2, 1, 2, 0), (S.x3_ready, 1, 1, 3, 1))
                    for m in range(4):
                        pe.matmul(B2[:, 0:D], cT[:, m, :], wo[:, m, :], start=m == 0, stop=False)
                if n.n2 is not None:
                    pe.wait_ge(S.v1_ready, 2 * n.n2 + 1)
                    bank_read(pe, n, (S.p1_exp, 3, 2, 1, 0), (S.eg_ready, 1, 1, 4, 0), (S.cT_act, 1, 1, 2, 1))
                    context(B3, range(4, 8))
                if n.n0 is not None:
                    pe.wait_ge(S.hw_ready, n.n0 + 1)
                    for m in range(H0 // P):
                        mm = pe.transpose(B0[:, P * m:P * m + P], hw[:, P * m:P * m + P], ident[:, :])
                    mm.then_inc(S.hw_t, 1)
                g_fill(n, 5)
                if n.n3 is not None:
                    pe.wait_ge(S.cT_dve, n.n3 + 1)
                    for m in range(4, 8):
                        mm = pe.matmul(B2[:, 0:D], cT[:, m, :], wo[:, m, :], start=False, stop=m == 7)
                    mm.then_inc(S.o1_mm, 1)
                if n.n0 is not None:
                    pe.wait_ge(S.hwT_ready, n.n0 + 1)
                    if isinstance(n.n0, int) and n.n0 == 0:
                        pe.wait_ge(S.scaled, 2)
                    for m in range(H0 // P):
                        mm = pe.matmul(B0[:, 0:D], hwT[:, P * m:P * m + P], vals[:, m, :], start=m == 0, stop=m == H0 // P - 1)
                    mm.then_inc(S.y0_mm, 1)
                g_fill(n, 6)
                if n.n2 is not None:
                    pe.wait_ge(S.p1T_act, 2 * n.n2 + 1)
                    context(B3, range(0, 4)).then_inc(S.pv_mm, 1)
            pipeline(pe, step)

            def columns(e, n):
                pe.wait_ge((S.xe_load0, S.xe_load1)[n], 16 * (e - n) + 32)
                at(pe, S.xeT_lo, e)
                at(pe, S.yb_ready, 3 * (e - 1))
                for s in range(ST):
                    k = P if s < ST - 1 else TAIL
                    mm = pe.transpose(banks[s // 4][:, P * (s % 4):P * (s % 4) + k], xe[n][0:k, s, 0:D], ident[0:k, 0:k])
                mm.then_inc(S.xeT_mm, 1)

            def hidden(e, n):
                pe.wait_ge(S.w1_split, e + 1)
                pe.wait_ge(S.xeT_lo, e + 1)
                for m in range(MC):
                    for j, (a, b) in enumerate(SH):
                        k = 2 * m + j
                        at(pe, S.h_ready, 2 * MC * e + k - 3)
                        w = slice(P * m, P * m + P)
                        dst = banks[2 + k % 4][:, 0:b - a]
                        pe.matmul(dst, w1_hi[n][:, w], xeT_hi[n][:, a:b], start=True, stop=False)
                        pe.matmul(dst, w1_hi[n][:, w], xeT_lo[n][:, a:b], start=False, stop=False)
                        pe.matmul(dst, w1_lo[n][:, w], xeT_hi[n][:, a:b], start=False, stop=True).then_inc(S.h_mm, 1)

            def y_rows(e, n):
                pe.wait_ge((S.w2_load0, S.w2_load1)[n], 8 * (e - n) + 16)
                pe.wait_ge(S.h_ready, 2 * MC * (e + 1))
                for j, (a, b) in enumerate(YS):
                    if j < 2 or isinstance(e, int) and e == NE - 1:
                        at(pe, S.yb_ready, 3 * e - 2 + j)
                    else:
                        pe.wait_ge(S.xeT_lo, e + 2)
                    for s in range(a, b):
                        k = P if s < ST - 1 else TAIL
                        for m in range(MC):
                            mm = pe.matmul((banks[6], banks[7], banks[1])[j][0:k, P * (s - a):P * (s - a) + D],
                                           hT[n][:, m, P * s:P * s + k], w2_sb[n][:, m, :], start=m == 0, stop=m == MC - 1)
                    mm.then_inc(S.y_mm, 1)

            def expert(e, n):
                columns(e + 1, 1 - n)
                y_rows(e, n)
                hidden(e + 1, 1 - n)

            keep_warm(WARM_EXPERTS)
            columns(0, 0)
            hidden(0, 0)
            expert(0, 0)
            with pe.Fori(1, NE // 2) as e:
                expert(2 * e - 1, 1)
                expert(2 * e, 0)
            y_rows(NE - 1, 1)

        @block.scalar
        def _(act):
            for q in range(4):
                act.wait_ge(S.m_mm, q + 1)
                for o in range(2):
                    dst = m_hi[:, :].rearrange("p (h d) -> p h d", d=P)[:, 4 * q + o:4 * q + o + 3:2, :]
                    act.copy(dst,
                             banks[q + 4 * o][:, 0:2 * P].rearrange("p (h d) -> p h d", d=P)).then_inc(S.m_hi_ready, 1)

            act.wait_ge(S.ld_gates, 16 * 4)
            act.activation(tg[:, :], gates[:, 0:4], ACT.Tanh, bias=0.0).then_inc(S.tanh_ready, 1)

            def g_group(g):
                for h in range(0, NH, 2):
                    act.wait_ge(S.g_mm, NH * g + h + 1)
                    dst = G[:, cols(g, GB), NK * h:NK * h + NK]
                    act.copy(dst, banks[h % 8][:, 0:GN].rearrange("p (b k) -> p b k", k=NK)).then_inc(S.g_act, 1)
            g_group(0)
            act.wait_ge(S.ld_wv, 16)
            act.copy(wv_hi[:, :], stage[:, 2, :]).then_inc(S.wv_hi_ready, 1)
            act.wait_ge(S.scaled, 1)
            act.wait_ge(S.ld_w, 16 * 8)
            act.activation(vals[:, :, :], vals[:, :, :], ACT.Copy, scale=valg[:, :]).then_inc(S.scaled, 1)
            act.wait_ge(S.tanh_ready, 1)
            act.activation(wo[:, :, :], wo[:, :, :], ACT.Copy, scale=tg[:, 1:2]).then_inc(S.scaled, 1)
            for g in range(1, G_FIRST):
                g_group(g)

            def g_fill(n, place):
                for q in g_products(n, place):
                    g, hh = G_FIRST + q // NH, q % NH
                    act.wait_ge(S.gf_mm, q + 1)
                    act.copy(G[:, cols(g, GB), NK * hh:NK * hh + NK],
                             banks[5 + q % 3][:, 0:GN].rearrange("p (b k) -> p b k", k=NK)).then_inc(S.gf_act, 1)

            def softmax_exp(j, n, bank):
                act.wait_ge(S.nm1_ready, 3 * n + 1 + j)
                if j == 0:
                    at(act, S.p1n_ready, n)
                for h in range(HCUT[j], HCUT[j + 1]):
                    c = NK * (h - HCUT[j])
                    last = act.activation(p1[:, h, :], bank[:, c:c + NK], ACT.Exp, bias=nm1[:, h:h + 1],
                                          accum_out=sum1[:, h:h + 1])
                last.then_inc(S.p1_exp, 1)

            def step(n):
                if n.n0 is not None:
                    act.wait_ge(S.xn0_t, n.n0 + 1)
                    at(act, S.s0_mm, n.n0)
                    act.mul(xnT[0][:, :], B1[:, 0:P], float(D) ** -0.5).then_inc(S.xnT0, 1)
                if n.n3 is not None:
                    act.wait_ge(S.pv_mm, 2 * n.n3 + 1)
                    at(act, S.o1_mm, n.n3)
                    act.copy(cT[:, 0:4, :], B3[:, :].rearrange("p (m q) -> p m q", q=NQ)).then_inc(S.cT_act, 1)
                if n.n0 is not None:
                    act.wait_ge(S.v0_mm, n.n0 + 1)
                    at(act, S.o0_mm, n.n0)
                    act.activation(v0[:, :], B0[0:NK, 0:D], ACT.Copy, scale=tg[0:NK, 0:1]).then_inc(S.v0_ready, 1)
                    act.wait_ge(S.nm0_ready, n.n0 + 1)
                    at(act, S.p0_t, n.n0)
                    at(act, S.ri0_ready, n.n0)
                    act.activation(p0[:, :], B1[:, 0:NK], ACT.Exp, bias=nm0[:, :],
                                   accum_out=sum0[:, :]).then_inc(S.p0_ready, 1)
                g_fill(n, 0)
                if n.n4 is not None:
                    act.wait_ge(S.xn3_t, n.n4 + 1)
                    act.copy(xnT[3][:, :], B3[:, 0:P]).then_inc(S.xnT3, 1)
                if n.n0 is not None:
                    act.wait_ge(S.p0_t, n.n0 + 1)
                    act.copy(p0T[:, :], B0[0:NK, 0:P]).then_inc(S.p0T_ready, 1)
                g_fill(n, 1)
                g_fill(n, 2)
                if n.n2 is not None:
                    act.wait_ge(S.v1_mm, 2 * n.n2 + 1)
                    act.wait_ge(S.indD_ready, n.n2 + 1)
                    at(act, S.pv_mm, 2 * n.n2 - 1 if not isinstance(n.n2, int) or n.n2 > 0 else 0)
                    act.activation(v1[:, 0:512], B2[0:NK, :], ACT.Copy, scale=indD[:, :]).then_inc(S.v1_ready, 1)
                if n.n1 is not None:
                    act.wait_ge(S.xn2_t, n.n1 + 1)
                    at(act, S.s1_mm, 3 * n.n1)
                    act.mul(xnT[2][:, :], B1[:, 0:P], float(HD) ** -0.5).then_inc(S.xnT2, 1)
                if n.n4 is not None:
                    act.wait_ge(S.nmg_ready, n.n4 + 1)
                    at(act, S.topgi_ready, n.n4)
                    at(act, S.rig_ready, n.n4)
                    act.activation(eg[:, :], B3[:, 0:NE], ACT.Exp, bias=nmg[:, :],
                                   accum_out=sumg[:, :]).then_inc(S.eg_ready, 1)
                if n.n2 is not None:
                    act.wait_ge(S.v1_mm, 2 * n.n2 + 2)
                    at(act, S.pv_mm, 2 * n.n2)
                    act.activation(v1[:, 512:1024], B4[0:NK, :], ACT.Copy, scale=indD[:, :]).then_inc(S.v1_ready, 1)
                if n.n1 is not None:
                    softmax_exp(0, n.n1, B2)
                if n.n0 is not None:
                    act.wait_ge(S.xn1_t, n.n0 + 1)
                    at(act, S.h0_mm, n.n0)
                    act.copy(xnT[1][:, :], B0[:, 0:P]).then_inc(S.xnT1, 1)
                    act.wait_ge(S.r0_mm, n.n0 + 1)
                    at(act, S.er1_ready, n.n0)
                    act.activation(er[:, :], B0[:, 0:NE0], ACT.Exp, bias=0.0, scale=-1.0).then_inc(S.er_ready, 1)
                g_fill(n, 3)
                if n.n1 is not None:
                    softmax_exp(1, n.n1, B3)
                if n.n2 is not None:
                    act.wait_ge(S.p1_t, 4 * n.n2 + 1)
                    at(act, S.pv_mm, 2 * n.n2 - 1 if not isinstance(n.n2, int) or n.n2 > 0 else 0)
                    act.copy(p1T[:, 0:512], B5[0:NK, :]).then_inc(S.p1T_act, 1)
                    act.wait_ge(S.p1_t, 4 * n.n2 + 3)
                    at(act, S.pv_mm, 2 * n.n2)
                    act.copy(p1T[:, 1024:1536], B7[0:NK, :]).then_inc(S.p1T_act, 1)
                g_fill(n, 4)
                if n.n0 is not None:
                    act.wait_ge(S.hw_t, n.n0 + 1)
                    at(act, S.y0_mm, n.n0)
                    act.copy(hwT[:, :], B0[:, :]).then_inc(S.hwT_ready, 1)
                g_fill(n, 5)
                g_fill(n, 6)
                if n.n1 is not None:
                    softmax_exp(2, n.n1, B4)
            pipeline(act, step)
            act.activation(eps_gelu[:, :], eps[:, :], ACT.Gelu, bias=0.0)

            def expert(e, n):
                act.wait_ge(S.xeT_mm, e + 1)
                act.copy(xeT_hi[n][:, 0:512], banks[0][:, :])
                act.copy(xeT_hi[n][:, 512:CAP], banks[1][:, 0:TAIL]).then_inc(S.xeT_hi, 1)
                for m in range(MC):
                    for j, (a, b) in enumerate(SH):
                        k = 2 * m + j
                        act.wait_ge(S.h_mm, 2 * MC * e + k + 1)
                        at(act, S.y_mm, 3 * (e - 1))
                        act.wait_ge(S.b1_ready, e + 1)
                        act.activation(hT[n][:, m, a:b], banks[2 + k % 4][:, 0:b - a], ACT.Gelu,
                                       bias=b1e[n][:, m:m + 1]).then_inc(S.h_ready, 1)
            expert(0, 0)
            expert(1, 1)
            with act.Fori(1, NE // 2) as e:
                for n in range(2):
                    expert(2 * e + n, n)

        @block.vector
        def _(dve):
            dve.wait_ge(S.ld_ctx, 16)
            dve.tensor_copy(ctx_split[:, 0, :], ctxT[:, :]).then_inc(S.ctx_split, 1)
            dve.wait_ge(S.ctx_split, 1)
            dve.tensor_tensor(ctx_split[:, 1, :], ctxT[:, :], ctx_split[:, 0, :].bitcast(F32),
                              ALU.subtract).then_inc(S.ctx_split, 1)
            for q in range(4):
                for o in range(2):
                    dve.wait_ge(S.m_hi_ready, 2 * q + o + 1)
                    h = slice(4 * q + o, 4 * q + o + 3, 2)
                    hi = m_hi[:, :].rearrange("p (h d) -> p h d", d=P)[:, h, :].bitcast(F32)
                    lo = m_lo[:, :].rearrange("p (h d) -> p h d", d=P)[:, h, :]
                    dve.tensor_tensor(lo, banks[q + 4 * o][:, 0:2 * P].rearrange("p (h d) -> p h d", d=P), hi,
                                      ALU.subtract).then_inc(S.m_lo_ready, 1)

            def mean_var0(a, b):
                for n in range(a, b):
                    own_wait(dve)
                    dve.wait_ge(S.st0, n + 1)
                    last = dve.bn_aggr(mv0[:, n, :], st0[:, n, :])
                last.then_inc(S.mv0, 1)

            def g_group(g, with_stats=False):
                for h in range(1, NH, 2):
                    if with_stats:
                        for b in (h - 1, h):
                            own_wait(dve)
                            dve.wait_ge(S.ld_x, 16)
                            dve.bn_stats(st0[:, b, :], x_sb[:, b, :]).then_inc(S.st0, 1)
                        for a, b in LN0_PARTS:
                            if h == b - 1:
                                mean_var0(a, b)
                    dve.wait_ge(S.g_mm, NH * g + h + 1)
                    dst = G[:, cols(g, GB), NK * h:NK * h + NK]
                    dve.tensor_copy(dst, banks[h % 8][:, 0:GN].rearrange("p (b k) -> p b k", k=NK)).then_inc(S.g_dve, 1)
            g_group(0, True)
            dve.wait_ge(S.wv_hi_ready, 1)
            dve.tensor_tensor(wv_lo[:, :], stage[:, 2, :], wv_hi[:, :].bitcast(F32),
                              ALU.subtract).then_inc(S.wv_split, 1)
            for g in range(1, G_FIRST):
                g_group(g)
            dve.wait_ge(S.rs0, 1)

            def stats(k, n, ready):
                own_wait(dve)
                dve.wait_ge(ready, n + 1)
                dve.bn_stats(st[k][:, :], row_of(res, n)).then_inc([S.st0, S.st1, S.st2, S.st3][k], 1)

            def mean_var(k, n):
                own_wait(dve)
                dve.wait_ge([S.st0, S.st1, S.st2, S.st3][k], n + 1)
                at(dve, [S.ve0, S.ve1, S.ve2, S.ve3][k], n)
                dve.bn_aggr(mv[k][:, :], st[k][:, :]).then_inc([S.mv0, S.mv1, S.mv2, S.mv3][k], 1)

            def normed(k, n, dst, reader):
                dve.wait_ge([S.rs0, S.rs1, S.rs2, S.rs3][k], n + 1)
                at(dve, reader, n)
                dve.tensor_scalar(dst, row_of(res, n), mv[k][:, 0:1], rs[k][:, :], ALU.subtract,
                                  ALU.mult).then_inc([S.xn0, S.xn1, S.xn2, S.xn3][k], 1)

            def row_max(j, n, bank):
                nh = HCUT[j + 1] - HCUT[j]
                dve.wait_ge(S.s1_mm, 3 * n + 1 + j)
                at(dve, S.p1_exp, 3 * n - 2 + j if not isinstance(n, int) or n > 0 else 0)
                dve.tensor_reduce(nm1[:, HCUT[j]:HCUT[j + 1]], bank[:, 0:nh * NK].rearrange("p (h k) -> p h k", k=NK), AX.X,
                                  ALU.max, negate=True).then_inc(S.nm1_ready, 1)

            def step(n):
                if n.n4 is not None:
                    dve.wait_ge(S.o1_mm, n.n4 + 1)
                    dve.tensor_tensor(row_of(res, n.n4), B2[:, 0:D], row_of(res, n.n4), ALU.add).then_inc(S.x3_ready, 1)
                    stats(3, n.n4, S.x3_ready)
                    mean_var(3, n.n4)
                if n.n1 is not None:
                    dve.wait_ge(S.y0_mm, n.n1 + 1)
                    dve.tensor_tensor(row_of(res, n.n1), B0[:, 0:D], row_of(res, n.n1), ALU.add).then_inc(S.x2_ready, 1)
                    stats(2, n.n1, S.x2_ready)
                    mean_var(2, n.n1)
                if n.n0 is not None:
                    dve.wait_ge(S.s0_mm, n.n0 + 1)
                    at(dve, S.p0_ready, n.n0)
                    dve.tensor_reduce(nm0[:, :], B1[:, 0:NK], AX.X, ALU.max, negate=True).then_inc(S.nm0_ready, 1)
                if n.n4 is not None:
                    dve.wait_ge(S.rs3, n.n4 + 1)
                    at(dve, S.xn3_t, n.n4)
                    at(dve, S.sc0_done, 16 * n.n4)
                    at(dve, S.sc1_done, 16 * n.n4)
                    x3 = res[:, one(n.n4), :].broadcast_to([P, 2, D])
                    dve.tensor_scalar(rows[:, :, 0:D], x3, mv[3][:, 0:1], rs[3][:, :], ALU.subtract,
                                      ALU.mult).then_inc(S.xn3, 1)
                if n.n2 is not None:
                    dve.wait_ge(S.p1_exp, 3 * n.n2 + 3)
                    at(dve, S.p1n_ready, n.n2)
                    dve.reciprocal(ri1[:, :], sum1[:, :]).then_inc(S.ri1_ready, 1)
                if n.n0 is not None:
                    dve.wait_ge(S.p0_ready, n.n0 + 1)
                    dve.reciprocal(ri0[:, :], sum0[:, :]).then_inc(S.ri0_ready, 1)
                if n.n1 is not None:
                    normed(2, n.n1, xn[2][:, :], S.xn2_t)
                if n.n3 is not None:
                    dve.wait_ge(S.pv_mm, 2 * n.n3 + 2)
                    at(dve, S.o1_mm, n.n3)
                    dve.tensor_copy(cT[:, 4:8, :], B5[:, :].rearrange("p (m q) -> p m q", q=NQ)).then_inc(S.cT_dve, 1)
                if n.n4 is not None:
                    dve.wait_ge(S.rg_mm, n.n4 + 1)
                    at(dve, S.eg_ready, n.n4)
                    dve.tensor_reduce(nmg[:, :], B3[:, 0:NE], AX.X, ALU.max, negate=True).then_inc(S.nmg_ready, 1)
                if n.n0 is not None:
                    dve.wait_ge(S.o0_mm, n.n0 + 1)
                    dve.wait_ge(S.ri0_ready, n.n0 + 1)
                    if isinstance(n.n0, int) and n.n0 == 0:
                        dve.wait_ge(S.xb_ready, 2)
                    dve.scalar_tensor_tensor(out=row_of(res, n.n0), in0=B0[:, 0:D], scalar=ri0[:, :], in1=row_of(res, n.n0),
                                             op0=ALU.mult, op1=ALU.add).then_inc(S.x1_ready, 1)
                    stats(1, n.n0, S.x1_ready)
                if n.n4 is not None:
                    own_wait(dve)
                    dve.wait_ge(S.eg_ready, n.n4 + 1)
                    dve.max(topg[:, :], eg[:, :]).then_inc(S.topg_ready, 1)
                if n.n0 is not None:
                    mean_var(1, n.n0)
                if n.n4 is not None:
                    own_wait(dve)
                    dve.wait_ge(S.topg_ready, n.n4 + 1)
                    dve.max_index(topgi[:, :], topg[:, :], eg[:, :]).then_inc(S.topgi_ready, 1)
                    dve.reciprocal(rig[:, :], sumg[:, :]).then_inc(S.rig_ready, 1)
                if n.n1 is not None:
                    row_max(0, n.n1, B2)
                if n.n4 is not None:
                    dve.wait_ge(S.topgi_ready, n.n4 + 1)
                    at(dve, S.slot_f, n.n4)
                    at(dve, S.pos_mm, n.n4)
                    dve.tensor_tensor(oh[:, :, :], iota16[:, None, 0:NE].broadcast_to([P, 2, NE]),
                                      topgi[:, 0:2, None].broadcast_to([P, 2, NE]), ALU.is_equal).then_inc(S.oh_ready, 1)
                    dve.wait_ge(S.rig_ready, n.n4 + 1)
                    dve.tensor_scalar(rows[:, :, D + 1:D + 2], topg[:, 0:2][:, :, None], rig[:, :], tg[:, 3:4], ALU.mult,
                                      ALU.mult).then_inc(S.cw_ready, 1)
                if n.n0 is not None:
                    normed(1, n.n0, xn[1][:, :], S.xn1_t)
                if n.n1 is not None:
                    row_max(1, n.n1, B3)
                if n.n4 is not None:
                    dve.wait_ge(S.pos_mm, n.n4 + 1)
                    at(dve, S.slot_e, n.n4)
                    dve.tensor_tensor(pos[:, :, :], B1[:, 0:2 * NE].rearrange("p (k e) -> p k e", k=2), carry[:, :, :],
                                      ALU.add).then_inc(S.pos_ready, 1)
                    dve.tensor_tensor(carry[:, :, :], B1[:, 2 * NE:4 * NE].rearrange("p (k e) -> p k e", k=2), carry[:, :, :],
                                      ALU.add).then_inc(S.carry_ready, 1)
                if n.l is not None:
                    at(dve, S.xn0_t, n.l)
                    if isinstance(n.l, int) and n.l == LN0_PARTS[0][1]:
                        dve.wait_ge(S.rs0, 2)
                    dve.tensor_scalar(xn[0][:, :], row_of(x_sb, n.l), mv0[:, one(n.l), 0], rs0[:, one(n.l)], ALU.subtract,
                                      ALU.mult).then_inc(S.xn0, 1)
                if n.n0 is not None:
                    dve.wait_ge(S.er_ready, n.n0 + 1)
                    dve.tensor_scalar(er1[:, :], er[:, :], 1.0, None, ALU.add).then_inc(S.er1_ready, 1)
                    dve.wait_ge(S.er1_ready, n.n0 + 1)
                    dve.reciprocal(sig[:, :], er1[:, :]).then_inc(S.sig_ready, 1)
                if n.n2 is not None:
                    dve.wait_ge(S.p1_t, 4 * n.n2 + 2)
                    dve.tensor_copy(p1T[:, 512:1024], B6[0:NK, :]).then_inc(S.p1T_dve, 1)
                if n.n0 is not None:
                    own_wait(dve)
                    dve.wait_ge(S.sig_ready, n.n0 + 1)
                    dve.max(top[:, :], sig[:, :]).then_inc(S.top_ready, 1)
                    own_wait(dve)
                    dve.wait_ge(S.top_ready, n.n0 + 1)
                    dve.max_index(topi[:, :], top[:, :], sig[:, :]).then_inc(S.topi_ready, 1)
                    dve.tensor_reduce(den[:, :], top[:, 0:TOPK0], AX.X, ALU.add).then_inc(S.den_ready, 1)
                    dve.wait_ge(S.topi_ready, n.n0 + 1)
                    dve.tensor_tensor(eq[:, :, :], iota16[:, None, :].broadcast_to([P, TOPK0, NE0]),
                                      topi[:, 0:TOPK0, None].broadcast_to([P, TOPK0, NE0]), ALU.is_equal).then_inc(S.eq_ready, 1)
                    dve.wait_ge(S.den_ready, n.n0 + 1)
                    dve.tensor_scalar(den1[:, :], den[:, :], 1e-9, None, ALU.max).then_inc(S.den1_ready, 1)
                    dve.wait_ge(S.eq_ready, n.n0 + 1)
                    dve.tensor_reduce(mask[:, :], eq[:, :, :].rearrange("p k e -> p e k"), AX.X,
                                      ALU.add).then_inc(S.mask_ready, 1)
                if n.n4 is not None:
                    dve.wait_ge(S.slot_f, n.n4 + 1)
                    with nc.allow_low_precision(reason="one whole number below 2^24 and zeros"):
                        dve.tensor_reduce(sidx[:, :], slot[:, :, :], AX.X, ALU.add).then_inc(S.sidx_ready, 1)
                if n.n0 is not None:
                    dve.wait_ge(S.den1_ready, n.n0 + 1)
                    dve.reciprocal(rden[:, :], den1[:, :]).then_inc(S.rden_ready, 1)
                    dve.wait_ge(S.rden_ready, n.n0 + 1)
                    dve.wait_ge(S.mask_ready, n.n0 + 1)
                    dve.scalar_tensor_tensor(out=w0[:, :], in0=sig[:, :], scalar=rden[:, :], in1=mask[:, :], op0=ALU.mult,
                                             op1=ALU.mult).then_inc(S.w0_ready, 1)
                    dve.wait_ge(S.w0_ready, n.n0 + 1)
                    dve.wait_ge(S.h0_mm, n.n0 + 1)
                    at(dve, S.hw_t, n.n0)
                    dve.scalar_tensor_tensor(out=hw[:, :].rearrange("p (e s) -> p e s", s=ES),
                                             in0=B1[:, :].rearrange("p (e s) -> p e s", s=ES), scalar=0.0,
                                             in1=w0[:, :, None].broadcast_to([P, NE0, ES]), op0=ALU.max,
                                             op1=ALU.mult).then_inc(S.hw_ready, 1)
                if n.n1 is not None:
                    row_max(2, n.n1, B4)
                if n.n2 is not None:
                    dve.wait_ge(S.p1_t, 4 * n.n2 + 4)
                    at(dve, S.pv_mm, 2 * n.n2)
                    dve.tensor_copy(p1T[:, 1536:2048], B6[0:NK, :]).then_inc(S.p1T_dve, 1)
            pipeline(dve, step)

            dve.wait_ge(S.ld_b2, 16)

            def split_w1(e, n):
                dve.wait_ge((S.w1_load0, S.w1_load1)[n], 8 * (e - n) + 16)
                at(dve, S.h_mm, 2 * MC * (e - 1))
                dve.tensor_copy(w1_hi[n], w1_sb[n]).then_inc(S.w1_hi, 1)
                dve.wait_ge(S.w1_hi, e + 1)
                dve.tensor_tensor(w1_lo[n], w1_sb[n], w1_hi[n].bitcast(F32), ALU.subtract).then_inc(S.w1_split, 1)

            def slots_in(e, n):
                dve.wait_ge(S.xeT_hi, e + 1)
                dve.tensor_tensor(xeT_lo[n][:, 0:512], banks[0][:, :], xeT_hi[n][:, 0:512].bitcast(F32), ALU.subtract)
                dve.tensor_tensor(xeT_lo[n][:, 512:CAP], banks[1][:, 0:TAIL], xeT_hi[n][:, 512:CAP].bitcast(F32),
                                  ALU.subtract).then_inc(S.xeT_lo, 1)
                at(dve, S.add_done, 16 * ST * (e - 1))
                dve.tensor_copy(tok_u[n][:, 0:ST - 1], xe[n][:, 0:ST - 1, D])
                dve.tensor_copy(tok_u[n][0:TAIL, ST - 1:ST], xe[n][0:TAIL, ST - 1, D:D + 1])
                dve.tensor_copy(gate_e[n][:, 0:ST - 1, :], xe[n][:, 0:ST - 1, D + 1:D + 2])
                dve.tensor_copy(gate_e[n][0:TAIL, ST - 1, :],
                                xe[n][0:TAIL, ST - 1, D + 1:D + 2]).then_inc(S.tok_conv, 1)

            def rows_out(e, n):
                for j, (a, b) in enumerate(YS):
                    k = P if j < 2 else TAIL
                    yj = ye[n][0:k, a:b, :]
                    dve.wait_ge(S.y_mm, 3 * e + 1 + j)
                    dve.tensor_tensor(yj, (banks[6], banks[7], banks[1])[j][0:k, 0:D * (b - a)].rearrange("p (s d) -> p s d", d=D),
                                      b2[0:k, one(e), :].broadcast_to([k, b - a, D]), ALU.add).then_inc(S.yb_ready, 1)
                    if j > 0:
                        dve.wait_ge(S.tok_conv, e + 1)
                        dve.wait_ge(S.yb_ready, 3 * e + 1 + j)
                        dve.tensor_tensor(yj, yj, gate_e[n][0:k, a:b, :].broadcast_to([k, b - a, D]),
                                          ALU.mult).then_inc((S.yw1_ready, S.yw2_ready)[j - 1], 1)

            def expert(e, n):
                slots_in(e + 1, 1 - n)
                rows_out(e, n)
                if not isinstance(e, int) or e + 2 < NE:
                    split_w1(e + 2, n)

            split_w1(0, 0)
            split_w1(1, 1)
            slots_in(0, 0)
            expert(0, 0)
            with dve.Fori(1, NE // 2 - 1) as e:
                expert(2 * e - 1, 1)
                expert(2 * e, 0)
            expert(NE - 3, 1)
            expert(NE - 2, 0)
            rows_out(NE - 1, 1)


def kernel(x, ctx_1024, fside_BxS2_0, g_xattn, g_ffn, L0_xattn_W_out, L0_xattn_b_out, L0_ffn_expert_sel, L0_ffn_keys,
           L0_ffn_values, L0_ffn_route_scale, L1_xattn_Wq, L1_xattn_Wk, L1_xattn_Wv, L1_xattn_Wo, L1_ffn_Wg, L1_ffn_W1,
           L1_ffn_b1, L1_ffn_W2, L1_ffn_b2):
    import concourse.bacc as _bacc
    from concourse.bass_utils import run_bass_kernel_spmd as _run

    x = np.asarray(x)
    NB, NQ, D = x.shape
    E, _, H = L1_ffn_W1.shape
    NE0, _, ES = L0_ffn_keys.shape
    lay = {
        "x": x.transpose(1, 0, 2),
        "ctxT": np.asarray(ctx_1024).transpose(2, 0, 1).reshape(D, -1),
        "ind": np.asarray(fside_BxS2_0).T,
        "g_xattn": np.asarray(g_xattn)[None, :],
        "g_ffn": np.asarray(g_ffn)[None, :],
        "rscale": np.asarray(L0_ffn_route_scale)[None, :],
        "woutT": np.asarray(L0_xattn_W_out).T,
        "bout": np.asarray(L0_xattn_b_out)[None, :],
        "selT": np.asarray(L0_ffn_expert_sel).T,
        "keys": np.asarray(L0_ffn_keys).transpose(1, 0, 2).reshape(D, NE0 * ES),
        "vals": np.asarray(L0_ffn_values).reshape(NE0 * ES // P, P, D).transpose(1, 0, 2),
        "wqT": np.asarray(L1_xattn_Wq).T.reshape(-1, P, D).transpose(1, 0, 2),
        "wkT": np.asarray(L1_xattn_Wk).T.reshape(-1, P, D).transpose(1, 0, 2),
        "wv": np.asarray(L1_xattn_Wv),
        "wo": np.asarray(L1_xattn_Wo).reshape(-1, P, D).transpose(1, 0, 2),
        "wgT": np.asarray(L1_ffn_Wg).T,
        "w1": np.asarray(L1_ffn_W1),
        "b1": np.asarray(L1_ffn_b1).reshape(E * H // P, P).T,
        "w2": np.asarray(L1_ffn_W2).reshape(E, H // P, P, D).transpose(0, 2, 1, 3),
        "b2": np.asarray(L1_ffn_b2),
    }
    nc = _bacc.Bacc("TRN2", target_bir_lowering=False, num_devices=1)
    arrays, t = {}, {}
    for name, a in lay.items():
        arrays[f"in_{name}"] = np.ascontiguousarray(a)
        t[name] = nc.dram_tensor(f"in_{name}", a.shape, mybir.dt.from_np(a.dtype), kind="ExternalInput").ap()
    pad = -(-int(round(2 * NB * NQ * 1.05 / E)) // P) * P
    out = nc.dram_tensor("out", (NB * NQ + pad, D), F32, kind="ExternalOutput").ap()
    gated_layers_kernel(nc, t, out)
    r = _run(nc, [arrays], core_ids=[0])
    return r.results[0]["out"][:NB * NQ].reshape(NB, NQ, D)
```
